# Optimizing a Trainium2 kernel written in Bass

```python
import numpy as np
import jax
import jax.numpy as jnp

def _softmax(x, axis=-1):
    return jax.nn.softmax(x, axis=axis)

def _gelu(x):
    return jax.nn.gelu(x, approximate=True)

def _silu(x):
    return jax.nn.silu(x)

def _sigmoid(x):
    return jax.nn.sigmoid(x)

def _layernorm(x, axis=-1, eps=1e-05):
    m = jnp.mean(x, axis=axis, keepdims=True)
    v = jnp.var(x, axis=axis, keepdims=True)
    return (x - m) / jnp.sqrt(v + eps)

def _scatter_add(tgt, idx, src, axis=0):
    return tgt.at[idx].add(src)

def _segment_sum(src, seg, n):
    return jax.ops.segment_sum(src, seg, n)
kernel_name = 'mk_flamingo_gated_d1_seqx_r2_b00aae'

def setup_inputs(seed: int=0):
    np.random.seed(seed)
    _w = jnp.asarray

    def _rec_inputs():
        import jax
        import jax.numpy as jnp
        _rk = jax.random.key(seed)
        x = 7.22e-05 + 1 * jax.random.normal(jax.random.fold_in(_rk, 1), (8, 512, 512), jnp.float32)
        _lenS = 512 - jax.random.randint(jax.random.fold_in(_rk, 7), (8,), 0, max(1, 512 // 4) + 1, jnp.int32)
        _lenS2 = 512 - jax.random.randint(jax.random.fold_in(_rk, 8), (8,), 0, max(1, 512 // 4) + 1, jnp.int32)
        _ctx_768P = jax.random.normal(jax.random.fold_in(_rk, 11), (8, 16, 384), jnp.float32)
        _ctx_768c = jax.random.dirichlet(jax.random.fold_in(_rk, 511), 0.3 * jnp.ones((16,), jnp.float32), (8, 512))
        _ctx_768t = jnp.einsum('bsk,bkd->bsd', _ctx_768c, _ctx_768P)
        _ctx_768t = _ctx_768t * jax.lax.rsqrt(jnp.mean(jnp.square(_ctx_768t)) + 1e-12) * 0.953939
        ctx_768 = -0.000191848 + 0.999787 * (_ctx_768t + 0.3 * jax.random.normal(jax.random.fold_in(_rk, 611), (8, 512, 384), jnp.float32))
        _g = jax.random.normal(jax.random.fold_in(_rk, 9001), (2, 1), jnp.float32)
        _g = jnp.sign(_g) * jnp.maximum(jnp.abs(_g), 1.0) + (_g == 0) * 1.0
        g_xattn = _g[0]
        g_ffn = _g[1]
        return (x, ctx_768, g_xattn, g_ffn)
    x, ctx_768, g_xattn, g_ffn = _rec_inputs()

    def _L0_xattn_setup():
        import jax, jax.numpy as jnp
        import numpy as np
        NUM_HEADS = 16
        CLAMP = 10000.0
        key = jax.random.key(seed)
        ks = jax.random.split(key, 8)
        B, Nq, Nkv, Cq, Ckv = (4, 1024, 1024, 512, 384)
        s_q = 1.0 / np.sqrt(Cq)
        s_kv = 1.0 / np.sqrt(Ckv)
        return {'query': jax.random.normal(ks[0], (B, Nq, Cq), jnp.float32), 'key_value': jax.random.normal(ks[1], (B, Nkv, Ckv), jnp.float32), 'Wq': jax.random.normal(ks[2], (Cq, Cq), jnp.float32) * s_q, 'bq': jnp.zeros((Cq,), jnp.float32), 'Wk': jax.random.normal(ks[3], (Ckv, Cq), jnp.float32) * s_kv, 'bk': jnp.zeros((Cq,), jnp.float32), 'Wv': jax.random.normal(ks[4], (Ckv, Cq), jnp.float32) * s_kv, 'bv': jnp.zeros((Cq,), jnp.float32), 'Wo': jax.random.normal(ks[5], (Cq, Cq), jnp.float32) * s_q, 'bo': jnp.zeros((Cq,), jnp.float32)}
    _L0_xattn_all = _L0_xattn_setup()
    _L0_xattn_in = {k: v for k, v in _L0_xattn_all.items() if k in ('Wq', 'bq', 'Wk', 'bk', 'Wv', 'bv', 'Wo', 'bo')}
    del _L0_xattn_all

    def _L0_ffn_setup():
        import math
        import jax, jax.numpy as jnp
        import numpy as np
        NUM_EXPERTS = 8
        CAPACITY_FACTOR = 1.5
        key = jax.random.key(seed)
        ks = jax.random.split(key, 4)
        B, T, D, F, E = (4, 1024, 512, 2048, NUM_EXPERTS)
        scale = 0.02
        return {'x': jax.random.normal(ks[0], (B, T, D), dtype=jnp.float32), 'router_w': jax.random.normal(ks[1], (E, D), dtype=jnp.float32) * scale, 'w1': jax.random.normal(ks[2], (E, D, F), dtype=jnp.float32) * scale, 'b1': jnp.zeros((E, F), dtype=jnp.float32), 'w2': jax.random.normal(ks[3], (E, F, D), dtype=jnp.float32) * scale, 'b2': jnp.zeros((E, D), dtype=jnp.float32)}
    _L0_ffn_all = _L0_ffn_setup()
    _L0_ffn_in = {k: v for k, v in _L0_ffn_all.items() if k in ('router_w', 'w1', 'b1', 'w2', 'b2')}
    del _L0_ffn_all
    return {'x': x, 'ctx_768': ctx_768, 'g_xattn': g_xattn, 'g_ffn': g_ffn, 'L0_xattn_Wq': _L0_xattn_in['Wq'], 'L0_xattn_bq': _L0_xattn_in['bq'], 'L0_xattn_Wk': _L0_xattn_in['Wk'], 'L0_xattn_bk': _L0_xattn_in['bk'], 'L0_xattn_Wv': _L0_xattn_in['Wv'], 'L0_xattn_bv': _L0_xattn_in['bv'], 'L0_xattn_Wo': _L0_xattn_in['Wo'], 'L0_xattn_bo': _L0_xattn_in['bo'], 'L0_ffn_router_w': _L0_ffn_in['router_w'], 'L0_ffn_w1': _L0_ffn_in['w1'], 'L0_ffn_b1': _L0_ffn_in['b1'], 'L0_ffn_w2': _L0_ffn_in['w2'], 'L0_ffn_b2': _L0_ffn_in['b2']}

def reference(x, ctx_768, g_xattn, g_ffn, L0_xattn_Wq, L0_xattn_bq, L0_xattn_Wk, L0_xattn_bk, L0_xattn_Wv, L0_xattn_bv, L0_xattn_Wo, L0_xattn_bo, L0_ffn_router_w, L0_ffn_w1, L0_ffn_b1, L0_ffn_w2, L0_ffn_b2):
    import jax
    import jax.numpy as jnp

    def _L0_xattn_ref(query, key_value, Wq, bq, Wk, bk, Wv, bv, Wo, bo):
        import jax, jax.numpy as jnp
        import numpy as np
        NUM_HEADS = 16
        CLAMP = 10000.0
        B, Nq, Cq = query.shape
        Nkv = key_value.shape[1]
        H = NUM_HEADS
        D = Cq // H
        scale = D ** (-0.5)
        q = (query @ Wq + bq).reshape(B, Nq, H, D).transpose(0, 2, 1, 3)
        k = (key_value @ Wk + bk).reshape(B, Nkv, H, D).transpose(0, 2, 1, 3)
        v = (key_value @ Wv + bv).reshape(B, Nkv, H, D).transpose(0, 2, 1, 3)
        attn = jnp.einsum('bhqd,bhkd->bhqk', q, k) * scale
        attn = jnp.clip(attn, -CLAMP, CLAMP)
        attn = jax.nn.softmax(attn, axis=-1)
        attn = jnp.where(jnp.any(jnp.isnan(attn)), jnp.asarray(1.0 / Nkv, attn.dtype), attn)
        x = jnp.einsum('bhqk,bhkd->bqhd', attn, v).reshape(B, Nq, Cq)
        return x @ Wo + bo

    def _L0_ffn_ref(x, router_w, w1, b1, w2, b2):
        import math
        import jax, jax.numpy as jnp
        import numpy as np
        NUM_EXPERTS = 8
        CAPACITY_FACTOR = 1.5
        B, T, D = x.shape
        E = router_w.shape[0]
        N = B * T
        C = max(math.ceil(CAPACITY_FACTOR * N / E), 1)
        x_flat = x.reshape(N, D)
        logits = x_flat @ router_w.T
        probs = jax.nn.softmax(logits, axis=-1)
        chosen_e = jnp.argmax(probs, axis=-1)
        chosen_p = jnp.max(probs, axis=-1)
        onehot = jax.nn.one_hot(chosen_e, E, dtype=jnp.float32)
        pos = jnp.take_along_axis(jnp.cumsum(onehot, axis=0), chosen_e[:, None], axis=1)[:, 0] - 1.0
        pos = pos.astype(jnp.int32)
        kept = pos < C
        pos_c = jnp.clip(pos, 0, C - 1)
        buf = jnp.zeros((E, C, D), dtype=x.dtype).at[chosen_e, pos_c].add(x_flat * kept[:, None].astype(x.dtype))
        h = jax.nn.gelu(jnp.einsum('ecd,edf->ecf', buf, w1) + b1[:, None, :], approximate=False)
        eo = jnp.einsum('ecf,efd->ecd', h, w2) + b2[:, None, :]
        y = eo[chosen_e, pos_c] * (chosen_p * kept.astype(x.dtype))[:, None]
        return y.reshape(B, T, D)
    x = x + jnp.tanh(g_xattn[0]) * _L0_xattn_ref(_layernorm(x, axis=-1), ctx_768, L0_xattn_Wq, L0_xattn_bq, L0_xattn_Wk, L0_xattn_bk, L0_xattn_Wv, L0_xattn_bv, L0_xattn_Wo, L0_xattn_bo)
    x = x + jnp.tanh(g_ffn[0]) * _L0_ffn_ref(_layernorm(x, axis=-1), L0_ffn_router_w, L0_ffn_w1, L0_ffn_b1, L0_ffn_w2, L0_ffn_b2)
    return x

_drawn_inputs = setup_inputs


def setup_inputs(seed=0):
    import zlib

    import numpy as np

    out = dict(_drawn_inputs(seed))
    spreads = {'L0_xattn_bq': (0.0, 0.496),
     'L0_xattn_bk': (0.0, 0.8),
     'L0_xattn_bv': (0.0, 0.1),
     'L0_xattn_bo': (0.0, 0.1),
     'L0_ffn_b1': (0.0, 0.739),
     'L0_ffn_b2': (0.0, 0.393)}
    factors = {}
    for name, (base, spread) in spreads.items():
        noise = np.random.default_rng([zlib.crc32(name.encode()), seed]).standard_normal(out[name].shape)
        drawn = base * np.exp(spread * noise) if base else spread * noise
        out[name] = jnp.asarray(drawn.astype(out[name].dtype))
    for name, factor in factors.items():
        out[name] = (out[name] * factor).astype(out[name].dtype)
    return out
```

```python
from contextlib import ExitStack

import concourse.bass as bass
from concourse import mybir

F32 = mybir.dt.float32
F32R = mybir.dt.float32r
I32 = mybir.dt.int32
ALU = mybir.AluOpType
ACT = mybir.ActivationFunctionType
AX_X = mybir.AxisListType.X
P = 128
EPS = 1e-5
CLAMP = 10000.0
HEADS = 16
MADE = 5


def wait(eng, sem, base, count):
    if isinstance(base, int) and base + count <= 0:
        return
    eng.wait_ge(sem, base + count)


def wait_apart(eng, keep, sem, base, count):
    wait(eng, sem, base, count)
    if not isinstance(base, int):
        eng.sem_inc(keep["passed"], 1)


def make_pools(nc, ctx):
    def sb(name, shape, dt=F32):
        return ctx.enter_context(nc.sbuf_tensor(name, shape, dt))

    def ps(name):
        return ctx.enter_context(nc.psum_tensor(name, [P, 512], F32))

    def sem(name):
        return ctx.enter_context(nc.semaphore(name))

    return sb, ps, sem


def newton_rsqrt(dve, chain, base, n, var, sd, r0, tmp, r):
    dve.reciprocal(r0, sd).then_inc(chain, 1)
    wait(dve, chain, base, n + 1)
    dve.tensor_tensor(tmp, r0, r0, ALU.mult).then_inc(chain, 1)
    wait(dve, chain, base, n + 2)
    dve.scalar_tensor_tensor(out=tmp, in0=var, scalar=EPS, in1=tmp, op0=ALU.add, op1=ALU.mult).then_inc(chain, 1)
    wait(dve, chain, base, n + 3)
    dve.tensor_scalar(tmp, tmp, -0.5, 1.5, ALU.mult, ALU.add).then_inc(chain, 1)
    wait(dve, chain, base, n + 4)
    dve.tensor_tensor(r, r0, tmp, ALU.mult).then_inc(chain, 1)


def attention(nc, keep, x, ctx_in, Wq, bq, Wk, bk, Wv, attn_dram, mean_dram):
    B, S, C = x.shape
    CK = ctx_in.shape[2]
    QT, KT = S // P, S // P
    CT, CKT = C // P, CK // P
    HG = HEADS // CT
    D = C // HEADS
    SCALE = float(D) ** -0.5
    FILLS = CT + CKT + CT + CT + KT + 1 + CT

    with ExitStack() as ctx:
        sb, ps, sem = make_pools(nc, ctx)
        wq = sb("wq", [P, CT, C])
        wk = sb("wk", [P, CKT, C])
        wv = sb("wv", [P, CKT, C])
        bqT = sb("bqT", [P, CT])
        bkT = sb("bkT", [P, CT])
        xn = sb("xn", [P, QT, C])
        cx = sb("cx", [P, KT, CK])
        stats = sb("stats", [P, QT, 6])
        mv = sb("mv", [P, QT, 2])
        sd = sb("sd", [P, QT])
        r0 = sb("r0", [P, QT])
        tmp = sb("tmp", [P, QT])
        rs = sb("rs", [P, QT])
        xT = sb("xT", [P, CT, S])
        cT = sb("cT", [P, CKT, S])
        qT = sb("qT", [P, CT, S])
        kT = sb("kT", [P, CT, S])
        v = sb("v", [P, KT, C])
        qsum = sb("qsum", [P, CT])
        ksum = sb("ksum", [P, CT])
        meanv = sb("meanv", [P, CT])
        prob = [sb(f"prob{i}", [P, QT, S]) for i in range(2)]
        rowmax = [sb(f"rowmax{i}", [P, QT]) for i in range(2)]
        negmax = [sb(f"negmax{i}", [P, QT]) for i in range(2)]
        rowsum = [sb(f"rowsum{i}", [P, QT, HG]) for i in range(2)]
        rinv = sb("rinv", [P, QT, HG])
        rinvx = [sb(f"rinvx{i}", [P, QT, C // CT]) for i in range(2)]
        probT = [sb(f"probT{i}", [P, KT, S]) for i in range(2)]
        scaleT = [sb(f"scaleT{i}", [P, S]) for i in range(2)]
        att = [sb(f"att{i}", [P, S]) for i in range(2)]
        mean_w = sb("mean_w", [P, 1])

        proj_bank = [ps(f"proj_bank{i}") for i in range(2)]
        score_bank = [ps(f"score_bank{i}") for i in range(2)]
        probT_bank = [ps(f"probT_bank{i}") for i in range(2)]
        att_bank = [ps(f"att_bank{i}") for i in range(2)]

        w_in = sem("w_in")
        x_in = sem("x_in")
        ctx_in_s = sem("ctx_in_s")
        stats_done = sem("stats_done")
        aggr_done = sem("aggr_done")
        sqrt_done = sem("sqrt_done")
        newton = sem("newton")
        xn_done = sem("xn_done")
        proj_full = sem("proj_full")
        proj_read = sem("proj_read")
        nan_sum = sem("nan_sum")
        score_full = sem("score_full")
        score_read = sem("score_read")
        negmax_done = sem("negmax_done")
        clip_done = sem("clip_done")
        exp_done = sem("exp_done")
        probT_full = sem("probT_full")
        probT_read = sem("probT_read")
        att_full = sem("att_full")
        rinv_done = sem("rinv_done")
        rinvx_done = sem("rinvx_done")
        att_done = sem("att_done")
        att_out = sem("att_out")
        att_stored = sem("att_stored")
        mean_out = sem("mean_out")
        mean_stored = sem("mean_stored")
        consts = sem("consts")

        ident, nan_acc = keep["ident"], keep["nan_acc"]
        xr = x.rearrange("b (t p) c -> b p t c", p=P)
        cr = ctx_in.rearrange("b (t p) c -> b p t c", p=P)

        block = ctx.enter_context(nc.Block())

        def x_row(src, b):
            return src[b] if isinstance(b, int) else src[bass.ds(b, 1)].rearrange("o p t c -> (o p) t c")

        @block.sync
        def _(sp):
            sp.dma_start(xn[:], xr[0]).then_inc(x_in, 16)
            sp.dma_start(cx[:], cr[0]).then_inc(ctx_in_s, 16)
            sp.dma_start(wq[:], Wq.rearrange("(t p) n -> p t n", p=P)).then_inc(w_in, 16)
            sp.dma_start(wk[:], Wk.rearrange("(t p) n -> p t n", p=P)).then_inc(w_in, 16)
            sp.dma_start(wv[:], Wv.rearrange("(t p) n -> p t n", p=P)).then_inc(w_in, 16)
            sp.dma_start(bqT[:], bq.rearrange("(t p) -> p t", p=P), allow_slow_non_contiguous=True).then_inc(w_in, 16)
            sp.dma_start(bkT[:], bk.rearrange("(t p) -> p t", p=P), allow_slow_non_contiguous=True).then_inc(w_in, 16)

            def next_inputs(b):
                wait_apart(sp, keep, proj_full, b * FILLS, CT)
                sp.dma_start(xn[:], xr[b + 1] if isinstance(b, int) else xr[bass.ds(b + 1, 1)].rearrange(
                    "o p t c -> (o p) t c")).then_inc(x_in, 16)
                wait_apart(sp, keep, proj_full, b * FILLS, CT + CKT)
                sp.dma_start(cx[:], cr[b + 1] if isinstance(b, int) else cr[bass.ds(b + 1, 1)].rearrange(
                    "o p t c -> (o p) t c")).then_inc(ctx_in_s, 16)

            with sp.Fori(0, B - 1) as b:
                next_inputs(b)

        def groups_at(step):
            h = step - 2
            return h // HG if 0 <= h < HEADS and h % HG == HG - 1 else None

        @block.gpsimd
        def _(pool):
            def stores(b):
                row = lambda t, n: t[b * CT + n] if isinstance(b, int) else t[bass.ds(b * CT + n, 1)].rearrange("o p s -> (o p) s")
                wait_apart(pool, keep, proj_read, b * FILLS, FILLS - CT)
                m = mean_dram[b] if isinstance(b, int) else mean_dram[bass.ds(b, 1)].rearrange("o p g -> (o p) g")
                pool.dma_start(m, meanv[:]).then_inc(mean_out, 16)
                wait_apart(pool, keep, mean_out, b * 16, 16)
                pool.sem_inc(mean_stored, 1)
                for g in range(CT):
                    wait_apart(pool, keep, att_done, b * CT, g + 1)
                    pool.dma_start(row(attn_dram, g), att[g % 2][:]).then_inc(att_out, 16)
                    wait_apart(pool, keep, att_out, b * 16 * CT, 16 * (g + 1))
                    pool.sem_inc(att_stored, 1)

            stores(0)
            with pool.Fori(1, B) as b:
                stores(b)

        @block.tensor
        def _(pe):
            def fill_wait(b, n):
                wait(pe, proj_read, b * FILLS, n - 1)

            def project(b):
                n = 0
                wait(pe, xn_done, b * QT, QT)
                for c in range(CT):
                    fill_wait(b, n)
                    for t in range(QT):
                        last = pe.transpose(proj_bank[n % 2][:, t * P:(t + 1) * P], xn[:, t, c * P:(c + 1) * P], ident[:])
                    last.then_inc(proj_full, 1)
                    n += 1
                wait(pe, ctx_in_s, b * 16, 16)
                for c in range(CKT):
                    fill_wait(b, n)
                    for t in range(KT):
                        last = pe.transpose(proj_bank[n % 2][:, t * P:(t + 1) * P], cx[:, t, c * P:(c + 1) * P], ident[:])
                    last.then_inc(proj_full, 1)
                    n += 1
                pe.wait_ge(w_in, 80)
                wait(pe, proj_read, b * FILLS, CT)
                for w, src, tiles, need in ((wq, xT, CT, CT), (wk, cT, CKT, CT + CKT)):
                    wait(pe, proj_read, b * FILLS, need)
                    for g in range(CT):
                        fill_wait(b, n)
                        for c in range(tiles):
                            last = pe.matmul(proj_bank[n % 2][:], w[:, c, g * P:(g + 1) * P], src[:, c, :],
                                             start=(c == 0), stop=(c == tiles - 1))
                        last.then_inc(proj_full, 1)
                        n += 1
                for t in range(KT):
                    fill_wait(b, n)
                    for c in range(CKT):
                        last = pe.matmul(proj_bank[n % 2][:], cT[:, c, t * P:(t + 1) * P], wv[:, c, :],
                                         start=(c == 0), stop=(c == CKT - 1))
                    last.then_inc(proj_full, 1)
                    n += 1
                wait(pe, proj_read, b * FILLS, n)
                for g in range(CT):
                    for t in range(KT):
                        last = pe.matmul(proj_bank[n % 2][:, g:g + 1], v[:, t, g * P:(g + 1) * P], mean_w[:],
                                         start=(t == 0), stop=(t == KT - 1))
                last.then_inc(proj_full, 1)
                return n + 1

            def scores(b, h):
                g, j = h // HG, h % HG
                rows = slice(j * D, (j + 1) * D)
                for t in range(QT):
                    wait(pe, score_read, b * HEADS * QT, h * QT + t - 1)
                    pe.matmul(score_bank[t % 2][:], qT[rows, g, t * P:(t + 1) * P], kT[rows, g, :],
                              start=True, stop=True).then_inc(score_full, 1)

            def turn(b, h):
                wait(pe, exp_done, b * HEADS * QT, (h + 1) * QT)
                for k in range(KT):
                    wait(pe, probT_read, b * HEADS * KT, h * KT + k - 1)
                    for t in range(QT):
                        last = pe.transpose(probT_bank[k % 2][:, t * P:(t + 1) * P], prob[h % 2][:, t, k * P:(k + 1) * P], ident[:])
                    last.then_inc(probT_full, 1)

            def weigh(b, h):
                g, j = h // HG, h % HG
                if j == 0:
                    wait(pe, att_done, b * CT, g - 1)
                wait(pe, probT_read, b * HEADS * KT, (h + 1) * KT)
                for k in range(KT):
                    last = pe.matmul(att_bank[g % 2][j * D:(j + 1) * D, :], v[:, k, h * D:(h + 1) * D], probT[h % 2][:, k, :],
                                     start=(k == 0), stop=(k == KT - 1))
                last.then_inc(att_full, 1)

            def spread_sums(b, g, n):
                wait(pe, rinvx_done, b * CT, g + 1)
                fill_wait(b, n)
                for t in range(QT):
                    last = pe.matmul(proj_bank[n % 2][:, t * P:(t + 1) * P],
                                     rinvx[g % 2][:, t, :], ident[:],
                                     start=True, stop=True)
                last.then_inc(proj_full, 1)

            def batch(b):
                n = project(b)
                wait(pe, proj_read, b * FILLS, CT + CKT + 2 * CT)
                for step in range(HEADS + 3):
                    if step < HEADS:
                        scores(b, step)
                    if 0 <= step - 1 < HEADS:
                        turn(b, step - 1)
                    if 0 <= step - 2 < HEADS:
                        weigh(b, step - 2)
                    g = groups_at(step)
                    if g is not None:
                        spread_sums(b, g, n + g)

            pe.wait_ge(consts, 1)
            batch(0)
            with pe.Fori(1, B) as b:
                batch(b)

        @block.scalar
        def _(act):
            act.wait_ge(w_in, 80)

            def deviation(b):
                wait(act, aggr_done, b * QT, QT)
                act.activation(sd[:], mv[:, :, 1], ACT.Sqrt, bias=keep["eps"][:, 0:1]).then_inc(sqrt_done, 1)

            def read_projections(b):
                n = 0

                def read(out, in_=None, **more):
                    nonlocal n
                    wait(act, proj_full, b * FILLS, n + 1)
                    act.activation(out, proj_bank[n % 2][:] if in_ is None else in_, ACT.Identity, **more).then_inc(proj_read, 1)
                    n += 1

                for c in range(CT):
                    read(xT[:, c, :])
                for c in range(CKT):
                    read(cT[:, c, :])
                wait(act, nan_sum, b, 0)
                for g in range(CT):
                    read(qT[:, g, :], bias=bqT[:, g:g + 1], accum_out=qsum[:, g:g + 1])
                for g in range(CT):
                    read(kT[:, g, :], bias=bkT[:, g:g + 1], accum_out=ksum[:, g:g + 1])
                for t in range(KT):
                    read(v[:, t, :])
                wait(act, mean_stored, b, 0)
                read(meanv[:], proj_bank[n % 2][:, 0:CT])

            def exps(b, h):
                g, j = h // HG, h % HG
                wait(act, clip_done, b * HEADS, h + 1)
                for t in range(QT):
                    act.activation(prob[h % 2][:, t, :], prob[h % 2][:, t, :], ACT.Exp, bias=negmax[h % 2][:, t:t + 1],
                                   accum_out=rowsum[g % 2][:, t, j:j + 1]).then_inc(exp_done, 1)

            def read_turned(b, h):
                wait(act, att_full, b * HEADS, h - 1)
                for k in range(KT):
                    wait(act, probT_full, b * HEADS * KT, h * KT + k + 1)
                    act.activation(probT[h % 2][:, k, :], probT_bank[k % 2][:], ACT.Identity).then_inc(probT_read, 1)

            def read_sums(b, g):
                n = FILLS - CT + g
                wait(act, att_done, b * CT, g - 1)
                wait(act, proj_full, b * FILLS, n + 1)
                act.activation(scaleT[g % 2][:], proj_bank[n % 2][:], ACT.Identity).then_inc(proj_read, 1)

            def batch(b, more):
                read_projections(b)
                for step in range(HEADS + 3):
                    g = groups_at(step - 1)
                    if g is not None:
                        read_sums(b, g)
                    if 0 <= step - 1 < HEADS:
                        read_turned(b, step - 1)
                    if step < HEADS:
                        exps(b, step)
                    if step == 8 and more:
                        deviation(b + 1)
                read_last(b)

            def read_last(b):
                g = groups_at(HEADS + 2 - 1)
                assert g is None or g == CT - 1

            deviation(0)
            batch(0, True)
            with act.Fori(1, B - 1) as b:
                batch(b, True)
            batch(B - 1, False)

        @block.vector
        def _(dve):
            dve.memset(mean_w[:], 1.0 / S).then_inc(consts, 1)

            def layernorm_stats(b):
                wait(dve, x_in, b * 16, 16)
                wait(dve, xn_done, b * QT, 0)
                for t in range(QT):
                    dve.bn_stats(stats[:, t, :], xn[:, t, :]).then_inc(stats_done, 1)
                wait_apart(dve, keep, stats_done, b * QT, QT)
                for t in range(QT):
                    dve.bn_aggr(mv[:, t, :], stats[:, t, :]).then_inc(aggr_done, 1)

            def layernorm(b):
                wait(dve, sqrt_done, b, 1)
                newton_rsqrt(dve, newton, b * 5, 0, mv[:, :, 1], sd[:], r0[:], tmp[:], rs[:])
                wait(dve, newton, b * 5, 5)
                for t in range(QT):
                    dve.tensor_scalar(xn[:, t, :], xn[:, t, :], mv[:, t, 0:1], rs[:, t:t + 1],
                                      ALU.subtract, ALU.mult).then_inc(xn_done, 1)

            def clip_scores(b, h):
                m = h % 2
                wait(dve, probT_full, b * HEADS * KT, (h - 1) * KT)
                for t in range(QT):
                    wait(dve, score_full, b * HEADS * QT, h * QT + t + 1)
                    dve.tensor_scalar(prob[m][:, t, :], score_bank[t % 2][:], SCALE, -CLAMP, ALU.mult, ALU.max,
                                      accum_out=rowmax[m][:, t:t + 1]).then_inc(score_read, 1)
                wait(dve, score_read, b * HEADS * QT, (h + 1) * QT)
                dve.tensor_scalar(negmax[m][:], rowmax[m][:], CLAMP, -1.0, ALU.min, ALU.mult).then_inc(negmax_done, 1)
                dve.tensor_scalar(prob[m][:], prob[m][:], CLAMP, -CLAMP, ALU.min, ALU.max).then_inc(clip_done, 1)

            def batch(b, more):
                wait(dve, proj_read, b * FILLS, CT + CKT + 2 * CT)
                acc = nan_acc[:, b * CT:(b + 1) * CT] if isinstance(b, int) else nan_acc[:, bass.ds(b * CT, CT)]
                dve.tensor_tensor(acc, qsum[:], ksum[:], ALU.mult).then_inc(nan_sum, 1)
                for step in range(HEADS + 4):
                    if step < HEADS:
                        clip_scores(b, step)
                    if step == 7 and more:
                        layernorm_stats(b + 1)
                    if step == 9 and more:
                        layernorm(b + 1)
                    g = groups_at(step)
                    if g is not None:
                        wait(dve, exp_done, b * HEADS * QT, (g + 1) * HG * QT)
                        wait(dve, proj_full, b * FILLS, FILLS - CT + g - 1 if g >= 2 else 0)
                        wait(dve, rinvx_done, b * CT, g)
                        dve.reciprocal(rinv[:], rowsum[g % 2][:]).then_inc(rinv_done, 1)
                        wait(dve, rinv_done, b * CT, g + 1)
                        dve.tensor_copy(rinvx[g % 2][:].rearrange("p t (j d) -> p (t j) d", d=D),
                                        rinv[:].rearrange("p t j -> p (t j)").unsqueeze(2).to_broadcast([P, QT * HG, D])
                                        ).then_inc(rinvx_done, 1)
                    g = groups_at(step - 1)
                    if g is not None:
                        wait(dve, proj_read, b * FILLS, FILLS - CT + g + 1)
                        wait(dve, att_full, b * HEADS, (g + 1) * HG)
                        wait(dve, att_stored, b * CT, g - 1)
                        dve.tensor_tensor(att[g % 2][:], att_bank[g % 2][:], scaleT[g % 2][:], ALU.mult).then_inc(att_done, 1)

            layernorm_stats(0)
            layernorm(0)
            batch(0, True)
            with dve.Fori(1, B - 1) as b:
                batch(b, True)
            batch(B - 1, False)


def projection(nc, keep, x, bv, Wo, bo, g_xattn, g_ffn, router_w, attn_dram, mean_dram, rows_dram, out):
    B, S, C = x.shape
    T, CT = S // P, C // P
    E = router_w.shape[0]
    N = B * S
    W = rows_dram.shape[1]
    with ExitStack() as ctx:
        sb, ps, sem = make_pools(nc, ctx)
        wo = sb("wo", [P, CT, C])
        bvT = sb("bvT", [P, CT])
        bo_b = sb("bo_b", [P, C])
        gate = sb("gate", [P, 1])
        rw = sb("rw", [E, C])
        rwT = sb("rwT", [P, CT, E])
        nan_row = sb("nan_row", [P, 1])
        nan_tot = sb("nan_tot", [P, 1])
        nan_f = sb("nan_f", [P, 1])
        nan_mask = sb("nan_mask", [P, 1], I32)
        att = [sb(f"pat{i}", [P, CT, S]) for i in range(2)]
        meanv = [sb(f"pmean{i}", [P, CT]) for i in range(2)]
        xs = [sb(f"xs{i}", [P, T, C]) for i in range(2)]
        xn = [sb(f"pxn{i}", [P, T, C]) for i in range(2)]
        stats = sb("pstats", [P, T, 6])
        mv = sb("pmv", [P, T, 2])
        sd = sb("psd", [P, T])
        r0 = sb("pr0", [P, T])
        tmp = sb("ptmp", [P, T])
        rs = sb("prs", [P, T])
        xT = sb("pxT", [P, CT, S])
        padrow = sb("padrow", [1, W])

        y_bank = [ps(f"y_bank{i}") for i in range(2)]
        t_bank = [ps(f"t_bank{i}") for i in range(2)]
        l_bank = [ps(f"l_bank{i}") for i in range(2)]
        c_bank = ps("c_bank")
        d_bank = ps("d_bank")

        w_in = sem("b_w_in")
        w_in2 = sem("b_w_in2")
        in_s = [sem(f"b_in{i}") for i in range(2)]
        setup = sem("b_setup")
        pad_made = sem("b_pad_made")
        nan_s = sem("b_nan")
        const_pe = sem("b_const_pe")
        const_act = sem("b_const_act")
        blended = sem("b_blended")
        biased = sem("b_biased")
        y_full = sem("b_y_full")
        x1_done = sem("b_x1_done")
        stats_done = sem("b_stats")
        aggr_done = sem("b_aggr")
        sqrt_done = sem("b_sqrt")
        newton = sem("b_newton")
        kept_stats = sem("b_kept")
        xn_done = sem("b_xn")
        t_full = sem("b_t_full")
        t_read = sem("b_t_read")
        l_full = sem("b_l_full")
        l_read = sem("b_l_read")
        stored = [sem(f"b_stored{i}") for i in range(2)]
        pad_out = sem("b_pad_out")

        ident, ones, gate2 = keep["ident"], keep["ones"], keep["gate2"]
        xr = x.rearrange("b (t p) c -> b p t c", p=P)
        ar = attn_dram.rearrange("(b g) p s -> b p g s", g=CT)
        orow = out.rearrange("b (t p) c -> b p t c", p=P)
        rrow = rows_dram[0:N, :].rearrange("(b t p) w -> b p t w", p=P, t=T)

        def at(t, b):
            if isinstance(b, int):
                return t[b]
            names = "p t c" if len(t.shape) == 4 else "p c"
            return t[bass.ds(b, 1)].rearrange(f"o {names} -> (o {names.split()[0]}) {' '.join(names.split()[1:])}")

        block = ctx.enter_context(nc.Block())

        @block.sync
        def _(sp):
            sp.dma_start(wo[:], Wo.rearrange("(t p) n -> p t n", p=P)).then_inc(w_in, 16)
            sp.dma_start(bvT[:], bv.rearrange("(t p) -> p t", p=P), allow_slow_non_contiguous=True).then_inc(w_in, 16)
            sp.dma_start(bo_b[:], bo.rearrange("(o n) -> o n", o=1).to_broadcast([P, C])).then_inc(w_in, 16)
            sp.dma_start(rw[:], router_w).then_inc(w_in, 16)
            sp.dma_start(gate[:], g_xattn.rearrange("(o n) -> o n", o=1).to_broadcast([P, 1])).then_inc(w_in2, 16)
            sp.dma_start(gate2[:], g_ffn.rearrange("(o n) -> o n", o=1).to_broadcast([P, 1])).then_inc(w_in2, 16)

            def pair(i):
                for u in range(2):
                    wait_apart(sp, keep, y_full, i * 2 * T, (u - 1) * T)
                    wait_apart(sp, keep, stored[u], i * 32, 0)
                    wait_apart(sp, keep, xn_done, i * 2 * T, (u - 1) * T)
                    b = 2 * i + u
                    sp.dma_start(att[u][:], at(ar, b)).then_inc(in_s[u], 16)
                    sp.dma_start(meanv[u][:], at(mean_dram, b)).then_inc(in_s[u], 16)
                    sp.dma_start(xs[u][:], at(xr, b)).then_inc(in_s[u], 16)

            pair(0)
            with sp.Fori(1, B // 2) as i:
                pair(i)

        @block.gpsimd
        def _(pool):
            pool.memset(padrow[:], 0.0).then_inc(pad_made, 1)
            pool.wait_ge(pad_made, 1)
            pool.dma_start(rows_dram[N:N + 1, :], padrow[:]).then_inc(pad_out, 16)
            pool.wait_ge(nan_s, 5)

            def pair(i):
                for u in range(2):
                    b = 2 * i + u
                    wait_apart(pool, keep, in_s[u], i * 48, 48)
                    pool.tensor_tensor(xs[u][:], xs[u][:], bo_b[:].unsqueeze(1).to_broadcast([P, T, C]), ALU.add).then_inc(biased, 1)

                    wait_apart(pool, keep, x1_done, i * 2 * T, (u + 1) * T)
                    pool.dma_start(at(orow, b), xs[u][:]).then_inc(stored[u], 16)
                    pool.dma_start(at(rrow, b)[:, :, 0:C], xs[u][:]).then_inc(stored[u], 16)

            pair(0)
            with pool.Fori(1, B // 2) as i:
                pair(i)
            for u in range(2):
                pool.wait_ge(stored[u], 32 * (B // 2))
            pool.wait_ge(pad_out, 16)

        @block.tensor
        def _(pe):
            pe.wait_ge(w_in, 64)
            for g in range(CT):
                last = pe.matmul(c_bank[:], bvT[:, g:g + 1].to_broadcast([P, P]), wo[:, g, :], start=(g == 0), stop=(g == CT - 1))
            last.then_inc(const_pe, 1)
            for c in range(CT):
                last = pe.transpose(d_bank[:, c * E:(c + 1) * E], rw[:, c * P:(c + 1) * P], ident[0:E, 0:E])
            last.then_inc(const_pe, 1)
            pe.wait_ge(const_act, 2)
            pe.wait_ge(nan_s, 1)
            pe.matmul(d_bank[:, 0:1], ones[:], nan_row[:], start=True, stop=True).then_inc(const_pe, 1)

            def products(i, u):
                wait(pe, blended, i * 2, u + 1)
                for t in range(T):
                    wait(pe, x1_done, i * 2 * T, u * T + t - 1)
                    for g in range(CT):
                        last = pe.matmul(y_bank[t % 2][:], att[u][:, g, t * P:(t + 1) * P], wo[:, g, :], start=(g == 0), stop=(g == CT - 1))
                    last.then_inc(y_full, 1)

            def route(i, u):
                wait(pe, xn_done, i * 2 * T, (u + 1) * T)
                for c in range(CT):
                    wait(pe, t_read, i * 2 * CT, u * CT + c - 1)
                    for t in range(T):
                        last = pe.transpose(t_bank[c % 2][:, t * P:(t + 1) * P], xn[u][:, t, c * P:(c + 1) * P], ident[:])
                    last.then_inc(t_full, 1)
                wait(pe, t_read, i * 2 * CT, (u + 1) * CT)
                wait(pe, l_read, i * 2, u - 1)
                for t in range(T):
                    for c in range(CT):
                        last = pe.matmul(l_bank[u][:, t * E:(t + 1) * E], xT[:, c, t * P:(t + 1) * P], rwT[:, c, :],
                                         start=(c == 0), stop=(c == CT - 1))
                last.then_inc(l_full, 1)

            products(0, 0)
            products(0, 1)
            route(0, 0)
            with pe.Fori(1, B // 2) as i:
                products(i, 0)
                route(i - 1, 1)
                products(i, 1)
                route(i, 0)
            route(B // 2 - 1, 1)

        @block.scalar
        def _(act):
            act.wait_ge(w_in2, 32)
            act.activation(gate[:], gate[:], ACT.Tanh).then_inc(const_act, 1)
            act.activation(gate2[:], gate2[:], ACT.Tanh)
            act.wait_ge(const_pe, 2)
            act.activation(rwT[:], d_bank[:, 0:CT * E], ACT.Identity).then_inc(const_act, 1)

            def deviation(i, u):
                wait(act, aggr_done, i * 2 * T, (u + 1) * T)
                wait(act, newton, i * 10, 5 * u)
                act.activation(sd[:], mv[:, :, 1], ACT.Sqrt, bias=keep["eps"][:, 0:1]).then_inc(sqrt_done, 1)

            def read_turned(i, u):
                wait(act, l_full, i * 2, u)
                for c in range(CT):
                    wait(act, t_full, i * 2 * CT, u * CT + c + 1)
                    act.activation(xT[:, c, :], t_bank[c % 2][:], ACT.Identity).then_inc(t_read, 1)
                wait(act, l_full, i * 2, u + 1)
                b = 2 * i + u
                dst = keep["logits"][:, b * T:(b + 1) * T, :] if isinstance(i, int) else keep["logits"][:, bass.ds(b * T, T), :]
                act.activation(dst, l_bank[u][:, 0:T * E].rearrange("p (t e) -> p t e", t=T), ACT.Identity).then_inc(l_read, 1)

            deviation(0, 0)
            deviation(0, 1)
            read_turned(0, 0)
            with act.Fori(1, B // 2) as i:
                deviation(i, 0)
                read_turned(i - 1, 1)
                deviation(i, 1)
                read_turned(i, 0)
            read_turned(B // 2 - 1, 1)

        @block.vector
        def _(dve):
            dve.tensor_reduce(nan_row[:], keep["nan_acc"][:], AX_X, ALU.add).then_inc(nan_s, 1)
            dve.wait_ge(const_pe, 3)
            dve.tensor_copy(nan_tot[:], d_bank[:, 0:1]).then_inc(nan_s, 1)
            dve.wait_ge(nan_s, 2)
            dve.tensor_tensor(nan_f[:], nan_tot[:], nan_tot[:], ALU.not_equal).then_inc(nan_s, 1)
            dve.wait_ge(nan_s, 3)
            dve.tensor_copy(nan_mask[:], nan_f[:]).then_inc(nan_s, 1)
            dve.wait_ge(const_act, 1)
            dve.tensor_tensor(bo_b[:], c_bank[:], bo_b[:], ALU.add).then_inc(setup, 1)
            dve.wait_ge(setup, 1)
            dve.tensor_scalar(bo_b[:], bo_b[:], gate[:, 0:1], None, ALU.mult).then_inc(nan_s, 1)
            dve.wait_ge(nan_s, 5)

            def blend(i, u):
                wait_apart(dve, keep, in_s[u], i * 48, 48)
                dve.copy_predicated(att[u][:], nan_mask[:, 0:1].unsqueeze(2).to_broadcast([P, CT, S]),
                                    meanv[u][:].unsqueeze(2).to_broadcast([P, CT, S])).then_inc(blended, 1)

            def residual(i, u):
                wait(dve, biased, i * 2, u + 1)
                for t in range(T):
                    wait(dve, y_full, i * 2 * T, u * T + t + 1)
                    dve.scalar_tensor_tensor(out=xs[u][:, t, :], in0=y_bank[t % 2][:], scalar=gate[:, 0:1], in1=xs[u][:, t, :],
                                             op0=ALU.mult, op1=ALU.add).then_inc(x1_done, 1)
                wait(dve, xn_done, i * 2 * T, u * T)
                wait(dve, kept_stats, i * 4, 2 * u)
                for t in range(T):
                    wait(dve, x1_done, i * 2 * T, u * T + t + 1)
                    dve.bn_stats(stats[:, t, :], xs[u][:, t, :]).then_inc(stats_done, 1)
                wait_apart(dve, keep, stats_done, i * 2 * T, (u + 1) * T)
                for t in range(T):
                    dve.bn_aggr(mv[:, t, :], stats[:, t, :]).then_inc(aggr_done, 1)

            def normalise(i, u):
                b = 2 * i + u
                wait(dve, sqrt_done, i * 2, u + 1)
                newton_rsqrt(dve, newton, i * 10, 5 * u, mv[:, :, 1], sd[:], r0[:], tmp[:], rs[:])
                wait(dve, newton, i * 10, 5 * u + 5)
                wait(dve, t_full, i * 2 * CT, (u - 1) * CT)
                for t in range(T):
                    dve.tensor_scalar(xn[u][:, t, :], xs[u][:, t, :], mv[:, t, 0:1], rs[:, t:t + 1],
                                      ALU.subtract, ALU.mult).then_inc(xn_done, 1)
                rows = slice(b * T, (b + 1) * T) if isinstance(i, int) else bass.ds(b * T, T)
                dve.tensor_copy(keep["token"][:, rows, 0], mv[:, :, 0]).then_inc(kept_stats, 1)
                dve.tensor_copy(keep["token"][:, rows, 1], rs[:]).then_inc(kept_stats, 1)

            def pair(i):
                for u in range(2):
                    blend(i, u)
                    residual(i, u)
                    normalise(i, u)

            pair(0)
            with dve.Fori(1, B // 2) as i:
                pair(i)


def routing(nc, keep, N, E, CAP, C, rows_dram, table):
    NT = N // P
    NONE = 2 * E * CAP
    with ExitStack() as ctx:
        sb, ps, sem = make_pools(nc, ctx)
        mx = sb("mx", [P, NT])
        e_ = sb("e_", [P, NT, E])
        sm = sb("sm", [P, NT])
        ri = sb("ri", [P, NT])
        pr = sb("pr", [P, NT, E])
        rank = sb("rank", [P, E])
        first = sb("first", [P, E])
        oh = sb("oh", [P, NT, E])
        tot = sb("tot", [P, E, NT])
        run = sb("run", [P, E, NT])
        one = sb("one", [P, NT])
        pos = sb("pos", [P, NT, E])
        keepm = sb("keepm", [P, NT, E])
        base = sb("base", [P, E])
        slot_f = sb("slot_f", [P, NT])
        slot = sb("slot", [P, NT], I32)
        tok = sb("tok", [P, NT], I32)
        tri = sb("tri", [P, P])
        pad = sb("pad", [P, E * CAP // P], I32)
        a_bank = ps("a_bank")
        b_bank = ps("b_bank")
        ch = sem("c_chain")
        ex = sem("c_exp")
        cn = sem("c_counts")
        token_ready = sem("c_token")
        chosen_ready = sem("c_chosen")
        slot_ready = sem("c_slot")
        setup = sem("c_setup")
        pad_s = sem("c_pad")
        sc = sem("c_scatter")
        st = sem("c_stats_out")
        block = ctx.enter_context(nc.Block())
        logits, token = keep["logits"], keep["token"]
        bc = lambda t: t.unsqueeze(2).to_broadcast([P, NT, E])
        ec = lambda t: t.unsqueeze(1).to_broadcast([P, NT, E])

        @block.gpsimd
        def _(pool):
            pool.iota(pad[:], pattern=[[0, E * CAP // P]], base=N, channel_multiplier=0).then_inc(setup, 1)
            pool.iota(tok[:], pattern=[[P, NT]], base=0, channel_multiplier=1).then_inc(setup, 1)
            pool.iota(rank[:], pattern=[[-1, E]], base=E, channel_multiplier=0, allow_small_or_imprecise_dtypes=True).then_inc(setup, 1)
            pool.iota(base[:], pattern=[[CAP, E]], base=-1 - NONE, channel_multiplier=0, allow_small_or_imprecise_dtypes=True).then_inc(setup, 1)
            pool.memset(tri[:], 1.0).then_inc(setup, 1)
            pool.memset(first[:], 0.0).then_inc(setup, 1)
            pool.memset(one[:], 1.0).then_inc(setup, 1)
            pool.wait_ge(setup, 7)
            pool.affine_select(out=tri[:], in_=tri[:], compare_op=ALU.is_ge, fill=0.0, base=0, pattern=[[1, P]],
                               channel_multiplier=-1).then_inc(setup, 1)
            pool.memset(first[:, 0:1], 0.5).then_inc(setup, 1)
            pool.dma_start(table.rearrange("(p k) o -> p (k o)", p=P), pad[:]).then_inc(pad_s, 16)
            pool.wait_ge(pad_s, 16)
            pool.wait_ge(slot_ready, 1)
            for t in range(NT):
                pool.indirect_dma_start(table, bass.IndirectOffsetOnAxis(ap=slot[:, t:t + 1], axis=0), tok[:, t:t + 1], None,
                                        bounds_check=E * CAP - 1, oob_is_err=False).then_inc(sc, 16)
            pool.wait_ge(sc, 16 * NT)

        @block.sync
        def _(sp):
            sp.wait_ge(token_ready, 1)
            sp.dma_start(rows_dram[0:N, C:C + 4].rearrange("(t p) w -> p t w", p=P), token[:],
                         allow_slow_non_contiguous=True).then_inc(st, 16)
            sp.wait_ge(st, 16)

        @block.scalar
        def _(act):
            act.wait_ge(ch, 2)
            act.activation(e_[:], e_[:], ACT.Exp).then_inc(ex, 1)

        @block.tensor
        def _(pe):
            pe.wait_ge(chosen_ready, 1)
            pe.wait_ge(setup, 9)
            flat = oh[:].rearrange("p t e -> p (t e)")
            pe.matmul(a_bank[:, 0:NT * E], tri[:], flat, start=True, stop=True).then_inc(cn, 1)
            pe.matmul(b_bank[:, 0:NT * E], keep["ones"][:], flat, start=True, stop=True).then_inc(cn, 1)

        @block.vector
        def _(dve):
            n = [0]

            def step(ins):
                n[0] += 1
                ins.then_inc(ch, 1)
                dve.wait_ge(ch, n[0])

            step(dve.tensor_reduce(mx[:], logits[:], AX_X, ALU.max))
            step(dve.tensor_tensor(e_[:], logits[:], bc(mx[:]), ALU.subtract))
            dve.wait_ge(ex, 1)
            step(dve.tensor_reduce(sm[:], e_[:], AX_X, ALU.add))
            step(dve.reciprocal(ri[:], sm[:]))
            step(dve.tensor_tensor(pr[:], e_[:], bc(ri[:]), ALU.mult))
            step(dve.tensor_reduce(mx[:], pr[:], AX_X, ALU.max))
            dve.tensor_copy(token[:, :, 2], mx[:]).then_inc(token_ready, 1)
            step(dve.tensor_tensor(pr[:], pr[:], bc(mx[:]), ALU.is_equal))
            dve.wait_ge(setup, 9)
            step(dve.tensor_tensor(pr[:], pr[:], ec(rank[:]), ALU.mult))
            step(dve.tensor_tensor(pr[:], pr[:], ec(first[:]), ALU.max))
            step(dve.tensor_reduce(mx[:], pr[:], AX_X, ALU.max))
            dve.tensor_tensor(oh[:], pr[:], bc(mx[:]), ALU.is_equal).then_inc(chosen_ready, 1)
            dve.wait_ge(cn, 2)
            step(dve.tensor_copy(tot[:].rearrange("p e t -> p t e"), b_bank[:, 0:NT * E].rearrange("p (t e) -> p t e", t=NT)))
            for x in range(E):
                step(dve.tensor_tensor_scan(run[:, x, :], one[:], tot[:, x, :], 0.0, ALU.mult, ALU.add))
            step(dve.tensor_tensor(run[:], run[:], tot[:], ALU.subtract))
            step(dve.tensor_tensor(pos[:], a_bank[:, 0:NT * E].rearrange("p (t e) -> p t e", t=NT), run[:].rearrange("p e t -> p t e"), ALU.add))
            step(dve.tensor_scalar(keepm[:], pos[:], float(CAP), None, ALU.is_le))
            step(dve.tensor_tensor(pos[:], pos[:], ec(base[:]), ALU.add))
            step(dve.tensor_tensor(keepm[:], keepm[:], oh[:], ALU.mult))
            step(dve.tensor_tensor(pos[:], pos[:], keepm[:], ALU.mult))
            step(dve.tensor_reduce(slot_f[:], pos[:], AX_X, ALU.add))
            dve.tensor_scalar(slot[:], slot_f[:], float(NONE), None, ALU.add).then_inc(slot_ready, 1)


def experts(nc, keep, w1, b1, w2, b2, rows_dram, table, out, CAP):
    E, C, FF = w1.shape
    W = rows_dram.shape[1]
    N = rows_dram.shape[0] - 1
    CT = C // P
    ST = CAP // P
    CH = 4
    FT = FF // P // CH
    FW = FT * P
    HALF = CAP // 2
    TH = HALF // P
    UP = 2 * FT
    TF = 2 * CT
    with ExitStack() as ctx:
        sb, ps, sem = make_pools(nc, ctx)
        w1s = sb("w1s", [P, CT, FW])
        w2s = sb("w2s", [P, FT, C])
        w1h = [sb(f"w1h{i}", [P, CT, FW], F32R) for i in range(2)]
        w1l = [sb(f"w1l{i}", [P, CT, FW], F32R) for i in range(2)]
        w2h = [sb(f"w2h{i}", [P, FT, C], F32R) for i in range(2)]
        w2l = [sb(f"w2l{i}", [P, FT, C], F32R) for i in range(2)]
        b1all = sb("b1all", [P, E * CH * FT])
        b1s = sb("b1s", [P, CH * FT])
        b2b = sb("b2b", [P, C])
        gel = [sb(f"gel{i}", [P, CAP]) for i in range(2)]
        hh = [sb(f"hh{i}", [P, FT, CAP], F32R) for i in range(2)]
        hl = [sb(f"hl{i}", [P, FT, CAP], F32R) for i in range(2)]
        xTh = sb("xTh", [P, CT, CAP], F32R)
        xTl = sb("xTl", [P, CT, CAP], F32R)
        xg = sb("xg", [P, ST, W])
        xn = sb("exn", [P, ST, C])
        res = sb("res", [P, ST, C])
        idx_g = sb("idx_g", [P, ST], I32)
        idx_s = sb("idx_s", [P, ST], I32)
        gp = sb("gp", [P, ST])

        up_bank = [ps(f"up_bank{i}") for i in range(2)]
        y_bank = [ps(f"ey_bank{i}") for i in range(ST)]

        b1_in = sem("d_b1_in")
        b1_set = sem("d_b1_set")
        w1_in = sem("d_w1_in")
        w2_in = sem("d_w2_in")
        b2_in = sem("d_b2_in")
        idx_in = sem("d_idx_in")
        w1h_done = sem("d_w1h")
        w1l_done = sem("d_w1l")
        w2h_done = sem("d_w2h")
        w2l_done = sem("d_w2l")
        rows_in = sem("d_rows_in")
        gp_done = sem("d_gp")
        xn_done = sem("d_xn")
        t_full = sem("d_t_full")
        th_done = sem("d_th")
        tl_done = sem("d_tl")
        up_full = sem("d_up_full")
        gelu_done = sem("d_gelu")
        hh_done = sem("d_hh")
        hl_done = sem("d_hl")
        down_done = sem("d_down")
        y_full = sem("d_y_full")
        res_done = sem("d_res")
        idx_kept = sem("d_idx_kept")
        out_done = sem("d_out_done")
        scattered = sem("d_scattered")

        ident, gate2 = keep["ident"], keep["gate2"]
        w1v = w1.rearrange("e (k p) f -> e p k f", p=P)
        w2v = w2.rearrange("e (c f p) d -> (e c) p f d", p=P, c=CH)
        tv = table.rearrange("(e p k) o -> e p (k o)", e=E, p=P)
        f32 = lambda t: t.bitcast(F32)

        def at(t, i):
            if isinstance(i, int):
                return t[i]
            names = ["p", "k", "f"][:len(t.shape) - 1]
            return t[bass.ds(i, 1)].rearrange(f"o {' '.join(names)} -> (o p) {' '.join(names[1:])}")

        block = ctx.enter_context(nc.Block())

        @block.sync
        def _(sp):
            sp.dma_start(b1all[:], b1.rearrange("e (t p) -> p (e t)", p=P), allow_slow_non_contiguous=True).then_inc(b1_in, 16)

            def load_rows_index(e):
                wait_apart(sp, keep, idx_kept, e, 0)
                sp.dma_start(idx_g[:], at(tv, e)).then_inc(idx_in, 16)

            def expert(e, more):
                wait_apart(sp, keep, gp_done, e, 0)
                wait_apart(sp, keep, res_done, e * ST, 0)
                b2row = b2[e:e + 1] if isinstance(e, int) else b2[bass.ds(e, 1)]
                sp.dma_start(b2b[:], b2row.to_broadcast([P, C])).then_inc(b2_in, 16)
                for c in range(CH):
                    wait_apart(sp, keep, w1l_done, e * CH * CT, c * CT)
                    sp.dma_start(w1s[:], at(w1v, e)[:, :, c * FW:(c + 1) * FW]).then_inc(w1_in, 16)
                    wait_apart(sp, keep, w2l_done, e * CH * FT, c * FT)
                    sp.dma_start(w2s[:], at(w2v, e * CH + c)).then_inc(w2_in, 16)
                    if c == 1 and more:
                        load_rows_index(e + 1)

            load_rows_index(0)
            expert(0, True)
            with sp.Fori(1, E - 1) as e:
                expert(e, True)
            expert(E - 1, False)

        @block.gpsimd
        def _(pool):
            def gather(e):
                wait_apart(pool, keep, idx_in, e * 16, 16)
                wait_apart(pool, keep, xn_done, e * ST, 0)
                wait_apart(pool, keep, res_done, e * ST, 0)
                for k in range(ST):
                    pool.indirect_dma_start(xg[:, k, :], None, rows_dram, bass.IndirectOffsetOnAxis(ap=idx_g[:, k:k + 1], axis=0),
                                            bounds_check=N, oob_is_err=False).then_inc(rows_in, 16)

            def scatter(e):
                for k in range(ST):
                    wait_apart(pool, keep, out_done, e * ST, k + 1)
                    pool.indirect_dma_start(out, bass.IndirectOffsetOnAxis(ap=idx_s[:, k:k + 1], axis=0), res[:, k, :], None,
                                            bounds_check=N - 1, oob_is_err=False).then_inc(scattered, 16)

            gather(0)
            gather(1)
            scatter(0)
            with pool.Fori(1, E - 1) as e:
                gather(e + 1)
                scatter(e)
            scatter(E - 1)
            pool.wait_ge(scattered, 16 * ST * E)

        @block.tensor
        def _(pe):
            def turn(e):
                wait(pe, xn_done, e * ST, ST)
                for n in range(TF):
                    c, half = n // 2, n % 2
                    if n < 2:
                        wait(pe, gelu_done, e * CH * UP, n - 1)
                    else:
                        wait(pe, tl_done, e * TF, n - 1)
                    for k in range(TH):
                        t = half * TH + k
                        last = pe.transpose(up_bank[n % 2][:, k * P:(k + 1) * P], xn[:, t, c * P:(c + 1) * P], ident[:])
                    last.then_inc(t_full, 1)

            def up(e, c):
                s = c % 2
                wait(pe, w1l_done, e * CH * CT, (c + 1) * CT)
                if c == 0:
                    wait(pe, tl_done, e * TF, TF)
                for n in range(UP):
                    f, half = n // 2, n % 2
                    if c > 0 or n > 1:
                        wait(pe, gelu_done, e * CH * UP, c * UP + n - 1)
                    parts = ((w1l[s], xTh), (w1h[s], xTl), (w1h[s], xTh))
                    for i, (w, t) in enumerate(parts):
                        for k in range(CT):
                            last = pe.matmul(up_bank[n % 2][:, 0:HALF], w[:, k, f * P:(f + 1) * P], t[:, k, half * HALF:(half + 1) * HALF],
                                             start=(i == 0 and k == 0), stop=(i == 2 and k == CT - 1))
                    last.then_inc(up_full, 1)

            def down(e, c):
                s = c % 2
                wait(pe, hl_done, e * CH * FT, (c + 1) * FT)
                wait(pe, w2l_done, e * CH * FT, (c + 1) * FT)
                for k in range(ST):
                    if c == 0:
                        wait(pe, out_done, e * ST, k + 1 - ST)
                    parts = ((hl[s], w2h[s]), (hh[s], w2l[s]), (hh[s], w2h[s]))
                    for i, (h, w) in enumerate(parts):
                        for f in range(FT):
                            last = pe.matmul(y_bank[k][:], h[:, f, k * P:(k + 1) * P], w[:, f, :],
                                             start=(c == 0 and i == 0 and f == 0), stop=(c == CH - 1 and i == 2 and f == FT - 1))
                    if c == CH - 1:
                        last.then_inc(y_full, 1)
                    elif k == ST - 1:
                        last.then_inc(down_done, 1)

            def expert(e, more):
                up(e, 0)
                up(e, 1)
                down(e, 0)
                up(e, 2)
                down(e, 1)
                up(e, 3)
                down(e, 2)
                if more:
                    turn(e + 1)
                down(e, 3)

            turn(0)
            expert(0, True)
            with pe.Fori(1, E - 1) as e:
                expert(e, True)
            expert(E - 1, False)

        def downs(e, c):
            if c == CH - 1:
                return y_full, e * ST, ST
            return down_done, e * (CH - 1), c + 1

        @block.scalar
        def _(act):
            def w1_high(e, c, k):
                s = c % 2
                if k == 0:
                    wait(act, w1_in, e * CH * 16, (c + 1) * 16)
                    wait(act, up_full, e * CH * UP, (c - 1) * UP)
                act.activation(w1h[s][:, k, :], w1s[:, k, :], ACT.Copy).then_inc(w1h_done, 1)

            def w2_high(e, c, k):
                s = c % 2
                if k == 0:
                    wait(act, w2_in, e * CH * 16, (c + 1) * 16)
                    if c >= 2:
                        wait(act, *downs(e, c - 2))
                    elif not (isinstance(e, int) and e == 0):
                        wait(act, *downs(e - 1, c + 2))
                act.activation(w2h[s][:, k, :], w2s[:, k, :], ACT.Copy).then_inc(w2h_done, 1)

            def turned(e):
                for n in range(TF):
                    c, half = n // 2, n % 2
                    wait(act, t_full, e * TF, n + 1)
                    act.activation(xTh[:, c, half * HALF:(half + 1) * HALF], up_bank[n % 2][:, 0:HALF], ACT.Copy).then_inc(th_done, 1)

            def expert(e, more):
                wait(act, b1_set, e, 1)
                for c in range(CH):
                    for n in range(UP):
                        f, half = n // 2, n % 2
                        wait(act, up_full, e * CH * UP, c * UP + n + 1)
                        if half == 0:
                            wait(act, hl_done, e * CH * FT, c * FT + f - 1)
                        act.activation(gel[f % 2][:, half * HALF:(half + 1) * HALF], up_bank[n % 2][:, 0:HALF], ACT.Gelu,
                                       bias=b1s[:, c * FT + f:c * FT + f + 1]).then_inc(gelu_done, 1)
                        if n < CT:
                            w2_high(e, c, n)
                        elif c < CH - 1:
                            w1_high(e, c + 1, n - CT)
                        elif more:
                            w1_high(e + 1, 0, n - CT)
                if more:
                    turned(e + 1)

            for k in range(CT):
                w1_high(0, 0, k)
            turned(0)
            expert(0, True)
            with act.Fori(1, E - 1) as e:
                expert(e, True)
            expert(E - 1, False)

        @block.vector
        def _(dve):
            def w1_low(e, c, k):
                wait(dve, w1h_done, e * CH * CT, c * CT + k + 1)
                if k == 0:
                    wait(dve, up_full, e * CH * UP, (c - 1) * UP)
                s = c % 2
                dve.tensor_tensor(w1l[s][:, k, :], w1s[:, k, :], f32(w1h[s][:, k, :]), ALU.subtract).then_inc(w1l_done, 1)

            def w2_low(e, c, k):
                wait(dve, w2h_done, e * CH * FT, c * FT + k + 1)
                s = c % 2
                dve.tensor_tensor(w2l[s][:, k, :], w2s[:, k, :], f32(w2h[s][:, k, :]), ALU.subtract).then_inc(w2l_done, 1)

            def normalise(e):
                wait(dve, rows_in, e * 16 * ST, 16 * ST)
                wait(dve, t_full, e * TF, 0)
                for k in range(ST):
                    dve.tensor_scalar(xn[:, k, :], xg[:, k, 0:C], xg[:, k, C:C + 1], xg[:, k, C + 1:C + 2],
                                      ALU.subtract, ALU.mult).then_inc(xn_done, 1)

            def turned(e):
                for n in range(TF):
                    c, half = n // 2, n % 2
                    cols = slice(half * HALF, (half + 1) * HALF)
                    wait(dve, th_done, e * TF, n + 1)
                    dve.tensor_tensor(xTl[:, c, cols], up_bank[n % 2][:, 0:HALF], f32(xTh[:, c, cols]), ALU.subtract).then_inc(tl_done, 1)

            def set_bias(e):
                src = b1all[:, e * CH * FT:(e + 1) * CH * FT] if isinstance(e, int) else b1all[:, bass.ds(e * CH * FT, CH * FT)]
                wait(dve, gelu_done, e * CH * UP, 0)
                dve.tensor_copy(b1s[:], src).then_inc(b1_set, 1)

            def residual(e):
                wait(dve, b2_in, e * 16, 16)
                dve.tensor_scalar(gp[:], xg[:, :, C + 2], gate2[:, 0:1], None, ALU.mult).then_inc(gp_done, 1)
                wait(dve, scattered, e * 16 * ST, 0)
                dve.tensor_copy(idx_s[:], idx_g[:]).then_inc(idx_kept, 1)
                wait(dve, gp_done, e, 1)
                for k in range(ST):
                    dve.scalar_tensor_tensor(out=res[:, k, :], in0=b2b[:], scalar=gp[:, k:k + 1], in1=xg[:, k, 0:C],
                                             op0=ALU.mult, op1=ALU.add).then_inc(res_done, 1)

            def finish(e):
                for k in range(ST):
                    wait(dve, y_full, e * ST, k + 1)
                    wait(dve, res_done, e * ST, k + 1)
                    dve.scalar_tensor_tensor(out=res[:, k, :], in0=y_bank[k][:], scalar=gp[:, k:k + 1], in1=res[:, k, :],
                                             op0=ALU.mult, op1=ALU.add).then_inc(out_done, 1)

            def expert(e, more):
                for c in range(CH):
                    s = c % 2
                    for f in range(FT):
                        wait(dve, gelu_done, e * CH * UP, c * UP + 2 * f + 2)
                        if f == 0:
                            if c >= 2:
                                wait(dve, *downs(e, c - 2))
                            elif not (isinstance(e, int) and e == 0):
                                wait(dve, *downs(e - 1, c + 2))
                        dve.tensor_copy(hh[s][:, f, :], gel[f % 2][:]).then_inc(hh_done, 1)
                        if f < 2:
                            w2_low(e, c, 2 * f)
                            w2_low(e, c, 2 * f + 1)
                        elif c < CH - 1 or more:
                            nxt = (e, c + 1) if c < CH - 1 else (e + 1, 0)
                            w1_low(*nxt, 2 * f - CT)
                            w1_low(*nxt, 2 * f - CT + 1)
                        wait(dve, hh_done, e * CH * FT, c * FT + f + 1)
                        dve.tensor_tensor(hl[s][:, f, :], gel[f % 2][:], f32(hh[s][:, f, :]), ALU.subtract).then_inc(hl_done, 1)
                    if c == 0:
                        residual(e)
                    if c == 2 and more:
                        normalise(e + 1)
                if more:
                    set_bias(e + 1)
                    turned(e + 1)
                finish(e)

            dve.wait_ge(b1_in, 16)
            set_bias(0)
            normalise(0)
            for k in range(CT):
                w1_low(0, 0, k)
            turned(0)
            expert(0, True)
            with dve.Fori(1, E - 1) as e:
                expert(e, True)
            expert(E - 1, False)


def program(nc, x, ctx_768, g_xattn, g_ffn, Wq, bq, Wk, bk, Wv, bv, Wo, bo, router_w, w1, b1, w2, b2, out):
    B, S, C = x.shape
    N = B * S
    E = router_w.shape[0]
    CAP = -(-3 * N // (2 * E))
    CT = C // P
    attn_dram = nc.dram_tensor("attn_dram", [B * CT, P, S], F32).ap()
    mean_dram = nc.dram_tensor("mean_dram", [B, P, CT], F32).ap()
    rows_dram = nc.dram_tensor("rows_dram", [N + 1, C + 4], F32).ap()
    table = nc.dram_tensor("table", [E * CAP, 1], I32).ap()
    flat_out = out.rearrange("b s c -> (b s) c")
    with ExitStack() as ctx:
        def sb(name, shape, dt=F32):
            return ctx.enter_context(nc.sbuf_tensor(name, shape, dt))

        keep = {
            "ident": sb("ident", [P, P]),
            "ones": sb("ones", [P, P]),
            "eps": sb("eps", [P, 1]),
            "nan_acc": sb("nan_acc", [P, B * CT]),
            "gate2": sb("gate2", [P, 1]),
            "logits": sb("logits", [P, N // P, E]),
            "token": sb("token", [P, N // P, 4]),
        }
        made = ctx.enter_context(nc.semaphore("made"))
        keep["passed"] = ctx.enter_context(nc.semaphore("passed"))
        with nc.Block() as block:
            @block.gpsimd
            def _(pool):
                pool.memset(keep["ident"][:], 0.0).then_inc(made, 1)
                pool.memset(keep["ones"][:], 1.0).then_inc(made, 1)
                pool.memset(keep["eps"][:], EPS).then_inc(made, 1)
                pool.memset(keep["token"][:], 0.0).then_inc(made, 1)
                pool.wait_ge(made, 4)
                pool.affine_select(out=keep["ident"][:], in_=keep["ident"][:], compare_op=ALU.not_equal, fill=1.0, base=0,
                                   pattern=[[-1, P]], channel_multiplier=1).then_inc(made, 1)
                pool.wait_ge(made, MADE)
        attention(nc, keep, x, ctx_768, Wq, bq, Wk, bk, Wv, attn_dram, mean_dram)
        projection(nc, keep, x, bv, Wo, bo, g_xattn, g_ffn, router_w, attn_dram, mean_dram, rows_dram, out)
        routing(nc, keep, N, E, CAP, C, rows_dram, table)
        experts(nc, keep, w1, b1, w2, b2, rows_dram, table, flat_out, CAP)


_INS = ["x", "ctx_768", "g_xattn", "g_ffn", "L0_xattn_Wq", "L0_xattn_bq", "L0_xattn_Wk", "L0_xattn_bk", "L0_xattn_Wv",
        "L0_xattn_bv", "L0_xattn_Wo", "L0_xattn_bo", "L0_ffn_router_w", "L0_ffn_w1", "L0_ffn_b1", "L0_ffn_w2", "L0_ffn_b2"]


def kernel(**inputs):
    import numpy as np
    import concourse.bacc as bacc
    from concourse.bass_utils import run_bass_kernel_spmd

    nc = bacc.Bacc("TRN2", target_bir_lowering=False, num_devices=1)
    arrays, args = {}, []
    for name in _INS:
        a = np.ascontiguousarray(inputs[name])
        arrays[f"in_{name}"] = a
        args.append(nc.dram_tensor(f"in_{name}", a.shape, mybir.dt.from_np(a.dtype), kind="ExternalInput").ap())
    args.append(nc.dram_tensor("out_0", inputs["x"].shape, F32, kind="ExternalOutput").ap())
    program(nc, *args)
    return run_bass_kernel_spmd(nc, [arrays], core_ids=[0]).results[0]["out_0"]
```

```python
from contextlib import ExitStack

import concourse.bass as bass
from concourse import mybir

F32 = mybir.dt.float32
F32R = mybir.dt.float32r
I32 = mybir.dt.int32
ALU = mybir.AluOpType
ACT = mybir.ActivationFunctionType
AX_X = mybir.AxisListType.X
P = 128
EPS = 1e-5
CLAMP = 10000.0
HEADS = 16
MADE = 5


def wait(eng, sem, base, count):
    if isinstance(base, int) and base + count <= 0:
        return
    eng.wait_ge(sem, base + count)


def wait_apart(eng, keep, sem, base, count):
    wait(eng, sem, base, count)
    if not isinstance(base, int):
        eng.sem_inc(keep["passed"], 1)


def make_pools(nc, ctx):
    def sb(name, shape, dt=F32):
        return ctx.enter_context(nc.sbuf_tensor(name, shape, dt))

    def ps(name):
        return ctx.enter_context(nc.psum_tensor(name, [P, 512], F32))

    def sem(name):
        return ctx.enter_context(nc.semaphore(name))

    return sb, ps, sem


def newton_rsqrt(dve, chain, base, n, var, sd, r0, tmp, r):
    dve.reciprocal(r0, sd).then_inc(chain, 1)
    wait(dve, chain, base, n + 1)
    dve.tensor_tensor(tmp, r0, r0, ALU.mult).then_inc(chain, 1)
    wait(dve, chain, base, n + 2)
    dve.scalar_tensor_tensor(out=tmp, in0=var, scalar=EPS, in1=tmp, op0=ALU.add, op1=ALU.mult).then_inc(chain, 1)
    wait(dve, chain, base, n + 3)
    dve.tensor_scalar(tmp, tmp, -0.5, 1.5, ALU.mult, ALU.add).then_inc(chain, 1)
    wait(dve, chain, base, n + 4)
    dve.tensor_tensor(r, r0, tmp, ALU.mult).then_inc(chain, 1)


def attention(nc, keep, x, ctx_in, Wq, bq, Wk, bk, Wv, attn_dram, mean_dram):
    B, S, C = x.shape
    CK = ctx_in.shape[2]
    T = S // P
    CT, CKT = C // P, CK // P
    HG = HEADS // CT
    D = C // HEADS
    R3 = 3 * D
    STACK = 3 * 16
    SCALE = float(D) ** -0.5
    EXP, TURN, LOW, WEIGH, JOIN = 1, 3, 0, 6, 10
    QB = HEADS * T
    assert T == 4 and HG == 4 and CT == 4

    PLAN = [(4, "sum", CT - 1, False), (7, "q", 1, False), (10, "k", 1, False)]
    PLAN += [(12 + 2 * t, "v", T + t, False) for t in range(T)]
    PLAN += [(21, "q", 2, False), (22, "sum", 0, False), (25, "k", 2, False)]
    PLAN += [(32, "q", 3, False), (35, "k", 3, False), (37, "sum", 1, False)]
    PLAN += [(38 + c, "x", c, True) for c in range(CT)] + [(42 + c, "c", c, True) for c in range(CKT)]
    PLAN += [(48, "q", 0, True), (51, "k", 0, True), (53, "sum", 2, False)]
    PLAN += [(55 + 2 * t, "v", t, True) for t in range(T)] + [(63, "mean", 0, True)]
    SPLIT = ("q", "k", "v", "x", "c")
    HEAD = [f for f in PLAN if f[3]]

    def fills(b):
        if b < 0:
            return HEAD
        if b == B:
            return PLAN[:1]
        return [f for f in PLAN if not (b == 0 and f is PLAN[0]) and not (b == B - 1 and f[3])]

    def before(b, fill, kinds=None):
        count = lambda fs: sum(1 for f in fs if kinds is None or f[1] in kinds)
        if isinstance(b, int):
            fs = fills(b)
            return 0, sum(count(fills(c)) for c in range(-1, b)) + count(fs[:fs.index(fill)])
        return b * count(PLAN), count(HEAD) + count(fills(0)) - count(PLAN) + count(PLAN[:PLAN.index(fill)])

    def upto(b, fill, kinds=None):
        base, num = before(b, fill, kinds)
        return base, num + 1

    def planned(kind, n):
        return next(f for f in PLAN if f[1:3] == (kind, n))

    def plan_at(b, quarter):
        return [f for f in (fills(b) if isinstance(b, int) else PLAN) if f[0] == quarter]

    def quarters(b):
        return range(QB) if not (isinstance(b, int) and b == B) else range(JOIN + T)

    def tile_at(b, quarter, trail):
        n = quarter - trail
        if isinstance(b, int) and (b == 0 and n < 0 or b == B and n >= 0):
            return None
        return n

    def run(eng, body):
        body(0)
        with eng.Fori(1, B - 1) as b:
            body(b)
        body(B - 1)
        body(B)

    with ExitStack() as ctx:
        sb, ps, sem = make_pools(nc, ctx)
        wqh, wql = sb("wqh", [P, CT, C], F32R), sb("wql", [P, CT, C], F32R)
        wkh, wkl = sb("wkh", [P, CKT, C], F32R), sb("wkl", [P, CKT, C], F32R)
        wvh, wvl = sb("wvh", [P, CKT, C], F32R), sb("wvl", [P, CKT, C], F32R)
        bqT = sb("bqT", [P, CT])
        bkT = sb("bkT", [P, CT])
        xn = sb("xn", [P, T, C])
        cx = sb("cx", [P, T, CK])
        stats = sb("stats", [P, T, 6])
        mv = sb("mv", [P, T, 2])
        sd = sb("sd", [P, T])
        r0 = sb("r0", [P, T])
        tmp = sb("tmp", [P, T])
        rs = sb("rs", [P, T])
        xTh, xTl = sb("xTh", [P, CT, S], F32R), sb("xTl", [P, CT, S], F32R)
        cTh, cTl = sb("cTh", [P, CKT, S], F32R), sb("cTl", [P, CKT, S], F32R)
        qh, ql = sb("qh", [P, S], F32R), sb("ql", [P, S], F32R)
        kh, kl = sb("kh", [P, S], F32R), sb("kl", [P, S], F32R)
        qs = [sb(f"qs{i}", [R3, HG, S], F32R) for i in range(2)]
        ks = [sb(f"ks{i}", [R3, HG, S], F32R) for i in range(2)]
        v = sb("v", [P, T, HEADS, 2, D], F32R)
        qsum = sb("qsum", [P, CT])
        ksum = sb("ksum", [P, CT])
        csum = sb("csum", [P, CKT])
        meanv = sb("meanv", [P, CT])
        prob = [sb(f"prob{i}", [P, T, S]) for i in range(2)]
        negmax = [sb(f"negmax{i}", [P, T]) for i in range(2)]
        rowsum = [sb(f"rowsum{i}", [P, T, HG]) for i in range(2)]
        rinv = sb("rinv", [P, T, HG])
        rinvx = sb("rinvx", [P, T, C // CT])
        probTh, probTl = (sb(name, [P, 2, T, 2 * P], F32R) for name in ("probTh", "probTl"))
        scaleT = sb("scaleT", [P, S])
        vlow = [sb(f"vlow{i}", [D, S]) for i in range(2)]
        att = [sb(f"att{i}", [P, S]) for i in range(2)]

        proj_bank = [ps(f"proj_bank{i}") for i in range(2)]
        score_bank = [ps(f"score_bank{i}") for i in range(2)]
        turn_bank = [ps(f"turn_bank{i}") for i in range(2)]
        att_bank = [ps(f"att_bank{i}") for i in range(2)]

        wq_in = sem("wq_in")
        wk_in = sem("wk_in")
        wv_in = sem("wv_in")
        bias_in = sem("bias_in")
        w_high = sem("w_high")
        w_low = sem("w_low")
        x_in = sem("x_in")
        ctx_in_s = sem("ctx_in_s")
        stats_done = sem("stats_done")
        aggr_done = sem("aggr_done")
        sqrt_done = sem("sqrt_done")
        newton = sem("newton")
        xn_done = sem("xn_done")
        proj_full = sem("proj_full")
        proj_high = sem("proj_high")
        proj_low = sem("proj_low")
        nan_sum = sem("nan_sum")
        q_written = sem("q_written")
        k_written = sem("k_written")
        q_stacked = sem("q_stacked")
        k_stacked = sem("k_stacked")
        score_full = sem("score_full")
        score_read = sem("score_read")
        exp_done = sem("exp_done")
        turn_full = sem("turn_full")
        turn_high = sem("turn_high")
        turn_low = sem("turn_low")
        weighed = sem("weighed")
        vlow_done = sem("vlow_done")
        joined = sem("joined")
        rinv_done = sem("rinv_done")
        rinvx_done = sem("rinvx_done")
        att_done = sem("att_done")
        att_out = [sem(f"att_out{i}") for i in range(2)]
        mean_out = sem("mean_out")

        ident, nan_acc = keep["ident"], keep["nan_acc"]
        xr = x.rearrange("b (t p) c -> b p t c", p=P)
        cr = ctx_in.rearrange("b (t p) c -> b p t c", p=P)
        f32 = lambda t: t.bitcast(F32)
        turned = lambda t, n: t[:, n // 2 % 2, :, n % 2 * P:(n % 2 + 1) * P]
        by_key = lambda bank: bank[:].rearrange("p (k q) -> p k q", q=P)
        at_batch = lambda t, b: t[b] if isinstance(b, int) else t[bass.ds(b, 1)].rearrange("o p t c -> (o p) t c")
        stage = (prob[0][:], prob[1][:, 0:CKT, :], prob[0][:, 0:CKT, :])

        parts_dram = {kind: nc.dram_tensor(f"parts_{kind}", [2, P, S], F32).ap() for kind in "qk"}

        def parts_written(b, f):
            _, kind, n, ahead = f
            return (q_written if kind == "q" else k_written), b * CT * 32, 32 * (n + CT if ahead else n) + 32

        def bank_of(b, f):
            assert len(PLAN) % 2 == 0
            return proj_bank[(sum(before(b, f)) if isinstance(b, int) else before(b, f)[1]) % 2]

        block = ctx.enter_context(nc.Block())

        @block.sync
        def _(sp):
            sp.dma_start(xn[:], xr[0]).then_inc(x_in, 16)
            sp.dma_start(cx[:], cr[0]).then_inc(ctx_in_s, 16)
            sp.dma_start(stage[0], Wq.rearrange("(t p) n -> p t n", p=P)).then_inc(wq_in, 16)
            sp.dma_start(stage[1], Wk.rearrange("(t p) n -> p t n", p=P)).then_inc(wk_in, 16)
            sp.dma_start(bqT[:], bq.rearrange("(t p) -> p t", p=P), allow_slow_non_contiguous=True).then_inc(bias_in, 16)
            sp.dma_start(bkT[:], bk.rearrange("(t p) -> p t", p=P), allow_slow_non_contiguous=True).then_inc(bias_in, 16)

            sp.wait_ge(w_low, 2)
            sp.dma_start(stage[2], Wv.rearrange("(t p) n -> p t n", p=P)).then_inc(wv_in, 16)

            def tasks(b, fs):
                for f in fs:
                    _, kind, n, ahead = f
                    base, num = before(b, f)
                    if kind in "qk":
                        high, low, written = (qh, ql, q_written) if kind == "q" else (kh, kl, k_written)
                        wait_apart(sp, keep, proj_high, base, num + 1)
                        sp.dma_start(parts_dram[kind][0], f32(high[:])).then_inc(written, 16)
                        wait_apart(sp, keep, proj_low, *upto(b, f, SPLIT))
                        sp.dma_start(parts_dram[kind][1], f32(low[:])).then_inc(written, 16)
                    nxt = b + 2 if ahead else b + 1
                    more = not isinstance(b, int) or b + 2 < B
                    if kind == "x" and n == CT - 1 and more:
                        wait_apart(sp, keep, proj_full, base, num + 1)
                        sp.dma_start(xn[:], at_batch(xr, nxt)).then_inc(x_in, 16)
                    if kind == "c" and n == CKT - 1 and more:
                        wait_apart(sp, keep, proj_full, base, num + 1)
                        sp.dma_start(cx[:], at_batch(cr, nxt)).then_inc(ctx_in_s, 16)

            def body(b):
                tasks(b, fills(b) if isinstance(b, int) else PLAN)

            tasks(-1, HEAD)
            body(0)
            with sp.Fori(1, B - 2) as b:
                body(b)
            body(B - 2)
            body(B - 1)

        @block.gpsimd
        def _(pool):
            def stack(b, f):
                _, kind, n, ahead = f
                g = n + CT if ahead else n
                wait_apart(pool, keep, score_full, b * QB, (g - 1) * HG * T)
                wait_apart(pool, keep, *parts_written(b, f))
                stacked, done = (qs, q_stacked) if kind == "q" else (ks, k_stacked)
                for i, part in enumerate((0, 0, 1) if kind == "q" else (0, 1, 0)):
                    pool.dma_start(stacked[n % 2][i * D:(i + 1) * D, :, :], parts_dram[kind][part].rearrange("(j p) s -> p j s", p=D)).then_inc(done, 16)

            def body(b):
                for quarter in quarters(b):
                    for f in plan_at(b, quarter - 1):
                        if f[1] in "qk":
                            stack(b, f)
                    n = tile_at(b, quarter, JOIN)
                    if n is not None and n % (HG * T) == (HG - 1) * T:
                        g = n // (HG * T)
                        wait(pool, proj_high, *upto(b, planned("sum", g % CT)))
                        wait(pool, joined, b * HEADS, (g + 1) * HG)
                        pool.tensor_tensor(att[g % 2][:], att[g % 2][:], scaleT[:], ALU.mult).then_inc(att_done, 1)
                        wait_apart(pool, keep, att_done, b * CT, g + 1)
                        row = attn_dram[b * CT + g] if isinstance(b, int) else attn_dram[bass.ds(b * CT + g, 1)].rearrange("o p s -> (o p) s")
                        pool.dma_start(row, att[g % 2][:]).then_inc(att_out[g % 2], 16)
                if not (isinstance(b, int) and b >= B - 1):
                    mean(b)

            def mean(b):
                wait_apart(pool, keep, proj_high, *upto(b, PLAN[-1]))
                m = mean_dram[b + 1] if isinstance(b, int) else mean_dram[bass.ds(b + 1, 1)].rearrange("o p g -> (o p) g")
                pool.dma_start(m, meanv[:]).then_inc(mean_out, 16)

            for f in HEAD:
                if f[1] in "qk":
                    stack(-1, f)
            mean(-1)
            run(pool, body)
            for i in range(2):
                pool.wait_ge(att_out[i], 8 * CT * B)
            pool.wait_ge(mean_out, 16 * B)

        @block.tensor
        def _(pe):
            def fill(b, f, parts=(0, 1, 2)):
                _, kind, n, ahead = f
                base, num = before(b, f)
                bank = bank_of(b, f)
                wait(pe, proj_high, base, num - 1)
                wait(pe, proj_low, *low_before(b, f))
                if kind in "xc":
                    src, high = (xn, xn_done) if kind == "x" else (cx, ctx_in_s)
                    per = T if kind == "x" else 16
                    if n == 0:
                        wait(pe, high, b * per, 2 * per if ahead else per)
                    for t in range(T):
                        last = pe.transpose(bank[:, t * P:(t + 1) * P], src[:, t, n * P:(n + 1) * P], ident[:])
                elif kind in "qk":
                    wh, wl, th, tl, tiles = (wqh, wql, xTh, xTl, CT) if kind == "q" else (wkh, wkl, cTh, cTl, CKT)
                    if n == 0 and 0 in parts:
                        wait(pe, proj_low, *upto(b, planned("c", CKT - 1), SPLIT))
                    for i in parts:
                        w, t = ((wl, th), (wh, tl), (wh, th))[i]
                        for c in range(tiles):
                            last = pe.matmul(bank[:], w[:, c, n * P:(n + 1) * P], t[:, c, :],
                                             start=(i == 0 and c == 0), stop=(i == 2 and c == tiles - 1))
                elif kind == "v":
                    cols = slice((n // T) * C // 2, (n // T + 1) * C // 2)
                    t = n % T
                    for i, (c_, w) in enumerate(((cTl, wvh), (cTh, wvl), (cTh, wvh))):
                        for c in range(CKT):
                            last = pe.matmul(bank[:, 0:C // 2], c_[:, c, t * P:(t + 1) * P], w[:, c, cols],
                                             start=(i == 0 and c == 0), stop=(i == 2 and c == CKT - 1))
                elif kind == "mean":
                    for g in range(CT):
                        for i, w in enumerate((wvl, wvh)):
                            for c in range(CKT):
                                last = pe.matmul(bank[:, g:g + 1], f32(w[:, c, g * P:(g + 1) * P]), csum[:, c:c + 1],
                                                 start=(i == 0 and c == 0), stop=(i == 1 and c == CKT - 1))
                else:
                    g = n - CT if f is PLAN[0] else n
                    wait(pe, rinvx_done, b * CT, g + 1)
                    for t in range(T):
                        last = pe.matmul(bank[:, t * P:(t + 1) * P], rinvx[:, t, :], ident[:], start=True, stop=True)
                if 2 in parts:
                    last.then_inc(proj_full, 1)

            def low_before(b, f):
                fs = fills(b) if isinstance(b, int) else PLAN
                if f is fs[0]:
                    last = fills(B - 1)[-1] if isinstance(b, int) and b == B else PLAN[-1]
                else:
                    last = fs[fs.index(f) - 1]
                base, num = before(b, f, SPLIT)
                return base, num - (last[1] in SPLIT)

            def body(b):
                for quarter in quarters(b):
                    n = tile_at(b, quarter, WEIGH)
                    if n is not None:
                        h, pair, half = n // T, n // 2, n % 2
                        if n % T == 0:
                            wait(pe, joined, b * HEADS, h - 1)
                        if n == 0:
                            wait(pe, proj_low, *upto(b - 1, planned("v", T - 1), SPLIT))
                        elif n == QB // 2:
                            wait(pe, proj_low, *upto(b, planned("v", 2 * T - 1), SPLIT))
                        if half == 0:
                            wait(pe, turn_low, b * QB, n + 2)
                        out = att_bank[h % 2][0:2 * D, pair % 2 * 2 * P:(pair % 2 + 1) * 2 * P]
                        for k in range(half * T // 2, (half + 1) * T // 2):
                            for part in (probTl, probTh):
                                last = pe.matmul(out, v[:, k, h % HEADS, :, :].rearrange("p i d -> p (i d)"), part[:, pair % 2, k, :],
                                                 start=(k == 0 and part is probTl), stop=(k == T - 1 and part is probTh))
                        last.then_inc(weighed, 1)
                    n = tile_at(b, quarter, TURN)
                    if n is not None:
                        h, t = n // T, n % T
                        wait(pe, exp_done, b * QB, n + 1)
                        wait(pe, turn_low, b * QB, n - 1)
                        for k in range(T):
                            last = pe.transpose(turn_bank[n % 2][:, k * P:(k + 1) * P], prob[h % 2][:, t, k * P:(k + 1) * P], ident[:])
                        last.then_inc(turn_full, 1)
                    n = tile_at(b, quarter, 0)
                    if n is not None:
                        h, t = n // T, n % T
                        g, j = h // HG, h % HG
                        if n % (HG * T) == 0:
                            wait(pe, q_stacked, b * CT * STACK, (g + 1) * STACK)
                            wait(pe, k_stacked, b * CT * STACK, (g + 1) * STACK)
                        wait(pe, score_read, b * QB, n - 1)
                        pe.matmul(score_bank[n % 2][:], qs[g % 2][:, j, t * P:(t + 1) * P], ks[g % 2][:, j, :],
                                  start=True, stop=True).then_inc(score_full, 1)
                    for f in plan_at(b, quarter):
                        fill(b, f, (2,) if f[1] in "qk" else (0, 1, 2))
                    for late in (1, 2):
                        for f in plan_at(b, quarter + late):
                            if f[1] in "qk":
                                fill(b, f, (2 - late,))

            pe.wait_ge(keep["made"], MADE)
            pe.wait_ge(w_low, 4)
            for f in HEAD:
                fill(-1, f)
            run(pe, body)

        @block.scalar
        def _(act):
            def deviation(b):
                wait(act, aggr_done, b * T, 2 * T)
                act.activation(sd[:], mv[:, :, 1], ACT.Sqrt, bias=keep["eps"][:, 0:1]).then_inc(sqrt_done, 1)

            def read(b, f):
                _, kind, n, ahead = f
                base, num = before(b, f)
                bank = bank_of(b, f)
                more = {}
                if kind == "x":
                    out = xTh[:, n, :]
                elif kind == "c":
                    out, more = cTh[:, n, :], {"accum_out": csum[:, n:n + 1]}
                elif kind == "v":
                    half = n // T
                    out = v[:, n % T, half * HEADS // 2:(half + 1) * HEADS // 2, 0, :]
                    wait(act, proj_full, base, num + 1)
                    act.activation(out, bank[:, 0:C // 2].rearrange("p (h d) -> p h d", d=D), ACT.Identity).then_inc(proj_high, 1)
                    return
                elif kind == "mean":
                    wait(act, mean_out, b * 16, 16)
                    wait(act, proj_full, base, num + 1)
                    act.activation(meanv[:], bank[:, 0:CT], ACT.Copy, scale=1.0 / S).then_inc(proj_high, 1)
                    return
                elif kind == "sum":
                    g = n if f is not PLAN[0] else n - CT
                    wait(act, att_done, b * CT, g)
                    out = scaleT[:]
                else:
                    high, bias, total, stacked = (qh, bqT, qsum, q_stacked) if kind == "q" else (kh, bkT, ksum, k_stacked)
                    if n == 0:
                        act.wait_ge(w_low, 1)
                        wait(act, nan_sum, b, 1)
                    g = n + CT if ahead else n
                    wait(act, stacked, b * CT * STACK, g * STACK)
                    out, more = high[:], {"bias": bias[:, n:n + 1], "accum_out": total[:, n:n + 1]}
                wait(act, proj_full, base, num + 1)
                act.activation(out, bank[:], ACT.Identity, **more).then_inc(proj_high, 1)

            def body(b):
                for quarter in quarters(b):
                    n = tile_at(b, quarter, JOIN)
                    if n is not None and n % T == 0:
                        h = n // T
                        wait(act, weighed, b * QB, (h + 1) * T)
                        act.activation(vlow[h % 2][:], att_bank[h % 2][D:2 * D, :], ACT.Identity).then_inc(vlow_done, 1)
                    n = tile_at(b, quarter, TURN)
                    if n is not None:
                        wait(act, turn_full, b * QB, n + 1)
                        act.activation(turned(probTh, n), by_key(turn_bank[n % 2]), ACT.Identity).then_inc(turn_high, 1)
                    n = tile_at(b, quarter, EXP)
                    if n is not None:
                        h, t = n // T, n % T
                        g, j = h // HG, h % HG
                        wait(act, score_read, b * QB, n + 1)
                        act.activation(prob[h % 2][:, t, :], prob[h % 2][:, t, :], ACT.Exp, bias=negmax[h % 2][:, t:t + 1], scale=-1.0,
                                       accum_out=rowsum[g % 2][:, t, j:j + 1]).then_inc(exp_done, 1)
                    for f in plan_at(b, quarter):
                        read(b, f)
                    if quarter == 31 and not (isinstance(b, int) and b >= B - 1):
                        deviation(b)

            deviation(-1)
            for i, (loaded, w) in enumerate(((wq_in, wqh), (wk_in, wkh), (wv_in, wvh))):
                act.wait_ge(loaded, 16)
                act.activation(w[:], stage[i], ACT.Copy, scale=-SCALE if i == 0 else 1.0).then_inc(w_high, 1)
            act.wait_ge(bias_in, 32)
            for f in HEAD:
                read(-1, f)
            run(act, body)

        @block.vector
        def _(dve):
            def layernorm_stats(b, t):
                if t == 0:
                    wait(dve, x_in, b * 16, 32)
                dve.bn_stats(stats[:, t, :], xn[:, t, :]).then_inc(stats_done, 1)

            def layernorm_sums(b):
                wait_apart(dve, keep, stats_done, b * T, 2 * T)
                for t in range(T):
                    dve.bn_aggr(mv[:, t, :], stats[:, t, :]).then_inc(aggr_done, 1)

            def layernorm_deviation(b):
                wait(dve, sqrt_done, b, 2)
                newton_rsqrt(dve, newton, b * 5 + 5, 0, mv[:, :, 1], sd[:], r0[:], tmp[:], rs[:])

            def layernorm(b, t):
                if t == 0:
                    wait(dve, newton, b * 5, 10)
                dve.tensor_scalar(xn[:, t, :], xn[:, t, :], mv[:, t, 0:1], rs[:, t:t + 1],
                                  ALU.subtract, ALU.mult).then_inc(xn_done, 1)

            def low(b, f):
                _, kind, n, ahead = f
                base, num = before(b, f)
                bank = bank_of(b, f)
                wait(dve, proj_high, base, num + 1)
                if kind == "x":
                    dve.tensor_tensor(xTl[:, n, :], bank[:], f32(xTh[:, n, :]), ALU.subtract).then_inc(proj_low, 1)
                elif kind == "c":
                    dve.tensor_tensor(cTl[:, n, :], bank[:], f32(cTh[:, n, :]), ALU.subtract).then_inc(proj_low, 1)
                elif kind == "v":
                    heads = slice(n // T * HEADS // 2, (n // T + 1) * HEADS // 2)
                    dve.tensor_tensor(v[:, n % T, heads, 1, :], bank[:, 0:C // 2].rearrange("p (h d) -> p h d", d=D),
                                      f32(v[:, n % T, heads, 0, :]), ALU.subtract).then_inc(proj_low, 1)
                else:
                    high, part, bias = (qh, ql, bqT) if kind == "q" else (kh, kl, bkT)
                    dve.scalar_tensor_tensor(out=part[:], in0=bank[:], scalar=bias[:, n:n + 1], in1=f32(high[:]),
                                             op0=ALU.add, op1=ALU.subtract).then_inc(proj_low, 1)

            def body(b):
                for quarter in quarters(b):
                    n = tile_at(b, quarter, TURN + LOW)
                    if n is not None:
                        wait(dve, turn_high, b * QB, n + 1)
                        dve.tensor_tensor(turned(probTl, n), by_key(turn_bank[n % 2]), f32(turned(probTh, n)), ALU.subtract).then_inc(turn_low, 1)
                    n = tile_at(b, quarter, 0)
                    if n is not None:
                        h, t = n // T, n % T
                        if t == 0:
                            wait(dve, turn_full, b * QB, (h - 1) * T)
                        wait(dve, score_full, b * QB, n + 1)
                        dve.tensor_scalar(prob[h % 2][:, t, :], score_bank[n % 2][:], -CLAMP, CLAMP, ALU.max, ALU.min,
                                          accum_out=negmax[h % 2][:, t:t + 1]).then_inc(score_read, 1)
                    n = tile_at(b, quarter, JOIN)
                    if n is not None and n % T == 0:
                        h = n // T
                        g, j = h // HG, h % HG
                        if j == 0:
                            wait(dve, att_out[g % 2], b * 8 * CT, 16 * (g // 2))
                        wait(dve, vlow_done, b * HEADS, h + 1)
                        dve.tensor_tensor(att[g % 2][j * D:(j + 1) * D, :], att_bank[h % 2][0:D, :], vlow[h % 2][:], ALU.add).then_inc(joined, 1)
                    n = tile_at(b, quarter, HG * T + 2)
                    if n is not None and n % (HG * T) == 0:
                        g = n // (HG * T)
                        wait(dve, exp_done, b * QB, (g + 1) * HG * T)
                        wait(dve, rinvx_done, b * CT, g)
                        dve.reciprocal(rinv[:], rowsum[g % 2][:]).then_inc(rinv_done, 1)
                        if g < 0:
                            wait(dve, proj_full, *upto(b - 1, planned("sum", CT - 2)))
                        elif not (isinstance(b, int) and b == 0 and g == 0):
                            wait(dve, proj_full, *upto(b, planned("sum", (g - 1) % CT)))
                        wait(dve, rinv_done, b * CT, g + 1)
                        dve.tensor_copy(rinvx[:].rearrange("p t (j d) -> p (t j) d", d=D),
                                        rinv[:].rearrange("p t j -> p (t j)").unsqueeze(2).to_broadcast([P, T * HG, D])
                                        ).then_inc(rinvx_done, 1)
                    for f in plan_at(b, quarter):
                        if f[1] in SPLIT:
                            low(b, f)
                    if quarter == 40 and not (isinstance(b, int) and b >= B):
                        wait(dve, proj_high, *upto(b, planned("k", CT - 1)))
                        acc = nan_acc[:, b * CT:(b + 1) * CT] if isinstance(b, int) else nan_acc[:, bass.ds(b * CT, CT)]
                        dve.tensor_tensor(acc, qsum[:], ksum[:], ALU.mult).then_inc(nan_sum, 1)
                    if not (isinstance(b, int) and b >= B - 1):
                        if quarter in range(26, 26 + T):
                            layernorm_stats(b, quarter - 26)
                        if quarter == 30:
                            layernorm_sums(b)
                        if quarter == 33:
                            layernorm_deviation(b)
                        if quarter in range(34, 34 + T):
                            layernorm(b, quarter - 34)

            for t in range(T):
                layernorm_stats(-1, t)
            layernorm_sums(-1)
            layernorm_deviation(-1)
            for t in range(T):
                layernorm(-1, t)
            dve.wait_ge(bias_in, 32)
            dve.tensor_scalar(bqT[:], bqT[:], -SCALE, None, ALU.mult).then_inc(w_low, 1)
            for i, (h, l) in enumerate(((wqh, wql), (wkh, wkl), (wvh, wvl))):
                dve.wait_ge(w_high, i + 1)
                dve.scalar_tensor_tensor(out=l[:], in0=stage[i], scalar=-SCALE if i == 0 else 1.0, in1=f32(h[:]),
                                         op0=ALU.mult, op1=ALU.subtract).then_inc(w_low, 1)
            for f in HEAD:
                if f[1] in SPLIT:
                    low(-1, f)
            run(dve, body)


def projection(nc, keep, x, bv, Wo, bo, g_xattn, g_ffn, router_w, attn_dram, mean_dram, rows_dram, out):
    B, S, C = x.shape
    T, CT = S // P, C // P
    E = router_w.shape[0]
    N = B * S
    W = rows_dram.shape[1]
    with ExitStack() as ctx:
        sb, ps, sem = make_pools(nc, ctx)
        wo = sb("wo", [P, CT, C])
        bvT = sb("bvT", [P, CT])
        bo_b = sb("bo_b", [P, C])
        gate = sb("gate", [P, 1])
        rw = sb("rw", [E, C])
        rwT = sb("rwT", [P, CT, E])
        nan_row = sb("nan_row", [P, 1])
        nan_tot = sb("nan_tot", [P, 1])
        nan_f = sb("nan_f", [P, 1])
        nan_mask = sb("nan_mask", [P, 1], I32)
        att = [sb(f"pat{i}", [P, CT, S]) for i in range(2)]
        meanv = [sb(f"pmean{i}", [P, CT]) for i in range(2)]
        xs = [sb(f"xs{i}", [P, T, C]) for i in range(2)]
        xn = [sb(f"pxn{i}", [P, T, C]) for i in range(2)]
        stats = sb("pstats", [P, T, 6])
        mv = sb("pmv", [P, T, 2])
        sd = sb("psd", [P, T])
        r0 = sb("pr0", [P, T])
        tmp = sb("ptmp", [P, T])
        rs = sb("prs", [P, T])
        xT = sb("pxT", [P, CT, S])
        padrow = sb("padrow", [1, W])

        y_bank = [ps(f"y_bank{i}") for i in range(2)]
        t_bank = [ps(f"t_bank{i}") for i in range(2)]
        l_bank = [ps(f"l_bank{i}") for i in range(2)]
        c_bank = ps("c_bank")
        d_bank = ps("d_bank")

        w_in = sem("b_w_in")
        w_in2 = sem("b_w_in2")
        in_s = [sem(f"b_in{i}") for i in range(2)]
        setup = sem("b_setup")
        pad_made = sem("b_pad_made")
        nan_s = sem("b_nan")
        const_pe = sem("b_const_pe")
        const_act = sem("b_const_act")
        blended = sem("b_blended")
        biased = sem("b_biased")
        y_full = sem("b_y_full")
        x1_done = sem("b_x1_done")
        stats_done = sem("b_stats")
        aggr_done = sem("b_aggr")
        sqrt_done = sem("b_sqrt")
        newton = sem("b_newton")
        kept_stats = sem("b_kept")
        xn_done = sem("b_xn")
        t_full = sem("b_t_full")
        t_read = sem("b_t_read")
        l_full = sem("b_l_full")
        l_read = sem("b_l_read")
        stored = [sem(f"b_stored{i}") for i in range(2)]
        pad_out = sem("b_pad_out")

        ident, ones, gate2 = keep["ident"], keep["ones"], keep["gate2"]
        xr = x.rearrange("b (t p) c -> b p t c", p=P)
        ar = attn_dram.rearrange("(b g) p s -> b p g s", g=CT)
        orow = out.rearrange("b (t p) c -> b p t c", p=P)
        rrow = rows_dram[0:N, :].rearrange("(b t p) w -> b p t w", p=P, t=T)

        def at(t, b):
            if isinstance(b, int):
                return t[b]
            names = "p t c" if len(t.shape) == 4 else "p c"
            return t[bass.ds(b, 1)].rearrange(f"o {names} -> (o {names.split()[0]}) {' '.join(names.split()[1:])}")

        block = ctx.enter_context(nc.Block())

        @block.sync
        def _(sp):
            sp.dma_start(wo[:], Wo.rearrange("(t p) n -> p t n", p=P)).then_inc(w_in, 16)
            sp.dma_start(bvT[:], bv.rearrange("(t p) -> p t", p=P), allow_slow_non_contiguous=True).then_inc(w_in, 16)
            sp.dma_start(bo_b[:], bo.rearrange("(o n) -> o n", o=1).to_broadcast([P, C])).then_inc(w_in, 16)
            sp.dma_start(rw[:], router_w).then_inc(w_in, 16)
            sp.dma_start(gate[:], g_xattn.rearrange("(o n) -> o n", o=1).to_broadcast([P, 1])).then_inc(w_in2, 16)
            sp.dma_start(gate2[:], g_ffn.rearrange("(o n) -> o n", o=1).to_broadcast([P, 1])).then_inc(w_in2, 16)

            def pair(i):
                for u in range(2):
                    wait_apart(sp, keep, y_full, i * 2 * T, (u - 1) * T)
                    wait_apart(sp, keep, stored[u], i * 32, 0)
                    wait_apart(sp, keep, xn_done, i * 2 * T, (u - 1) * T)
                    b = 2 * i + u
                    sp.dma_start(att[u][:], at(ar, b)).then_inc(in_s[u], 16)
                    sp.dma_start(meanv[u][:], at(mean_dram, b)).then_inc(in_s[u], 16)
                    sp.dma_start(xs[u][:], at(xr, b)).then_inc(in_s[u], 16)

            pair(0)
            with sp.Fori(1, B // 2) as i:
                pair(i)

        @block.gpsimd
        def _(pool):
            pool.memset(padrow[:], 0.0).then_inc(pad_made, 1)
            pool.wait_ge(pad_made, 1)
            pool.dma_start(rows_dram[N:N + 1, :], padrow[:]).then_inc(pad_out, 16)
            pool.wait_ge(nan_s, 5)

            def pair(i):
                for u in range(2):
                    b = 2 * i + u
                    wait_apart(pool, keep, in_s[u], i * 48, 48)
                    pool.tensor_tensor(xs[u][:], xs[u][:], bo_b[:].unsqueeze(1).to_broadcast([P, T, C]), ALU.add).then_inc(biased, 1)

                    wait_apart(pool, keep, x1_done, i * 2 * T, (u + 1) * T)
                    pool.dma_start(at(orow, b), xs[u][:]).then_inc(stored[u], 16)
                    pool.dma_start(at(rrow, b)[:, :, 0:C], xs[u][:]).then_inc(stored[u], 16)

            pair(0)
            with pool.Fori(1, B // 2) as i:
                pair(i)
            for u in range(2):
                pool.wait_ge(stored[u], 32 * (B // 2))
            pool.wait_ge(pad_out, 16)

        @block.tensor
        def _(pe):
            pe.wait_ge(w_in, 64)
            for g in range(CT):
                last = pe.matmul(c_bank[:], bvT[:, g:g + 1].to_broadcast([P, P]), wo[:, g, :], start=(g == 0), stop=(g == CT - 1))
            last.then_inc(const_pe, 1)
            for c in range(CT):
                last = pe.transpose(d_bank[:, c * E:(c + 1) * E], rw[:, c * P:(c + 1) * P], ident[0:E, 0:E])
            last.then_inc(const_pe, 1)
            pe.wait_ge(const_act, 2)
            pe.wait_ge(nan_s, 1)
            pe.matmul(d_bank[:, 0:1], ones[:], nan_row[:], start=True, stop=True).then_inc(const_pe, 1)

            def products(i, u):
                wait(pe, blended, i * 2, u + 1)
                for t in range(T):
                    wait(pe, x1_done, i * 2 * T, u * T + t - 1)
                    for g in range(CT):
                        last = pe.matmul(y_bank[t % 2][:], att[u][:, g, t * P:(t + 1) * P], wo[:, g, :], start=(g == 0), stop=(g == CT - 1))
                    last.then_inc(y_full, 1)

            def route(i, u):
                wait(pe, xn_done, i * 2 * T, (u + 1) * T)
                for c in range(CT):
                    wait(pe, t_read, i * 2 * CT, u * CT + c - 1)
                    for t in range(T):
                        last = pe.transpose(t_bank[c % 2][:, t * P:(t + 1) * P], xn[u][:, t, c * P:(c + 1) * P], ident[:])
                    last.then_inc(t_full, 1)
                wait(pe, t_read, i * 2 * CT, (u + 1) * CT)
                for t in range(T):
                    for c in range(CT):
                        last = pe.matmul(l_bank[u][:, t * E:(t + 1) * E], xT[:, c, t * P:(t + 1) * P], rwT[:, c, :],
                                         start=(c == 0), stop=(c == CT - 1))
                last.then_inc(l_full, 1)

            products(0, 0)
            products(0, 1)
            route(0, 0)
            with pe.Fori(1, B // 2) as i:
                products(i, 0)
                route(i - 1, 1)
                products(i, 1)
                route(i, 0)
            route(B // 2 - 1, 1)

        @block.scalar
        def _(act):
            act.wait_ge(w_in2, 32)
            act.activation(gate[:], gate[:], ACT.Tanh).then_inc(const_act, 1)
            act.activation(gate2[:], gate2[:], ACT.Tanh)
            act.wait_ge(const_pe, 2)
            act.activation(rwT[:], d_bank[:, 0:CT * E], ACT.Identity).then_inc(const_act, 1)

            def deviation(i, u):
                wait(act, aggr_done, i * 2 * T, (u + 1) * T)
                wait(act, newton, i * 10, 5 * u)
                act.activation(sd[:], mv[:, :, 1], ACT.Sqrt, bias=keep["eps"][:, 0:1]).then_inc(sqrt_done, 1)

            def read_turned(i, u):
                wait(act, l_full, i * 2, u)
                for c in range(CT):
                    wait(act, t_full, i * 2 * CT, u * CT + c + 1)
                    act.activation(xT[:, c, :], t_bank[c % 2][:], ACT.Identity).then_inc(t_read, 1)
                wait(act, l_full, i * 2, u + 1)
                b = 2 * i + u
                dst = keep["logits"][:, b * T:(b + 1) * T, :] if isinstance(i, int) else keep["logits"][:, bass.ds(b * T, T), :]
                act.activation(dst, l_bank[u][:, 0:T * E].rearrange("p (t e) -> p t e", t=T), ACT.Identity).then_inc(l_read, 1)

            deviation(0, 0)
            deviation(0, 1)
            read_turned(0, 0)
            with act.Fori(1, B // 2) as i:
                deviation(i, 0)
                read_turned(i - 1, 1)
                deviation(i, 1)
                read_turned(i, 0)
            read_turned(B // 2 - 1, 1)

        @block.vector
        def _(dve):
            dve.tensor_reduce(nan_row[:], keep["nan_acc"][:], AX_X, ALU.add).then_inc(nan_s, 1)
            dve.wait_ge(const_pe, 3)
            dve.tensor_copy(nan_tot[:], d_bank[:, 0:1]).then_inc(nan_s, 1)
            dve.wait_ge(nan_s, 2)
            dve.tensor_tensor(nan_f[:], nan_tot[:], nan_tot[:], ALU.not_equal).then_inc(nan_s, 1)
            dve.wait_ge(nan_s, 3)
            dve.tensor_copy(nan_mask[:], nan_f[:]).then_inc(nan_s, 1)
            dve.wait_ge(const_act, 1)
            dve.tensor_tensor(bo_b[:], c_bank[:], bo_b[:], ALU.add).then_inc(setup, 1)
            dve.wait_ge(setup, 1)
            dve.tensor_scalar(bo_b[:], bo_b[:], gate[:, 0:1], None, ALU.mult).then_inc(nan_s, 1)
            dve.wait_ge(nan_s, 5)

            def blend(i, u):
                wait_apart(dve, keep, in_s[u], i * 48, 48)
                dve.copy_predicated(att[u][:], nan_mask[:, 0:1].unsqueeze(2).to_broadcast([P, CT, S]),
                                    meanv[u][:].unsqueeze(2).to_broadcast([P, CT, S])).then_inc(blended, 1)

            def residual(i, u):
                wait(dve, biased, i * 2, u + 1)
                for t in range(T):
                    wait(dve, y_full, i * 2 * T, u * T + t + 1)
                    dve.scalar_tensor_tensor(out=xs[u][:, t, :], in0=y_bank[t % 2][:], scalar=gate[:, 0:1], in1=xs[u][:, t, :],
                                             op0=ALU.mult, op1=ALU.add).then_inc(x1_done, 1)
                wait(dve, xn_done, i * 2 * T, u * T)
                wait(dve, kept_stats, i * 4, 2 * u)
                for t in range(T):
                    wait(dve, x1_done, i * 2 * T, u * T + t + 1)
                    dve.bn_stats(stats[:, t, :], xs[u][:, t, :]).then_inc(stats_done, 1)
                wait_apart(dve, keep, stats_done, i * 2 * T, (u + 1) * T)
                for t in range(T):
                    dve.bn_aggr(mv[:, t, :], stats[:, t, :]).then_inc(aggr_done, 1)

            def normalise(i, u):
                b = 2 * i + u
                wait(dve, sqrt_done, i * 2, u + 1)
                newton_rsqrt(dve, newton, i * 10, 5 * u, mv[:, :, 1], sd[:], r0[:], tmp[:], rs[:])
                wait(dve, newton, i * 10, 5 * u + 5)
                wait(dve, t_full, i * 2 * CT, (u - 1) * CT)
                for t in range(T):
                    dve.tensor_scalar(xn[u][:, t, :], xs[u][:, t, :], mv[:, t, 0:1], rs[:, t:t + 1],
                                      ALU.subtract, ALU.mult).then_inc(xn_done, 1)
                rows = slice(b * T, (b + 1) * T) if isinstance(i, int) else bass.ds(b * T, T)
                dve.tensor_copy(keep["token"][:, rows, 0], mv[:, :, 0]).then_inc(kept_stats, 1)
                dve.tensor_copy(keep["token"][:, rows, 1], rs[:]).then_inc(kept_stats, 1)

            def pair(i):
                for u in range(2):
                    blend(i, u)
                    residual(i, u)
                    normalise(i, u)

            pair(0)
            with dve.Fori(1, B // 2) as i:
                pair(i)


def routing(nc, keep, N, E, CAP, C, rows_dram, table):
    NT = N // P
    NONE = 2 * E * CAP
    with ExitStack() as ctx:
        sb, ps, sem = make_pools(nc, ctx)
        mx = sb("mx", [P, NT])
        e_ = sb("e_", [P, NT, E])
        sm = sb("sm", [P, NT])
        ri = sb("ri", [P, NT])
        pr = sb("pr", [P, NT, E])
        rank = sb("rank", [P, E])
        first = sb("first", [P, E])
        oh = sb("oh", [P, NT, E])
        tot = sb("tot", [P, E, NT])
        run = sb("run", [P, E, NT])
        one = sb("one", [P, NT])
        pos = sb("pos", [P, NT, E])
        keepm = sb("keepm", [P, NT, E])
        base = sb("base", [P, E])
        slot_f = sb("slot_f", [P, NT])
        slot = sb("slot", [P, NT], I32)
        tok = sb("tok", [P, NT], I32)
        tri = sb("tri", [P, P])
        pad = sb("pad", [P, E * CAP // P], I32)
        a_bank = ps("a_bank")
        b_bank = ps("b_bank")
        ch = sem("c_chain")
        ex = sem("c_exp")
        cn = sem("c_counts")
        token_ready = sem("c_token")
        chosen_ready = sem("c_chosen")
        slot_ready = sem("c_slot")
        setup = sem("c_setup")
        pad_s = sem("c_pad")
        sc = sem("c_scatter")
        st = sem("c_stats_out")
        block = ctx.enter_context(nc.Block())
        logits, token = keep["logits"], keep["token"]
        bc = lambda t: t.unsqueeze(2).to_broadcast([P, NT, E])
        ec = lambda t: t.unsqueeze(1).to_broadcast([P, NT, E])

        @block.gpsimd
        def _(pool):
            pool.iota(pad[:], pattern=[[0, E * CAP // P]], base=N, channel_multiplier=0).then_inc(setup, 1)
            pool.iota(tok[:], pattern=[[P, NT]], base=0, channel_multiplier=1).then_inc(setup, 1)
            pool.iota(rank[:], pattern=[[-1, E]], base=E, channel_multiplier=0, allow_small_or_imprecise_dtypes=True).then_inc(setup, 1)
            pool.iota(base[:], pattern=[[CAP, E]], base=-1 - NONE, channel_multiplier=0, allow_small_or_imprecise_dtypes=True).then_inc(setup, 1)
            pool.memset(tri[:], 1.0).then_inc(setup, 1)
            pool.memset(first[:], 0.0).then_inc(setup, 1)
            pool.memset(one[:], 1.0).then_inc(setup, 1)
            pool.wait_ge(setup, 7)
            pool.affine_select(out=tri[:], in_=tri[:], compare_op=ALU.is_ge, fill=0.0, base=0, pattern=[[1, P]],
                               channel_multiplier=-1).then_inc(setup, 1)
            pool.memset(first[:, 0:1], 0.5).then_inc(setup, 1)
            pool.dma_start(table.rearrange("(p k) o -> p (k o)", p=P), pad[:]).then_inc(pad_s, 16)
            pool.wait_ge(pad_s, 16)
            pool.wait_ge(slot_ready, 1)
            for t in range(NT):
                pool.indirect_dma_start(table, bass.IndirectOffsetOnAxis(ap=slot[:, t:t + 1], axis=0), tok[:, t:t + 1], None,
                                        bounds_check=E * CAP - 1, oob_is_err=False).then_inc(sc, 16)
            pool.wait_ge(sc, 16 * NT)

        @block.sync
        def _(sp):
            sp.wait_ge(token_ready, 1)
            sp.dma_start(rows_dram[0:N, C:C + 4].rearrange("(t p) w -> p t w", p=P), token[:],
                         allow_slow_non_contiguous=True).then_inc(st, 16)
            sp.wait_ge(st, 16)

        @block.scalar
        def _(act):
            act.wait_ge(ch, 2)
            act.activation(e_[:], e_[:], ACT.Exp).then_inc(ex, 1)

        @block.tensor
        def _(pe):
            pe.wait_ge(chosen_ready, 1)
            pe.wait_ge(setup, 9)
            flat = oh[:].rearrange("p t e -> p (t e)")
            pe.matmul(a_bank[:, 0:NT * E], tri[:], flat, start=True, stop=True).then_inc(cn, 1)
            pe.matmul(b_bank[:, 0:NT * E], keep["ones"][:], flat, start=True, stop=True).then_inc(cn, 1)

        @block.vector
        def _(dve):
            n = [0]

            def step(ins):
                n[0] += 1
                ins.then_inc(ch, 1)
                dve.wait_ge(ch, n[0])

            step(dve.tensor_reduce(mx[:], logits[:], AX_X, ALU.max))
            step(dve.tensor_tensor(e_[:], logits[:], bc(mx[:]), ALU.subtract))
            dve.wait_ge(ex, 1)
            step(dve.tensor_reduce(sm[:], e_[:], AX_X, ALU.add))
            step(dve.reciprocal(ri[:], sm[:]))
            step(dve.tensor_tensor(pr[:], e_[:], bc(ri[:]), ALU.mult))
            step(dve.tensor_reduce(mx[:], pr[:], AX_X, ALU.max))
            dve.tensor_copy(token[:, :, 2], mx[:]).then_inc(token_ready, 1)
            step(dve.tensor_tensor(pr[:], pr[:], bc(mx[:]), ALU.is_equal))
            dve.wait_ge(setup, 9)
            step(dve.tensor_tensor(pr[:], pr[:], ec(rank[:]), ALU.mult))
            step(dve.tensor_tensor(pr[:], pr[:], ec(first[:]), ALU.max))
            step(dve.tensor_reduce(mx[:], pr[:], AX_X, ALU.max))
            dve.tensor_tensor(oh[:], pr[:], bc(mx[:]), ALU.is_equal).then_inc(chosen_ready, 1)
            dve.wait_ge(cn, 2)
            step(dve.tensor_copy(tot[:].rearrange("p e t -> p t e"), b_bank[:, 0:NT * E].rearrange("p (t e) -> p t e", t=NT)))
            for x in range(E):
                step(dve.tensor_tensor_scan(run[:, x, :], one[:], tot[:, x, :], 0.0, ALU.mult, ALU.add))
            step(dve.tensor_tensor(run[:], run[:], tot[:], ALU.subtract))
            step(dve.tensor_tensor(pos[:], a_bank[:, 0:NT * E].rearrange("p (t e) -> p t e", t=NT), run[:].rearrange("p e t -> p t e"), ALU.add))
            step(dve.tensor_scalar(keepm[:], pos[:], float(CAP), None, ALU.is_le))
            step(dve.tensor_tensor(pos[:], pos[:], ec(base[:]), ALU.add))
            step(dve.tensor_tensor(keepm[:], keepm[:], oh[:], ALU.mult))
            step(dve.tensor_tensor(pos[:], pos[:], keepm[:], ALU.mult))
            step(dve.tensor_reduce(slot_f[:], pos[:], AX_X, ALU.add))
            dve.tensor_scalar(slot[:], slot_f[:], float(NONE), None, ALU.add).then_inc(slot_ready, 1)


def experts(nc, keep, w1, b1, w2, b2, rows_dram, table, out, CAP):
    E, C, FF = w1.shape
    W = rows_dram.shape[1]
    N = rows_dram.shape[0] - 1
    CT = C // P
    ST = CAP // P
    CH = 4
    FT = FF // P // CH
    FW = FT * P
    HALF = CAP // 2
    TH = HALF // P
    UP = 2 * FT
    TF = 2 * CT
    with ExitStack() as ctx:
        sb, ps, sem = make_pools(nc, ctx)
        w1s = sb("w1s", [P, CT, FW])
        w2s = sb("w2s", [P, FT, C])
        w1h = [sb(f"w1h{i}", [P, CT, FW], F32R) for i in range(2)]
        w1l = [sb(f"w1l{i}", [P, CT, FW], F32R) for i in range(2)]
        w2h = [sb(f"w2h{i}", [P, FT, C], F32R) for i in range(2)]
        w2l = [sb(f"w2l{i}", [P, FT, C], F32R) for i in range(2)]
        b1all = sb("b1all", [P, E * CH * FT])
        b1s = sb("b1s", [P, CH * FT])
        b2b = sb("b2b", [P, C])
        gel = [sb(f"gel{i}", [P, CAP]) for i in range(2)]
        hh = [sb(f"hh{i}", [P, FT, CAP], F32R) for i in range(2)]
        hl = [sb(f"hl{i}", [P, FT, CAP], F32R) for i in range(2)]
        xTh = sb("gTh", [P, CT, CAP], F32R)
        xTl = sb("gTl", [P, CT, CAP], F32R)
        xg = sb("xg", [P, ST, W])
        xn = sb("exn", [P, ST, C])
        res = sb("res", [P, ST, C])
        idx_g = sb("idx_g", [P, ST], I32)
        idx_s = sb("idx_s", [P, ST], I32)
        gp = sb("gp", [P, ST])

        up_bank = [ps(f"up_bank{i}") for i in range(2)]
        y_bank = [ps(f"ey_bank{i}") for i in range(ST)]

        b1_in = sem("d_b1_in")
        b1_set = sem("d_b1_set")
        w1_in = sem("d_w1_in")
        w2_in = sem("d_w2_in")
        b2_in = sem("d_b2_in")
        idx_in = sem("d_idx_in")
        w1h_done = sem("d_w1h")
        w1l_done = sem("d_w1l")
        w2h_done = sem("d_w2h")
        w2l_done = sem("d_w2l")
        rows_in = sem("d_rows_in")
        gp_done = sem("d_gp")
        xn_done = sem("d_xn")
        t_full = sem("d_t_full")
        th_done = sem("d_th")
        tl_done = sem("d_tl")
        up_full = sem("d_up_full")
        gelu_done = sem("d_gelu")
        hh_done = sem("d_hh")
        hl_done = sem("d_hl")
        down_done = sem("d_down")
        y_full = sem("d_y_full")
        res_done = sem("d_res")
        idx_kept = sem("d_idx_kept")
        out_done = sem("d_out_done")
        scattered = sem("d_scattered")

        ident, gate2 = keep["ident"], keep["gate2"]
        w1v = w1.rearrange("e (k p) f -> e p k f", p=P)
        w2v = w2.rearrange("e (c f p) d -> (e c) p f d", p=P, c=CH)
        tv = table.rearrange("(e p k) o -> e p (k o)", e=E, p=P)
        f32 = lambda t: t.bitcast(F32)

        def at(t, i):
            if isinstance(i, int):
                return t[i]
            names = ["p", "k", "f"][:len(t.shape) - 1]
            return t[bass.ds(i, 1)].rearrange(f"o {' '.join(names)} -> (o p) {' '.join(names[1:])}")

        block = ctx.enter_context(nc.Block())

        @block.sync
        def _(sp):
            sp.dma_start(b1all[:], b1.rearrange("e (t p) -> p (e t)", p=P), allow_slow_non_contiguous=True).then_inc(b1_in, 16)

            def load_rows_index(e):
                wait_apart(sp, keep, idx_kept, e, 0)
                sp.dma_start(idx_g[:], at(tv, e)).then_inc(idx_in, 16)

            def expert(e, more):
                wait_apart(sp, keep, gp_done, e, 0)
                wait_apart(sp, keep, res_done, e * ST, 0)
                b2row = b2[e:e + 1] if isinstance(e, int) else b2[bass.ds(e, 1)]
                sp.dma_start(b2b[:], b2row.to_broadcast([P, C])).then_inc(b2_in, 16)
                for c in range(CH):
                    wait_apart(sp, keep, w1l_done, e * CH * CT, c * CT)
                    sp.dma_start(w1s[:], at(w1v, e)[:, :, c * FW:(c + 1) * FW]).then_inc(w1_in, 16)
                    wait_apart(sp, keep, w2l_done, e * CH * FT, c * FT)
                    sp.dma_start(w2s[:], at(w2v, e * CH + c)).then_inc(w2_in, 16)
                    if c == 1 and more:
                        load_rows_index(e + 1)

            load_rows_index(0)
            expert(0, True)
            with sp.Fori(1, E - 1) as e:
                expert(e, True)
            expert(E - 1, False)

        @block.gpsimd
        def _(pool):
            def gather(e):
                wait_apart(pool, keep, idx_in, e * 16, 16)
                wait_apart(pool, keep, xn_done, e * ST, 0)
                wait_apart(pool, keep, res_done, e * ST, 0)
                for k in range(ST):
                    pool.indirect_dma_start(xg[:, k, :], None, rows_dram, bass.IndirectOffsetOnAxis(ap=idx_g[:, k:k + 1], axis=0),
                                            bounds_check=N, oob_is_err=False).then_inc(rows_in, 16)

            def scatter(e):
                for k in range(ST):
                    wait_apart(pool, keep, out_done, e * ST, k + 1)
                    pool.indirect_dma_start(out, bass.IndirectOffsetOnAxis(ap=idx_s[:, k:k + 1], axis=0), res[:, k, :], None,
                                            bounds_check=N - 1, oob_is_err=False).then_inc(scattered, 16)

            gather(0)
            gather(1)
            scatter(0)
            with pool.Fori(1, E - 1) as e:
                gather(e + 1)
                scatter(e)
            scatter(E - 1)
            pool.wait_ge(scattered, 16 * ST * E)

        @block.tensor
        def _(pe):
            def turn(e):
                wait(pe, xn_done, e * ST, ST)
                for n in range(TF):
                    c, half = n // 2, n % 2
                    if n < 2:
                        wait(pe, gelu_done, e * CH * UP, n - 1)
                    else:
                        wait(pe, tl_done, e * TF, n - 1)
                    for k in range(TH):
                        t = half * TH + k
                        last = pe.transpose(up_bank[n % 2][:, k * P:(k + 1) * P], xn[:, t, c * P:(c + 1) * P], ident[:])
                    last.then_inc(t_full, 1)

            def up(e, c):
                s = c % 2
                wait(pe, w1l_done, e * CH * CT, (c + 1) * CT)
                if c == 0:
                    wait(pe, tl_done, e * TF, TF)
                for n in range(UP):
                    f, half = n // 2, n % 2
                    if c > 0 or n > 1:
                        wait(pe, gelu_done, e * CH * UP, c * UP + n - 1)
                    parts = ((w1l[s], xTh), (w1h[s], xTl), (w1h[s], xTh))
                    for i, (w, t) in enumerate(parts):
                        for k in range(CT):
                            last = pe.matmul(up_bank[n % 2][:, 0:HALF], w[:, k, f * P:(f + 1) * P], t[:, k, half * HALF:(half + 1) * HALF],
                                             start=(i == 0 and k == 0), stop=(i == 2 and k == CT - 1))
                    last.then_inc(up_full, 1)

            def down(e, c):
                s = c % 2
                wait(pe, hl_done, e * CH * FT, (c + 1) * FT)
                wait(pe, w2l_done, e * CH * FT, (c + 1) * FT)
                for k in range(ST):
                    if c == 0:
                        wait(pe, out_done, e * ST, k + 1 - ST)
                    parts = ((hl[s], w2h[s]), (hh[s], w2l[s]), (hh[s], w2h[s]))
                    for i, (h, w) in enumerate(parts):
                        for f in range(FT):
                            last = pe.matmul(y_bank[k][:], h[:, f, k * P:(k + 1) * P], w[:, f, :],
                                             start=(c == 0 and i == 0 and f == 0), stop=(c == CH - 1 and i == 2 and f == FT - 1))
                    if c == CH - 1:
                        last.then_inc(y_full, 1)
                    elif k == ST - 1:
                        last.then_inc(down_done, 1)

            def expert(e, more):
                up(e, 0)
                up(e, 1)
                down(e, 0)
                up(e, 2)
                down(e, 1)
                up(e, 3)
                down(e, 2)
                if more:
                    turn(e + 1)
                down(e, 3)

            turn(0)
            expert(0, True)
            with pe.Fori(1, E - 1) as e:
                expert(e, True)
            expert(E - 1, False)

        def downs(e, c):
            if c == CH - 1:
                return y_full, e * ST, ST
            return down_done, e * (CH - 1), c + 1

        @block.scalar
        def _(act):
            def w1_high(e, c, k):
                s = c % 2
                if k == 0:
                    wait(act, w1_in, e * CH * 16, (c + 1) * 16)
                    wait(act, up_full, e * CH * UP, (c - 1) * UP)
                act.activation(w1h[s][:, k, :], w1s[:, k, :], ACT.Copy).then_inc(w1h_done, 1)

            def w2_high(e, c, k):
                s = c % 2
                if k == 0:
                    wait(act, w2_in, e * CH * 16, (c + 1) * 16)
                    if c >= 2:
                        wait(act, *downs(e, c - 2))
                    elif not (isinstance(e, int) and e == 0):
                        wait(act, *downs(e - 1, c + 2))
                act.activation(w2h[s][:, k, :], w2s[:, k, :], ACT.Copy).then_inc(w2h_done, 1)

            def turned(e):
                for n in range(TF):
                    c, half = n // 2, n % 2
                    wait(act, t_full, e * TF, n + 1)
                    act.activation(xTh[:, c, half * HALF:(half + 1) * HALF], up_bank[n % 2][:, 0:HALF], ACT.Copy).then_inc(th_done, 1)

            def expert(e, more):
                wait(act, b1_set, e, 1)
                for c in range(CH):
                    for n in range(UP):
                        f, half = n // 2, n % 2
                        wait(act, up_full, e * CH * UP, c * UP + n + 1)
                        if half == 0:
                            wait(act, hl_done, e * CH * FT, c * FT + f - 1)
                        act.activation(gel[f % 2][:, half * HALF:(half + 1) * HALF], up_bank[n % 2][:, 0:HALF], ACT.Gelu,
                                       bias=b1s[:, c * FT + f:c * FT + f + 1]).then_inc(gelu_done, 1)
                        if n < CT:
                            w2_high(e, c, n)
                        elif c < CH - 1:
                            w1_high(e, c + 1, n - CT)
                        elif more:
                            w1_high(e + 1, 0, n - CT)
                if more:
                    turned(e + 1)

            for k in range(CT):
                w1_high(0, 0, k)
            turned(0)
            expert(0, True)
            with act.Fori(1, E - 1) as e:
                expert(e, True)
            expert(E - 1, False)

        @block.vector
        def _(dve):
            def w1_low(e, c, k):
                wait(dve, w1h_done, e * CH * CT, c * CT + k + 1)
                if k == 0:
                    wait(dve, up_full, e * CH * UP, (c - 1) * UP)
                s = c % 2
                dve.tensor_tensor(w1l[s][:, k, :], w1s[:, k, :], f32(w1h[s][:, k, :]), ALU.subtract).then_inc(w1l_done, 1)

            def w2_low(e, c, k):
                wait(dve, w2h_done, e * CH * FT, c * FT + k + 1)
                s = c % 2
                dve.tensor_tensor(w2l[s][:, k, :], w2s[:, k, :], f32(w2h[s][:, k, :]), ALU.subtract).then_inc(w2l_done, 1)

            def normalise(e):
                wait(dve, rows_in, e * 16 * ST, 16 * ST)
                wait(dve, t_full, e * TF, 0)
                for k in range(ST):
                    dve.tensor_scalar(xn[:, k, :], xg[:, k, 0:C], xg[:, k, C:C + 1], xg[:, k, C + 1:C + 2],
                                      ALU.subtract, ALU.mult).then_inc(xn_done, 1)

            def turned(e):
                for n in range(TF):
                    c, half = n // 2, n % 2
                    cols = slice(half * HALF, (half + 1) * HALF)
                    wait(dve, th_done, e * TF, n + 1)
                    dve.tensor_tensor(xTl[:, c, cols], up_bank[n % 2][:, 0:HALF], f32(xTh[:, c, cols]), ALU.subtract).then_inc(tl_done, 1)

            def set_bias(e):
                src = b1all[:, e * CH * FT:(e + 1) * CH * FT] if isinstance(e, int) else b1all[:, bass.ds(e * CH * FT, CH * FT)]
                wait(dve, gelu_done, e * CH * UP, 0)
                dve.tensor_copy(b1s[:], src).then_inc(b1_set, 1)

            def residual(e):
                wait(dve, b2_in, e * 16, 16)
                dve.tensor_scalar(gp[:], xg[:, :, C + 2], gate2[:, 0:1], None, ALU.mult).then_inc(gp_done, 1)
                wait(dve, scattered, e * 16 * ST, 0)
                dve.tensor_copy(idx_s[:], idx_g[:]).then_inc(idx_kept, 1)
                wait(dve, gp_done, e, 1)
                for k in range(ST):
                    dve.scalar_tensor_tensor(out=res[:, k, :], in0=b2b[:], scalar=gp[:, k:k + 1], in1=xg[:, k, 0:C],
                                             op0=ALU.mult, op1=ALU.add).then_inc(res_done, 1)

            def finish(e):
                for k in range(ST):
                    wait(dve, y_full, e * ST, k + 1)
                    wait(dve, res_done, e * ST, k + 1)
                    dve.scalar_tensor_tensor(out=res[:, k, :], in0=y_bank[k][:], scalar=gp[:, k:k + 1], in1=res[:, k, :],
                                             op0=ALU.mult, op1=ALU.add).then_inc(out_done, 1)

            def expert(e, more):
                for c in range(CH):
                    s = c % 2
                    for f in range(FT):
                        wait(dve, gelu_done, e * CH * UP, c * UP + 2 * f + 2)
                        if f == 0:
                            if c >= 2:
                                wait(dve, *downs(e, c - 2))
                            elif not (isinstance(e, int) and e == 0):
                                wait(dve, *downs(e - 1, c + 2))
                        dve.tensor_copy(hh[s][:, f, :], gel[f % 2][:]).then_inc(hh_done, 1)
                        if f < 2:
                            w2_low(e, c, 2 * f)
                            w2_low(e, c, 2 * f + 1)
                        elif c < CH - 1 or more:
                            nxt = (e, c + 1) if c < CH - 1 else (e + 1, 0)
                            w1_low(*nxt, 2 * f - CT)
                            w1_low(*nxt, 2 * f - CT + 1)
                        wait(dve, hh_done, e * CH * FT, c * FT + f + 1)
                        dve.tensor_tensor(hl[s][:, f, :], gel[f % 2][:], f32(hh[s][:, f, :]), ALU.subtract).then_inc(hl_done, 1)
                    if c == 0:
                        residual(e)
                    if c == 2 and more:
                        normalise(e + 1)
                if more:
                    set_bias(e + 1)
                    turned(e + 1)
                finish(e)

            dve.wait_ge(b1_in, 16)
            set_bias(0)
            normalise(0)
            for k in range(CT):
                w1_low(0, 0, k)
            turned(0)
            expert(0, True)
            with dve.Fori(1, E - 1) as e:
                expert(e, True)
            expert(E - 1, False)


def program(nc, x, ctx_768, g_xattn, g_ffn, Wq, bq, Wk, bk, Wv, bv, Wo, bo, router_w, w1, b1, w2, b2, out):
    B, S, C = x.shape
    N = B * S
    E = router_w.shape[0]
    CAP = -(-3 * N // (2 * E))
    CT = C // P
    attn_dram = nc.dram_tensor("attn_dram", [B * CT, P, S], F32).ap()
    mean_dram = nc.dram_tensor("mean_dram", [B, P, CT], F32).ap()
    rows_dram = nc.dram_tensor("rows_dram", [N + 1, C + 4], F32).ap()
    table = nc.dram_tensor("table", [E * CAP, 1], I32).ap()
    flat_out = out.rearrange("b s c -> (b s) c")
    with ExitStack() as ctx:
        def sb(name, shape, dt=F32):
            return ctx.enter_context(nc.sbuf_tensor(name, shape, dt))

        keep = {
            "ident": sb("ident", [P, P]),
            "ones": sb("ones", [P, P]),
            "eps": sb("eps", [P, 1]),
            "nan_acc": sb("nan_acc", [P, B * CT]),
            "gate2": sb("gate2", [P, 1]),
            "logits": sb("logits", [P, N // P, E]),
            "token": sb("token", [P, N // P, 4]),
        }
        made = keep["made"] = ctx.enter_context(nc.semaphore("made"))
        keep["passed"] = ctx.enter_context(nc.semaphore("passed"))
        with nc.Block() as block:
            @block.gpsimd
            def _(pool):
                pool.memset(keep["ident"][:], 0.0).then_inc(made, 1)
                pool.memset(keep["ones"][:], 1.0).then_inc(made, 1)
                pool.memset(keep["eps"][:], EPS).then_inc(made, 1)
                pool.memset(keep["token"][:], 0.0).then_inc(made, 1)
                pool.wait_ge(made, 4)
                pool.affine_select(out=keep["ident"][:], in_=keep["ident"][:], compare_op=ALU.not_equal, fill=1.0, base=0,
                                   pattern=[[-1, P]], channel_multiplier=1).then_inc(made, 1)
                pool.wait_ge(made, MADE)
        attention(nc, keep, x, ctx_768, Wq, bq, Wk, bk, Wv, attn_dram, mean_dram)
        projection(nc, keep, x, bv, Wo, bo, g_xattn, g_ffn, router_w, attn_dram, mean_dram, rows_dram, out)
        routing(nc, keep, N, E, CAP, C, rows_dram, table)
        experts(nc, keep, w1, b1, w2, b2, rows_dram, table, flat_out, CAP)


_INS = ["x", "ctx_768", "g_xattn", "g_ffn", "L0_xattn_Wq", "L0_xattn_bq", "L0_xattn_Wk", "L0_xattn_bk", "L0_xattn_Wv",
        "L0_xattn_bv", "L0_xattn_Wo", "L0_xattn_bo", "L0_ffn_router_w", "L0_ffn_w1", "L0_ffn_b1", "L0_ffn_w2", "L0_ffn_b2"]


def kernel(**inputs):
    import numpy as np
    import concourse.bacc as bacc
    from concourse.bass_utils import run_bass_kernel_spmd

    nc = bacc.Bacc("TRN2", target_bir_lowering=False, num_devices=1)
    arrays, args = {}, []
    for name in _INS:
        a = np.ascontiguousarray(inputs[name])
        arrays[f"in_{name}"] = a
        args.append(nc.dram_tensor(f"in_{name}", a.shape, mybir.dt.from_np(a.dtype), kind="ExternalInput").ap())
    args.append(nc.dram_tensor("out_0", inputs["x"].shape, F32, kind="ExternalOutput").ap())
    program(nc, *args)
    return run_bass_kernel_spmd(nc, [arrays], core_ids=[0]).results[0]["out_0"]
```

```python
from contextlib import ExitStack

import concourse.bass as bass
from concourse import mybir

F32 = mybir.dt.float32
F32R = mybir.dt.float32r
I32 = mybir.dt.int32
ALU = mybir.AluOpType
ACT = mybir.ActivationFunctionType
AX_X = mybir.AxisListType.X
P = 128
EPS = 1e-5
CLAMP = 10000.0
HEADS = 16
MADE = 6


def wait(eng, sem, base, count):
    if isinstance(base, int) and base + count <= 0:
        return
    eng.wait_ge(sem, base + count)


def wait_apart(eng, keep, sem, base, count):
    wait(eng, sem, base, count)
    if not isinstance(base, int):
        eng.sem_inc(keep["passed"], 1)


def make_pools(nc, ctx):
    def sb(name, shape, dt=F32):
        return ctx.enter_context(nc.sbuf_tensor(name, shape, dt))

    def ps(name):
        return ctx.enter_context(nc.psum_tensor(name, [P, 512], F32))

    def sem(name):
        return ctx.enter_context(nc.semaphore(name))

    return sb, ps, sem


def pool_rsqrt(pool, keep, chain, base, var, r0):
    shape = list(var.shape)
    pool.tensor_tensor(r0, var, keep["eps"][:, 0:1].to_broadcast(shape), ALU.add).then_inc(chain, 1)
    wait(pool, chain, base, 1)
    pool.tensor_tensor(r0, r0, keep["minus_half"][:, 0:1].to_broadcast(shape), ALU.pow).then_inc(chain, 1)


def newton_rsqrt(dve, chain, base, var, r0, tmp, r):
    dve.tensor_tensor(tmp, r0, r0, ALU.mult).then_inc(chain, 1)
    wait(dve, chain, base, 1)
    dve.scalar_tensor_tensor(out=tmp, in0=var, scalar=EPS, in1=tmp, op0=ALU.add, op1=ALU.mult).then_inc(chain, 1)
    wait(dve, chain, base, 2)
    dve.tensor_scalar(tmp, tmp, -0.5, 1.5, ALU.mult, ALU.add).then_inc(chain, 1)
    wait(dve, chain, base, 3)
    dve.tensor_tensor(r, r0, tmp, ALU.mult).then_inc(chain, 1)


def attention(nc, keep, early, Wo, x, ctx_in, Wq, bq, Wk, bk, Wv, attn_dram):
    B, S, C = x.shape
    CK = ctx_in.shape[2]
    T = S // P
    CT, CKT = C // P, CK // P
    HG = HEADS // CT
    D = C // HEADS
    R3 = 3 * D
    STACK = 3 * 16
    SCALE = float(D) ** -0.5
    EXP, TURN, LOW, WEIGH, JOIN = 2, 4, 0, 7, 12
    QB = HEADS * T
    STATS, SUMS, RSQRT, NEWTON, ROWS = 22, 26, 28, 31, 32
    NAN_SUM, KEEP_CSUM = 40, 46
    JOINED = 2
    OUT = 2 * (HG - JOINED)
    assert T == 4 and HG == 4 and CT == 4

    PLAN = [(3, "sum", CT - 1, False), (5, "q", 1, False), (8, "k", 1, False)]
    PLAN += [(11, "v", 2, False), (13, "v", 3, False), (15, "v", 4, False)]
    PLAN += [(19, "sum", 0, False), (22, "q", 2, False), (25, "k", 2, False)]
    PLAN += [(32, "q", 3, False), (35, "k", 3, False), (37, "sum", 1, False)]
    PLAN += [(38 + c, "x", c, True) for c in range(CT)] + [(42 + c, "c", c, True) for c in range(CKT)]
    PLAN += [(47, "q", 0, True), (50, "k", 0, True), (52, "sum", 2, False)]
    PLAN += [(55, "v", 0, True), (58, "v", 1, True)]
    V_FILLS = ((0, 0, 2), (0, 2, 2), (1, 0, 2), (1, 2, 1), (1, 3, 1))
    PARTS = {"q": (0, 1, 2), "k": (0, 1, 2), "v": (1, 2)}
    SPLIT = ("q", "k", "v", "x", "c")
    HEAD = [f for f in PLAN if f[3]]

    def fills(b):
        if b < 0:
            return HEAD
        if b == B:
            return PLAN[:1]
        return [f for f in PLAN if not (b == 0 and f is PLAN[0]) and not (b == B - 1 and f[3])]

    def before(b, fill, kinds=None):
        count = lambda fs: sum(1 for f in fs if kinds is None or f[1] in kinds)
        if isinstance(b, int):
            fs = fills(b)
            return 0, sum(count(fills(c)) for c in range(-1, b)) + count(fs[:fs.index(fill)])
        return b * count(PLAN), count(HEAD) + count(fills(0)) - count(PLAN) + count(PLAN[:PLAN.index(fill)])

    def upto(b, fill, kinds=None):
        base, num = before(b, fill, kinds)
        return base, num + 1

    def planned(kind, n):
        return next(f for f in PLAN if f[1:3] == (kind, n))

    def plan_at(b, quarter):
        return [f for f in (fills(b) if isinstance(b, int) else PLAN) if f[0] == quarter]

    def quarters(b):
        return range(QB) if not (isinstance(b, int) and b == B) else range(JOIN + T)

    def tile_at(b, quarter, trail):
        n = quarter - trail
        if isinstance(b, int) and (b == 0 and n < 0 or b == B and n >= 0):
            return None
        return n

    def run(eng, body):
        body(0)
        with eng.Fori(1, B - 1) as b:
            body(b)
        body(B - 1)
        body(B)

    with ExitStack() as ctx:
        sb, ps, sem = make_pools(nc, ctx)
        wqh, wql = sb("wqh", [P, CT, C], F32R), sb("wql", [P, CT, C], F32R)
        wkh, wkl = sb("wkh", [P, CKT, C], F32R), sb("wkl", [P, CKT, C], F32R)
        wvh, wvl = sb("wvh", [P, CKT, C], F32R), sb("wvl", [P, CKT, C], F32R)
        bqT = sb("bqT", [P, CT])
        bkT = sb("bkT", [P, CT])
        xn = sb("xn", [P, T, C])
        cx = sb("cx", [P, T, CK])
        stats = sb("stats", [P, T, 6])
        mv = sb("mv", [P, T, 2])
        r0 = sb("r0", [P, T])
        tmp = sb("tmp", [P, T])
        rs = sb("rs", [P, T])
        xTh, xTl = sb("xTh", [P, CT, S], F32R), sb("xTl", [P, CT, S], F32R)
        cTh, cTl = sb("cTh", [P, CKT, S], F32R), sb("cTl", [P, CKT, S], F32R)
        qh, ql = sb("qh", [P, S], F32R), sb("ql", [P, S], F32R)
        kh, kl = sb("kh", [P, S], F32R), sb("kl", [P, S], F32R)
        qs = [sb(f"qs{i}", [R3, HG, S], F32R) for i in range(2)]
        ks = [sb(f"ks{i}", [R3, HG, S], F32R) for i in range(2)]
        v = sb("v", [P, T, HEADS, 2, D], F32R)
        qsum = sb("qsum", [P, CT])
        ksum = sb("ksum", [P, CT])
        csum = sb("csum", [P, CKT])
        csums = sb("csums", [P, CKT, B])
        prob = [sb(f"prob{i}", [P, T, S]) for i in range(2)]
        negmax = [sb(f"negmax{i}", [P, T]) for i in range(2)]
        rowsum = [sb(f"rowsum{i}", [P, T, HG]) for i in range(2)]
        rinv = sb("rinv", [P, T, HG])
        rinvx = sb("rinvx", [P, T, C // CT])
        probTh, probTl = (sb(name, [P, 2, T, 2 * P], F32R) for name in ("probTh", "probTl"))
        scaleT = sb("scaleT", [P, S])
        att_low = [sb(f"att_low{i}", [P, S]) for i in range(2)]
        vlow = [sb(f"vlow{i}", [D, S]) for i in range(2)]
        att = [sb(f"att{i}", [P, S]) for i in range(2)]

        proj_bank = [ps(f"proj_bank{i}") for i in range(2)]
        score_bank = [ps(f"score_bank{i}") for i in range(2)]
        turn_bank = [ps(f"turn_bank{i}") for i in range(2)]
        att_bank = [ps(f"att_bank{i}") for i in range(2)]

        wq_in = sem("wq_in")
        wk_in = sem("wk_in")
        wv_in = sem("wv_in")
        bias_in = sem("bias_in")
        w_high = sem("w_high")
        w_low = sem("w_low")
        x_in = sem("x_in")
        ctx_in_s = sem("ctx_in_s")
        stats_done = sem("stats_done")
        aggr_done = sem("aggr_done")
        rsqrt_done = sem("rsqrt_done")
        newton = sem("newton")
        xn_done = sem("xn_done")
        proj_full = sem("proj_full")
        proj_high = sem("proj_high")
        proj_low = sem("proj_low")
        nan_sum = sem("nan_sum")
        q_written = sem("q_written")
        k_written = sem("k_written")
        q_stacked = sem("q_stacked")
        k_stacked = sem("k_stacked")
        score_full = sem("score_full")
        score_read = sem("score_read")
        exp_done = sem("exp_done")
        turn_full = sem("turn_full")
        turn_high = sem("turn_high")
        turn_low = sem("turn_low")
        weighed = sem("weighed")
        vlow_done = sem("vlow_done")
        copied_out = sem("copied_out")
        added = sem("added")
        joined = sem("joined")
        rinv_done = sem("rinv_done")
        rinvx_done = sem("rinvx_done")
        att_done = sem("att_done")
        att_out = [sem(f"att_out{i}") for i in range(2)]
        csum_kept = sem("csum_kept")
        mean_full = sem("mean_full")

        ident, nan_acc = keep["ident"], keep["nan_acc"]
        xr = x.rearrange("b (t p) c -> b p t c", p=P)
        cr = ctx_in.rearrange("b (t p) c -> b p t c", p=P)
        f32 = lambda t: t.bitcast(F32)
        turned = lambda t, n: t[:, n // 2 % 2, :, n % 2 * P:(n % 2 + 1) * P]
        def v_part(n, part):
            half, t0, tiles = V_FILLS[n]
            return v[:, t0:t0 + tiles, half * HEADS // 2:(half + 1) * HEADS // 2, part, :]

        def v_filled(bank, n):
            return bank[:, 0:V_FILLS[n][2] * C // 2].rearrange("p (t h d) -> p t h d", d=D, h=HEADS // 2)

        by_key = lambda bank: bank[:].rearrange("p (k q) -> p k q", q=P)
        at_batch = lambda t, b: t[b] if isinstance(b, int) else t[bass.ds(b, 1)].rearrange("o p t c -> (o p) t c")
        stage = (prob[0][:], prob[1][:, 0:CKT, :], prob[0][:, 0:CKT, :])

        parts_dram = {kind: nc.dram_tensor(f"parts_{kind}", [2, P, S], F32).ap() for kind in "qk"}

        def parts_written(b, f):
            _, kind, n, ahead = f
            return (q_written if kind == "q" else k_written), b * CT * 32, 32 * (n + CT if ahead else n) + 32

        def bank_of(b, f):
            assert len(PLAN) % 2 == 0
            return proj_bank[(sum(before(b, f)) if isinstance(b, int) else before(b, f)[1]) % 2]

        block = ctx.enter_context(nc.Block())

        @block.sync
        def _(sp):
            sp.dma_start(xn[:], xr[0]).then_inc(x_in, 16)
            sp.dma_start(cx[:], cr[0]).then_inc(ctx_in_s, 16)
            sp.dma_start(stage[0], Wq.rearrange("(t p) n -> p t n", p=P)).then_inc(wq_in, 16)
            sp.dma_start(stage[1], Wk.rearrange("(t p) n -> p t n", p=P)).then_inc(wk_in, 16)
            sp.dma_start(bqT[:], bq.rearrange("(t p) -> p t", p=P), allow_slow_non_contiguous=True).then_inc(bias_in, 16)
            sp.dma_start(bkT[:], bk.rearrange("(t p) -> p t", p=P), allow_slow_non_contiguous=True).then_inc(bias_in, 16)

            sp.dma_start(early["wo"][:], Wo.rearrange("(t p) n -> p t n", p=P)).then_inc(early["w_in"], 16)
            sp.wait_ge(w_low, 2)
            sp.dma_start(stage[2], Wv.rearrange("(t p) n -> p t n", p=P)).then_inc(wv_in, 16)

            def tasks(b, fs):
                for f in fs:
                    _, kind, n, ahead = f
                    base, num = before(b, f)
                    if kind in "qk":
                        high, low, written = (qh, ql, q_written) if kind == "q" else (kh, kl, k_written)
                        wait_apart(sp, keep, proj_high, base, num + 1)
                        sp.dma_start(parts_dram[kind][0], f32(high[:])).then_inc(written, 16)
                        wait_apart(sp, keep, proj_low, *upto(b, f, SPLIT))
                        sp.dma_start(parts_dram[kind][1], f32(low[:])).then_inc(written, 16)
                    nxt = b + 2 if ahead else b + 1
                    more = not isinstance(b, int) or b + 2 < B
                    if kind == "x" and n == CT - 1 and more:
                        wait_apart(sp, keep, proj_full, base, num + 1)
                        sp.dma_start(xn[:], at_batch(xr, nxt)).then_inc(x_in, 16)
                    if kind == "c" and n == CKT - 1 and more:
                        wait_apart(sp, keep, proj_full, base, num + 1)
                        sp.dma_start(cx[:], at_batch(cr, nxt)).then_inc(ctx_in_s, 16)

            def body(b):
                tasks(b, fills(b) if isinstance(b, int) else PLAN)

            tasks(-1, HEAD)
            body(0)
            with sp.Fori(1, B - 2) as b:
                body(b)
            body(B - 2)
            body(B - 1)

        @block.gpsimd
        def _(pool):
            def deviation(b):
                wait(pool, aggr_done, b * T, 2 * T)
                pool_rsqrt(pool, keep, rsqrt_done, b * 2 + 2, mv[:, :, 1], r0[:])

            def stack(b, f):
                _, kind, n, ahead = f
                g = n + CT if ahead else n
                wait_apart(pool, keep, score_full, b * QB, (g - 1) * HG * T)
                wait_apart(pool, keep, *parts_written(b, f))
                stacked, done = (qs, q_stacked) if kind == "q" else (ks, k_stacked)
                for i, part in enumerate((0, 0, 1) if kind == "q" else (0, 1, 0)):
                    pool.dma_start(stacked[n % 2][i * D:(i + 1) * D, :, :], parts_dram[kind][part].rearrange("(j p) s -> p j s", p=D)).then_inc(done, 16)

            def body(b):
                for quarter in quarters(b):
                    for f in plan_at(b, quarter - 1):
                        if f[1] in "qk":
                            stack(b, f)
                    if quarter == RSQRT and not (isinstance(b, int) and b >= B - 1):
                        deviation(b)
                    n = tile_at(b, quarter, JOIN)
                    if n is not None and n % (HG * T) == (HG - 1) * T:
                        g = n // (HG * T)
                        wait(pool, proj_high, *upto(b, planned("sum", g % CT)))
                        wait_apart(pool, keep, copied_out, b * CT * OUT, (g + 1) * OUT)
                        rows = slice(JOINED * D, P)
                        pool.tensor_tensor(att[g % 2][rows, :], att[g % 2][rows, :], att_low[g % 2][rows, :], ALU.add).then_inc(added, 1)
                        wait(pool, joined, b * CT * JOINED, (g + 1) * JOINED)
                        wait(pool, added, b * CT, g + 1)
                        pool.tensor_tensor(att[g % 2][:], att[g % 2][:], scaleT[:], ALU.mult).then_inc(att_done, 1)
                        wait_apart(pool, keep, att_done, b * CT, g + 1)
                        row = attn_dram[b * CT + g] if isinstance(b, int) else attn_dram[bass.ds(b * CT + g, 1)].rearrange("o p s -> (o p) s")
                        pool.dma_start(row, att[g % 2][:]).then_inc(att_out[g % 2], 16)

            deviation(-1)
            for f in HEAD:
                if f[1] in "qk":
                    stack(-1, f)
            run(pool, body)
            for i in range(2):
                pool.wait_ge(att_out[i], 8 * CT * B)

        @block.tensor
        def _(pe):
            def fill(b, f, parts=(0, 1, 2)):
                _, kind, n, ahead = f
                base, num = before(b, f)
                bank = bank_of(b, f)
                if (parts_of(f) or parts)[0] in parts:
                    wait(pe, proj_high, base, num - 1)
                    wait(pe, proj_low, *low_before(b, f))
                if kind in "xc":
                    src, high = (xn, xn_done) if kind == "x" else (cx, ctx_in_s)
                    per = T if kind == "x" else 16
                    if n == 0:
                        wait(pe, high, b * per, 2 * per if ahead else per)
                    for t in range(T):
                        last = pe.transpose(bank[:, t * P:(t + 1) * P], src[:, t, n * P:(n + 1) * P], ident[:])
                elif kind in "qk":
                    wh, wl, th, tl, tiles = (wqh, wql, xTh, xTl, CT) if kind == "q" else (wkh, wkl, cTh, cTl, CKT)
                    if n == 0 and 0 in parts:
                        wait(pe, proj_low, *upto(b, planned("c", CKT - 1), SPLIT))
                    for i in parts:
                        w, t = ((wl, th), (wh, tl), (wh, th))[i]
                        for c in range(tiles):
                            last = pe.matmul(bank[:], w[:, c, n * P:(n + 1) * P], t[:, c, :],
                                             start=(i == 0 and c == 0), stop=(i == 2 and c == tiles - 1))
                elif kind == "v":
                    half, t0, tiles = V_FILLS[n]
                    cols = slice(half * C // 2, (half + 1) * C // 2)
                    for j in range(tiles):
                        if j + 3 - tiles not in parts:
                            continue
                        keys = slice((t0 + j) * P, (t0 + j + 1) * P)
                        for i, (c_, w) in enumerate(((cTl, wvh), (cTh, wvl), (cTh, wvh))):
                            for c in range(CKT):
                                last = pe.matmul(bank[:, j * C // 2:(j + 1) * C // 2], c_[:, c, keys], w[:, c, cols],
                                                 start=(i == 0 and c == 0), stop=(i == 2 and c == CKT - 1))
                else:
                    g = n - CT if f is PLAN[0] else n
                    wait(pe, rinvx_done, b * CT, g + 1)
                    for t in range(T):
                        last = pe.matmul(bank[:, t * P:(t + 1) * P], rinvx[:, t, :], ident[:], start=True, stop=True)
                if parts[-1] == 2:
                    last.then_inc(proj_full, 1)

            def low_before(b, f):
                fs = fills(b) if isinstance(b, int) else PLAN
                if f is fs[0]:
                    last = fills(B - 1)[-1] if isinstance(b, int) and b == B else PLAN[-1]
                else:
                    last = fs[fs.index(f) - 1]
                base, num = before(b, f, SPLIT)
                return base, num - (last[1] in SPLIT)

            def body(b):
                for quarter in quarters(b):
                    n = tile_at(b, quarter, WEIGH)
                    if n is not None:
                        h, pair, half = n // T, n // 2, n % 2
                        if n % T == 0:
                            g, j = (h - 2) // HG, (h - 2) % HG
                            if j < JOINED:
                                wait(pe, joined, b * CT * JOINED, g * JOINED + j + 1)
                            else:
                                wait(pe, copied_out, b * CT * OUT, g * OUT + 2 * (j - JOINED + 1))
                        if n == 0:
                            wait(pe, proj_low, *upto(b - 1, planned("v", 1), SPLIT))
                        elif n == QB // 2:
                            wait(pe, proj_low, *upto(b, planned("v", 4), SPLIT))
                        if half == 0:
                            wait(pe, turn_low, b * QB, n + 2)
                        out = att_bank[h % 2][0:2 * D, pair % 2 * 2 * P:(pair % 2 + 1) * 2 * P]
                        for k in range(half * T // 2, (half + 1) * T // 2):
                            for part in (probTl, probTh):
                                last = pe.matmul(out, v[:, k, h % HEADS, :, :].rearrange("p i d -> p (i d)"), part[:, pair % 2, k, :],
                                                 start=(k == 0 and part is probTl), stop=(k == T - 1 and part is probTh))
                        last.then_inc(weighed, 1)
                    n = tile_at(b, quarter, TURN)
                    if n is not None:
                        h, t = n // T, n % T
                        wait(pe, exp_done, b * QB, n + 1)
                        wait(pe, turn_low, b * QB, n - 1)
                        for k in range(T):
                            last = pe.transpose(turn_bank[n % 2][:, k * P:(k + 1) * P], prob[h % 2][:, t, k * P:(k + 1) * P], ident[:])
                        last.then_inc(turn_full, 1)
                    n = tile_at(b, quarter, 0)
                    if n is not None:
                        h, t = n // T, n % T
                        g, j = h // HG, h % HG
                        if n % (HG * T) == 0:
                            wait(pe, q_stacked, b * CT * STACK, (g + 1) * STACK)
                            wait(pe, k_stacked, b * CT * STACK, (g + 1) * STACK)
                        wait(pe, score_read, b * QB, n - 1)
                        pe.matmul(score_bank[n % 2][:], qs[g % 2][:, j, t * P:(t + 1) * P], ks[g % 2][:, j, :],
                                  start=True, stop=True).then_inc(score_full, 1)
                    for f in plan_at(b, quarter):
                        fill(b, f, (2,) if f[1] in PARTS else (0, 1, 2))
                    for late in (1, 2):
                        for f in plan_at(b, quarter + late):
                            if 2 - late in parts_of(f):
                                fill(b, f, (2 - late,))

            def parts_of(f):
                _, kind, n, _ = f
                return () if kind not in PARTS or kind == "v" and V_FILLS[n][2] == 1 else PARTS[kind]

            pe.wait_ge(keep["made"], MADE)
            for f in HEAD:
                if f[1:3] in (("q", 0), ("k", 0), ("v", 0)):
                    pe.wait_ge(w_low, {"q": 2, "k": 3, "v": 4}[f[1]])
                fill(-1, f)
            run(pe, body)
            pe.wait_ge(csum_kept, B)
            pe.wait_ge(proj_high, sum(len(fills(b)) for b in range(-1, B + 1)))
            for g in range(CT):
                for i, w in enumerate((wvl, wvh)):
                    for c in range(CKT):
                        last = pe.matmul(proj_bank[0][:, g * B:(g + 1) * B], f32(w[:, c, g * P:(g + 1) * P]), csums[:, c, :],
                                         start=(i == 0 and c == 0), stop=(i == 1 and c == CKT - 1))
            last.then_inc(mean_full, 1)

        @block.scalar
        def _(act):
            def read(b, f):
                _, kind, n, ahead = f
                base, num = before(b, f)
                bank = bank_of(b, f)
                more = {}
                if kind == "x":
                    out = xTh[:, n, :]
                elif kind == "c":
                    out, more = cTh[:, n, :], {"accum_out": csum[:, n:n + 1]}
                elif kind == "v":
                    wait(act, proj_full, base, num + 1)
                    act.activation(v_part(n, 0), v_filled(bank, n), ACT.Identity).then_inc(proj_high, 1)
                    return
                elif kind == "sum":
                    g = n if f is not PLAN[0] else n - CT
                    wait(act, att_done, b * CT, g)
                    out = scaleT[:]
                else:
                    high, bias, total, stacked = (qh, bqT, qsum, q_stacked) if kind == "q" else (kh, bkT, ksum, k_stacked)
                    if n == 0:
                        act.wait_ge(w_low, 1)
                        wait(act, nan_sum, b, 1)
                    g = n + CT if ahead else n
                    wait(act, stacked, b * CT * STACK, g * STACK)
                    out, more = high[:], {"bias": bias[:, n:n + 1], "accum_out": total[:, n:n + 1]}
                wait(act, proj_full, base, num + 1)
                act.activation(out, bank[:], ACT.Identity, **more).then_inc(proj_high, 1)

            def body(b):
                for quarter in quarters(b):
                    n = tile_at(b, quarter, JOIN)
                    if n is not None and n % T == 0:
                        h = n // T
                        g, j = h // HG, h % HG
                        wait(act, weighed, b * QB, (h + 1) * T)
                        if j < JOINED:
                            act.activation(vlow[h % 2][:], att_bank[h % 2][D:2 * D, :], ACT.Identity).then_inc(vlow_done, 1)
                        else:
                            if j == JOINED:
                                wait(act, att_out[g % 2], b * 8 * CT, 16 * (g // 2))
                            rows = slice(j * D, (j + 1) * D)
                            act.activation(att_low[g % 2][rows, :], att_bank[h % 2][D:2 * D, :], ACT.Identity).then_inc(copied_out, 1)
                            act.activation(att[g % 2][rows, :], att_bank[h % 2][0:D, :], ACT.Identity).then_inc(copied_out, 1)
                    n = tile_at(b, quarter, TURN)
                    if n is not None:
                        wait(act, turn_full, b * QB, n + 1)
                        act.activation(turned(probTh, n), by_key(turn_bank[n % 2]), ACT.Identity).then_inc(turn_high, 1)
                    n = tile_at(b, quarter, EXP)
                    if n is not None:
                        h, t = n // T, n % T
                        g, j = h // HG, h % HG
                        wait(act, score_read, b * QB, n + 1)
                        act.activation(prob[h % 2][:, t, :], prob[h % 2][:, t, :], ACT.Exp, bias=negmax[h % 2][:, t:t + 1], scale=-1.0,
                                       accum_out=rowsum[g % 2][:, t, j:j + 1]).then_inc(exp_done, 1)
                    for f in plan_at(b, quarter):
                        read(b, f)

            def weights_high(i):
                loaded, w = ((wq_in, wqh), (wk_in, wkh), (wv_in, wvh))[i]
                act.wait_ge(loaded, 16)
                act.activation(w[:], stage[i], ACT.Copy, scale=-SCALE if i == 0 else 1.0).then_inc(w_high, 1)

            weights_high(0)
            weights_high(1)
            act.wait_ge(bias_in, 32)
            for f in HEAD:
                if f[1:3] == ("q", 0):
                    weights_high(2)
                read(-1, f)
            run(act, body)
            act.wait_ge(mean_full, 1)
            act.activation(keep["meanv"][:], proj_bank[0][:, 0:CT * B].rearrange("p (g b) -> p g b", b=B), ACT.Copy, scale=1.0 / S)

        @block.vector
        def _(dve):
            def layernorm_stats(b, t):
                if t == 0:
                    wait(dve, x_in, b * 16, 32)
                dve.bn_stats(stats[:, t, :], xn[:, t, :]).then_inc(stats_done, 1)

            def layernorm_sums(b):
                wait_apart(dve, keep, stats_done, b * T, 2 * T)
                for t in range(T):
                    dve.bn_aggr(mv[:, t, :], stats[:, t, :]).then_inc(aggr_done, 1)

            def layernorm_deviation(b):
                wait(dve, rsqrt_done, b * 2, 4)
                newton_rsqrt(dve, newton, b * 4 + 4, mv[:, :, 1], r0[:], tmp[:], rs[:])

            def layernorm(b, t):
                if t == 0:
                    wait(dve, newton, b * 4, 8)
                dve.tensor_scalar(xn[:, t, :], xn[:, t, :], mv[:, t, 0:1], rs[:, t:t + 1],
                                  ALU.subtract, ALU.mult).then_inc(xn_done, 1)

            def low(b, f):
                _, kind, n, ahead = f
                base, num = before(b, f)
                bank = bank_of(b, f)
                wait(dve, proj_high, base, num + 1)
                if kind == "x":
                    dve.tensor_tensor(xTl[:, n, :], bank[:], f32(xTh[:, n, :]), ALU.subtract).then_inc(proj_low, 1)
                elif kind == "c":
                    dve.tensor_tensor(cTl[:, n, :], bank[:], f32(cTh[:, n, :]), ALU.subtract).then_inc(proj_low, 1)
                elif kind == "v":
                    dve.tensor_tensor(v_part(n, 1), v_filled(bank, n), f32(v_part(n, 0)), ALU.subtract).then_inc(proj_low, 1)
                else:
                    high, part, bias = (qh, ql, bqT) if kind == "q" else (kh, kl, bkT)
                    dve.scalar_tensor_tensor(out=part[:], in0=bank[:], scalar=bias[:, n:n + 1], in1=f32(high[:]),
                                             op0=ALU.add, op1=ALU.subtract).then_inc(proj_low, 1)

            def keep_csum(b):
                wait_apart(dve, keep, proj_high, *upto(b, planned("c", CKT - 1)))
                column = csums[:, :, b + 1:b + 2] if isinstance(b, int) else csums[:, :, bass.ds(b + 1, 1)]
                dve.tensor_copy(column, csum[:].unsqueeze(2)).then_inc(csum_kept, 1)

            def body(b):
                for quarter in quarters(b):
                    n = tile_at(b, quarter, TURN + LOW)
                    if n is not None:
                        wait(dve, turn_high, b * QB, n + 1)
                        dve.tensor_tensor(turned(probTl, n), by_key(turn_bank[n % 2]), f32(turned(probTh, n)), ALU.subtract).then_inc(turn_low, 1)
                    n = tile_at(b, quarter, 0)
                    if n is not None:
                        h, t = n // T, n % T
                        if t == 0:
                            wait(dve, turn_full, b * QB, (h - 1) * T)
                        wait(dve, score_full, b * QB, n + 1)
                        dve.tensor_scalar(prob[h % 2][:, t, :], score_bank[n % 2][:], -CLAMP, CLAMP, ALU.max, ALU.min,
                                          accum_out=negmax[h % 2][:, t:t + 1]).then_inc(score_read, 1)
                    n = tile_at(b, quarter, JOIN)
                    if n is not None and n % T == 0 and n // T % HG < JOINED:
                        h = n // T
                        g, j = h // HG, h % HG
                        if j == 0:
                            wait(dve, att_out[g % 2], b * 8 * CT, 16 * (g // 2))
                        wait(dve, vlow_done, b * CT * JOINED, g * JOINED + j + 1)
                        dve.tensor_tensor(att[g % 2][j * D:(j + 1) * D, :], att_bank[h % 2][0:D, :], vlow[h % 2][:], ALU.add).then_inc(joined, 1)
                    n = tile_at(b, quarter, HG * T + 1)
                    if n is not None and n % (HG * T) == 0:
                        g = n // (HG * T)
                        wait(dve, exp_done, b * QB, (g + 1) * HG * T)
                        wait(dve, rinvx_done, b * CT, g)
                        dve.reciprocal(rinv[:], rowsum[g % 2][:]).then_inc(rinv_done, 1)
                        if g < 0:
                            wait(dve, proj_full, *upto(b - 1, planned("sum", CT - 2)))
                        elif not (isinstance(b, int) and b == 0 and g == 0):
                            wait(dve, proj_full, *upto(b, planned("sum", (g - 1) % CT)))
                        wait(dve, rinv_done, b * CT, g + 1)
                        dve.tensor_copy(rinvx[:].rearrange("p t (j d) -> p (t j) d", d=D),
                                        rinv[:].rearrange("p t j -> p (t j)").unsqueeze(2).to_broadcast([P, T * HG, D])
                                        ).then_inc(rinvx_done, 1)
                    for f in plan_at(b, quarter):
                        if f[1] in SPLIT:
                            low(b, f)
                    if quarter == KEEP_CSUM and not (isinstance(b, int) and b >= B - 1):
                        keep_csum(b)
                    if quarter == NAN_SUM and not (isinstance(b, int) and b >= B):
                        wait(dve, proj_high, *upto(b, planned("k", CT - 1)))
                        acc = nan_acc[:, b * CT:(b + 1) * CT] if isinstance(b, int) else nan_acc[:, bass.ds(b * CT, CT)]
                        dve.tensor_tensor(acc, qsum[:], ksum[:], ALU.mult).then_inc(nan_sum, 1)
                    if not (isinstance(b, int) and b >= B - 1):
                        if quarter in range(STATS, STATS + T):
                            layernorm_stats(b, quarter - STATS)
                        if quarter == SUMS:
                            layernorm_sums(b)
                        if quarter == NEWTON:
                            layernorm_deviation(b)
                        if quarter in range(ROWS, ROWS + T):
                            layernorm(b, quarter - ROWS)

            for t in range(T):
                layernorm_stats(-1, t)
            layernorm_sums(-1)
            layernorm_deviation(-1)
            for t in range(T):
                layernorm(-1, t)
            dve.wait_ge(bias_in, 32)
            dve.tensor_scalar(bqT[:], bqT[:], -SCALE, None, ALU.mult).then_inc(w_low, 1)
            def weights_low(i):
                high, low_part = ((wqh, wql), (wkh, wkl), (wvh, wvl))[i]
                dve.wait_ge(w_high, i + 1)
                dve.scalar_tensor_tensor(out=low_part[:], in0=stage[i], scalar=-SCALE if i == 0 else 1.0, in1=f32(high[:]),
                                         op0=ALU.mult, op1=ALU.subtract).then_inc(w_low, 1)

            weights_low(0)
            weights_low(1)
            for f in HEAD:
                if f[1:3] == ("q", 0):
                    weights_low(2)
                if f[1] in SPLIT:
                    low(-1, f)
            keep_csum(-1)
            run(dve, body)


def projection(nc, keep, early, x, attn_dram, rows_dram):
    B, S, C = x.shape
    T, CT = S // P, C // P
    E = early["rw"].shape[0]
    N = B * S
    W = rows_dram.shape[1]
    U = 4
    with ExitStack() as ctx:
        sb, ps, sem = make_pools(nc, ctx)
        rwT = sb("rwT", [P, CT, E])
        nan_row = sb("nan_row", [P, 1])
        nan_tot = sb("nan_tot", [P, 1])
        nan_f = sb("nan_f", [P, 1])
        nan_mask = sb("nan_mask", [P, 1], I32)
        att = [sb(f"pat{i}", [P, CT, S]) for i in range(U)]
        woh, wol = sb("woh", [P, CT, C], F32R), sb("wol", [P, CT, C], F32R)
        atth = [sb(f"atth{i}", [P, CT, S], F32R) for i in range(2)]
        attl = [sb(f"attl{i}", [P, CT, S], F32R) for i in range(2)]
        xs = [sb(f"xs{i}", [P, T, C]) for i in range(U)]
        xn = [sb(f"pxn{i}", [P, T, C]) for i in range(2)]
        stats = sb("pstats", [P, T, 6])
        mv = sb("pmv", [P, T, 2])
        r0 = sb("pr0", [P, T])
        tmp = sb("ptmp", [P, T])
        rs = sb("prs", [P, T])
        xT = sb("pxT", [P, CT, S])
        lT = sb("lT", [E, S])
        padrow = sb("padrow", [1, W])

        y_bank = [ps(f"y_bank{i}") for i in range(T)]
        t_bank = [ps(f"t_bank{i}") for i in range(2)]
        expert_bank = ps("expert_bank")
        token_bank = ps("token_bank")
        c_bank, d_bank = y_bank[T - 2:]

        att_in = [sem(f"b_att_in{i}") for i in range(U)]
        x_in = [sem(f"b_x_in{i}") for i in range(U)]
        setup = sem("b_setup")
        pad_made = sem("b_pad_made")
        nan_s = sem("b_nan")
        const_pe = sem("b_const_pe")
        const_act = sem("b_const_act")
        blended = sem("b_blended")
        wo_high = sem("b_wo_high")
        wo_low = sem("b_wo_low")
        att_high = sem("b_att_high")
        att_low = sem("b_att_low")
        biased = sem("b_biased")
        y_full = sem("b_y_full")
        x1_done = sem("b_x1_done")
        stats_done = sem("b_stats")
        aggr_done = sem("b_aggr")
        rsqrt_done = sem("b_rsqrt")
        newton = sem("b_newton")
        kept_stats = sem("b_kept")
        xn_done = sem("b_xn")
        t_full = sem("b_t_full")
        t_read = sem("b_t_read")
        lT_full = sem("b_lT_full")
        lT_read = sem("b_lT_read")
        l_full = sem("b_l_full")
        l_read = sem("b_l_read")
        stored = [sem(f"b_stored{i}") for i in range(U)]
        pad_out = sem("b_pad_out")

        ident, ones, gate2 = keep["ident"], keep["ones"], keep["gate2"]
        wo, bvT, bo_b, gate, rw, w_in = (early[name] for name in ("wo", "bvT", "bo_b", "gate", "rw", "w_in"))
        xr = x.rearrange("b (t p) c -> b p t c", p=P)
        ar = attn_dram.rearrange("(b g) p s -> b p g s", g=CT)
        rrow = rows_dram[0:N, :].rearrange("(b t p) w -> b p t w", p=P, t=T)

        def at(t, b):
            if isinstance(b, int):
                return t[b]
            names = "p t c" if len(t.shape) == 4 else "p c"
            return t[bass.ds(b, 1)].rearrange(f"o {names} -> (o {names.split()[0]}) {' '.join(names.split()[1:])}")

        block = ctx.enter_context(nc.Block())

        @block.sync
        def _(sp):
            def round_of(i):
                for u in range(U):
                    b = U * i + u
                    wait_apart(sp, keep, att_low, i * U, u + 1 - U)
                    sp.dma_start(att[u][:], at(ar, b)).then_inc(att_in[u], 16)
                    wait_apart(sp, keep, xn_done, i * U * T, (u + 1 - U) * T)
                    wait_apart(sp, keep, stored[u], i * 16, 0)
                    sp.dma_start(xs[u][:], at(xr, b)).then_inc(x_in[u], 16)

            for i in range(B // U):
                round_of(i)

        @block.gpsimd
        def _(pool):
            pool.memset(padrow[:], 0.0).then_inc(pad_made, 1)
            pool.wait_ge(pad_made, 1)
            pool.dma_start(rows_dram[N:N + 1, :], padrow[:]).then_inc(pad_out, 16)
            pool.wait_ge(nan_s, 5)

            def add_bias(i, u):
                wait(pool, x_in[u], i * 16, 16)
                pool.tensor_tensor(xs[u][:], xs[u][:], bo_b[:].unsqueeze(1).to_broadcast([P, T, C]), ALU.add).then_inc(biased, 1)

            def round_of(i):
                for u in range(U):
                    b = U * i + u
                    wait(pool, aggr_done, i * U * T, (u + 1) * T)
                    wait(pool, newton, i * 4 * U, 4 * u)
                    pool_rsqrt(pool, keep, rsqrt_done, i * 2 * U + 2 * u, mv[:, :, 1], r0[:])
                    wait_apart(pool, keep, x1_done, i * U * T, (u + 1) * T)
                    pool.dma_start(at(rrow, b)[:, :, 0:C], xs[u][:]).then_inc(stored[u], 16)
                    if not (isinstance(i, int) and b + AHEAD >= B):
                        add_bias(i + (u + AHEAD) // U, (u + AHEAD) % U)

            AHEAD = 2
            for u in range(AHEAD):
                add_bias(0, u)
            round_of(0)
            assert B == 2 * U
            round_of(1)
            for u in range(U):
                pool.wait_ge(stored[u], 16 * (B // U))
            pool.wait_ge(pad_out, 16)

        @block.tensor
        def _(pe):
            pe.wait_ge(w_in, 96)
            for g in range(CT):
                last = pe.matmul(c_bank[:], bvT[:, g:g + 1].to_broadcast([P, P]), wo[:, g, :], start=(g == 0), stop=(g == CT - 1))
            last.then_inc(const_pe, 1)
            for c in range(CT):
                last = pe.transpose(d_bank[:, c * E:(c + 1) * E], rw[:, c * P:(c + 1) * P], ident[0:E, 0:E])
            last.then_inc(const_pe, 1)
            pe.wait_ge(const_act, 2)
            pe.wait_ge(nan_s, 1)
            pe.matmul(d_bank[:, 0:1], ones[:], nan_row[:], start=True, stop=True).then_inc(const_pe, 1)

            def products(i, u):
                wait(pe, att_low, i * U, u + 1)
                for t in range(T):
                    wait(pe, x1_done, i * U * T, (u - 1) * T + t + 1)
                    for k, (a, w) in enumerate(((attl, woh), (atth, wol), (atth, woh))):
                        for g in range(CT):
                            last = pe.matmul(y_bank[t][:], a[u % 2][:, g, t * P:(t + 1) * P], w[:, g, :],
                                             start=(k == 0 and g == 0), stop=(k == 2 and g == CT - 1))
                    last.then_inc(y_full, 1)

            def route(i, u):
                wait(pe, xn_done, i * U * T, (u + 1) * T)
                for c in range(CT):
                    wait(pe, t_read, i * U * CT, u * CT + c - 1)
                    for t in range(T):
                        last = pe.transpose(t_bank[c % 2][:, t * P:(t + 1) * P], xn[u % 2][:, t, c * P:(c + 1) * P], ident[:])
                    last.then_inc(t_full, 1)
                wait(pe, t_read, i * U * CT, (u + 1) * CT)
                for c in range(CT):
                    last = pe.matmul(expert_bank[0:E, :], rwT[:, c, :], xT[:, c, :], start=(c == 0), stop=(c == CT - 1))
                last.then_inc(lT_full, 1)

            def turn_logits(b):
                wait(pe, lT_read, 0, b + 1)
                wait(pe, l_read, 0, b)
                for t in range(T):
                    last = pe.transpose(token_bank[:, t * E:(t + 1) * E], lT[:, t * P:(t + 1) * P], ident[0:E, 0:E])
                last.then_inc(l_full, 1)

            pe.wait_ge(wo_low, 1)
            pe.wait_ge(nan_s, 5)
            for b in range(B):
                products(b // U, b % U)
                if b > 1:
                    turn_logits(b - 2)
                if b:
                    route((b - 1) // U, (b - 1) % U)
            turn_logits(B - 2)
            route((B - 1) // U, (B - 1) % U)
            turn_logits(B - 1)

        @block.scalar
        def _(act):
            act.wait_ge(w_in, 96)
            act.activation(gate[:], gate[:], ACT.Tanh).then_inc(const_act, 1)
            act.activation(gate2[:], gate2[:], ACT.Tanh)
            act.activation(woh[:], wo[:], ACT.Copy).then_inc(wo_high, 1)
            act.wait_ge(const_pe, 2)
            act.activation(rwT[:], d_bank[:, 0:CT * E], ACT.Identity).then_inc(const_act, 1)

            def read_turned(i, u):
                wait(act, lT_full, i * U, u)
                for c in range(CT):
                    wait(act, t_full, i * U * CT, u * CT + c + 1)
                    act.activation(xT[:, c, :], t_bank[c % 2][:], ACT.Identity).then_inc(t_read, 1)

            def read_expert_logits(b):
                wait(act, l_full, 0, b)
                wait(act, lT_full, 0, b + 1)
                act.activation(lT[:], expert_bank[0:E, :], ACT.Identity).then_inc(lT_read, 1)

            def read_logits(b):
                wait(act, l_full, 0, b + 1)
                act.activation(keep["logits"][:, b * T:(b + 1) * T, :],
                               token_bank[:, 0:T * E].rearrange("p (t e) -> p t e", t=T), ACT.Identity).then_inc(l_read, 1)

            def split(b):
                wait(act, blended, 0, b + 1)
                wait(act, y_full, 0, (b - 1) * T)
                act.activation(atth[b % 2][:], att[b % U][:], ACT.Copy).then_inc(att_high, 1)

            split(0)
            split(1)
            for b in range(B):
                if b + 2 < B:
                    split(b + 2)
                if b > 1:
                    read_logits(b - 2)
                if b:
                    read_expert_logits(b - 1)
                read_turned(b // U, b % U)
            read_logits(B - 2)
            read_expert_logits(B - 1)
            read_logits(B - 1)

        @block.vector
        def _(dve):
            dve.tensor_reduce(nan_row[:], keep["nan_acc"][:], AX_X, ALU.add).then_inc(nan_s, 1)
            dve.wait_ge(wo_high, 1)
            dve.tensor_tensor(wol[:], wo[:], woh[:].bitcast(F32), ALU.subtract).then_inc(wo_low, 1)
            dve.wait_ge(const_pe, 3)
            dve.tensor_copy(nan_tot[:], d_bank[:, 0:1]).then_inc(nan_s, 1)
            dve.wait_ge(nan_s, 2)
            dve.tensor_tensor(nan_f[:], nan_tot[:], nan_tot[:], ALU.not_equal).then_inc(nan_s, 1)
            dve.wait_ge(nan_s, 3)
            dve.tensor_copy(nan_mask[:], nan_f[:]).then_inc(nan_s, 1)
            dve.wait_ge(const_act, 1)
            dve.tensor_tensor(bo_b[:], c_bank[:], bo_b[:], ALU.add).then_inc(setup, 1)
            dve.wait_ge(setup, 1)
            dve.tensor_scalar(bo_b[:], bo_b[:], gate[:, 0:1], None, ALU.mult).then_inc(nan_s, 1)
            dve.wait_ge(nan_s, 5)

            def blend(i, u):
                wait_apart(dve, keep, att_in[u], i * 16, 16)
                dve.copy_predicated(att[u][:], nan_mask[:, 0:1].unsqueeze(2).to_broadcast([P, CT, S]),
                                    keep["meanv"][:, :, U * i + u].unsqueeze(2).to_broadcast([P, CT, S])).then_inc(blended, 1)

            def residual(i, u):
                wait(dve, biased, i * U, u + 1)
                for t in range(T):
                    wait(dve, y_full, i * U * T, u * T + t + 1)
                    dve.scalar_tensor_tensor(out=xs[u][:, t, :], in0=y_bank[t][:], scalar=gate[:, 0:1], in1=xs[u][:, t, :],
                                             op0=ALU.mult, op1=ALU.add).then_inc(x1_done, 1)
                wait(dve, xn_done, i * U * T, u * T)
                wait(dve, kept_stats, i * 2 * U, 2 * u)
                for t in range(T):
                    wait(dve, x1_done, i * U * T, u * T + t + 1)
                    dve.bn_stats(stats[:, t, :], xs[u][:, t, :]).then_inc(stats_done, 1)
                wait_apart(dve, keep, stats_done, i * U * T, (u + 1) * T)
                for t in range(T):
                    dve.bn_aggr(mv[:, t, :], stats[:, t, :]).then_inc(aggr_done, 1)

            def normalise(i, u):
                b = U * i + u
                wait(dve, rsqrt_done, i * 2 * U, 2 * u + 2)
                newton_rsqrt(dve, newton, i * 4 * U + 4 * u, mv[:, :, 1], r0[:], tmp[:], rs[:])
                wait(dve, newton, i * 4 * U, 4 * u + 4)
                wait(dve, t_full, i * U * CT, (u - 1) * CT)
                for t in range(T):
                    dve.tensor_scalar(xn[u % 2][:, t, :], xs[u][:, t, :], mv[:, t, 0:1], rs[:, t:t + 1],
                                      ALU.subtract, ALU.mult).then_inc(xn_done, 1)
                rows = slice(b * T, (b + 1) * T) if isinstance(i, int) else bass.ds(b * T, T)
                dve.tensor_copy(keep["token"][:, rows, 0], mv[:, :, 0]).then_inc(kept_stats, 1)
                dve.tensor_copy(keep["token"][:, rows, 1], rs[:]).then_inc(kept_stats, 1)

            def round_of(i):
                for u in range(U):
                    if U * i + u + 2 < B:
                        blend(i + (u + 2) // U, (u + 2) % U)
                    residual(i, u)
                    if U * i + u + 2 < B:
                        low(U * i + u + 2)
                    normalise(i, u)

            def low(b):
                wait(dve, att_high, 0, b + 1)
                dve.tensor_tensor(attl[b % 2][:], att[b % U][:], atth[b % 2][:].bitcast(F32), ALU.subtract).then_inc(att_low, 1)

            blend(0, 0)
            blend(0, 1)
            low(0)
            low(1)
            for i in range(B // U):
                round_of(i)


TILE_PLACE = (0, 1, 3, 4, 2, 5)


def routing(nc, keep, N, E, CAP, C, rows_dram):
    NT = N // P
    K = CAP // P
    assert sorted(TILE_PLACE) == list(range(K))
    with ExitStack() as ctx:
        sb, ps, sem = make_pools(nc, ctx)
        mx = sb("mx", [P, NT])
        e_ = sb("e_", [P, NT, E])
        sm = sb("sm", [P, NT])
        ri = sb("ri", [P, NT])
        pr = sb("pr", [P, NT, E])
        rank = sb("rank", [P, E])
        first = sb("first", [P, E])
        oh = sb("oh", [P, NT, E])
        tot = sb("tot", [P, E, NT])
        run = sb("run", [P, E, NT])
        one = sb("one", [P, NT])
        used = sb("used", [P, E])
        pos = sb("pos", [P, NT, E])
        place = sb("place", [P, NT])
        row = sb("row", [P, NT])
        column = sb("column", [P, NT])
        in_column = sb("in_column", [P, K, NT])
        tok = sb("tok", [P, NT])
        tok_oh = sb("tok_oh", [P, NT, E])
        tri = sb("tri", [P, P])
        lane = sb("lane", [P, P])
        by_row = sb("by_row", [P, NT, P])
        by_column = sb("by_column", [P, NT, E * K])
        a_bank = ps("a_bank")
        b_bank = ps("b_bank")
        i_bank = ps("i_bank")
        ch = sem("c_chain")
        ex = sem("c_exp")
        cn = sem("c_counts")
        token_ready = sem("c_token")
        chosen_ready = sem("c_chosen")
        setup = sem("c_setup")
        rows_made = sem("c_rows_made")
        columns_made = sem("c_columns_made")
        index_sum = sem("c_index_sum")
        index_made = sem("c_index_made")
        st = sem("c_stats_out")
        block = ctx.enter_context(nc.Block())
        logits, token = keep["logits"], keep["token"]
        bc = lambda t: t.unsqueeze(2).to_broadcast([P, NT, E])
        ec = lambda t: t.unsqueeze(1).to_broadcast([P, NT, E])

        @block.gpsimd
        def _(pool):
            pool.iota(tok[:], pattern=[[P, NT]], base=-N, channel_multiplier=1, allow_small_or_imprecise_dtypes=True).then_inc(setup, 1)
            pool.iota(lane[:], pattern=[[1, P]], base=1, channel_multiplier=0, allow_small_or_imprecise_dtypes=True).then_inc(setup, 1)
            pool.iota(rank[:], pattern=[[-1, E]], base=E, channel_multiplier=0, allow_small_or_imprecise_dtypes=True).then_inc(setup, 1)
            pool.memset(tri[:], 1.0).then_inc(setup, 1)
            pool.memset(first[:], 0.0).then_inc(setup, 1)
            pool.memset(one[:], 1.0).then_inc(setup, 1)
            pool.wait_ge(setup, 6)
            pool.affine_select(out=tri[:], in_=tri[:], compare_op=ALU.is_ge, fill=0.0, base=0, pattern=[[1, P]],
                               channel_multiplier=-1).then_inc(setup, 1)
            pool.memset(first[:, 0:1], 0.5).then_inc(setup, 1)
            pool.wait_ge(setup, 8)

        @block.sync
        def _(sp):
            sp.wait_ge(token_ready, 1)
            sp.dma_start(rows_dram[0:N, C:C + 4].rearrange("(t p) w -> p t w", p=P), token[:],
                         allow_slow_non_contiguous=True).then_inc(st, 16)
            sp.wait_ge(st, 16)

        @block.scalar
        def _(act):
            act.wait_ge(ch, 2)
            act.activation(e_[:], e_[:], ACT.Exp).then_inc(ex, 1)

        @block.tensor
        def _(pe):
            pe.wait_ge(chosen_ready, 1)
            pe.wait_ge(setup, 8)
            flat = oh[:].rearrange("p t e -> p (t e)")
            pe.matmul(a_bank[:, 0:NT * E], tri[:], flat, start=True, stop=True).then_inc(cn, 1)
            pe.matmul(b_bank[:, 0:NT * E], keep["ones"][:], flat, start=True, stop=True).then_inc(cn, 1)
            pe.wait_ge(columns_made, K)
            for t in range(NT):
                pe.wait_ge(rows_made, t + 1)
                last = pe.matmul(i_bank[:, 0:E * K], by_row[:, t, :], by_column[:, t, :], start=(t == 0), stop=(t == NT - 1))
            last.then_inc(index_sum, 1)

        @block.vector
        def _(dve):
            n = [0]

            def step(ins):
                n[0] += 1
                ins.then_inc(ch, 1)
                dve.wait_ge(ch, n[0])

            step(dve.tensor_reduce(mx[:], logits[:], AX_X, ALU.max))
            step(dve.tensor_tensor(e_[:], logits[:], bc(mx[:]), ALU.subtract))
            dve.wait_ge(ex, 1)
            step(dve.tensor_reduce(sm[:], e_[:], AX_X, ALU.add))
            step(dve.reciprocal(ri[:], sm[:]))
            step(dve.tensor_tensor(pr[:], e_[:], bc(ri[:]), ALU.mult))
            step(dve.tensor_reduce(mx[:], pr[:], AX_X, ALU.max))
            dve.tensor_copy(token[:, :, 2], mx[:]).then_inc(token_ready, 1)
            step(dve.tensor_tensor(pr[:], pr[:], bc(mx[:]), ALU.is_equal))
            dve.wait_ge(setup, 8)
            step(dve.tensor_tensor(pr[:], pr[:], ec(rank[:]), ALU.mult))
            step(dve.tensor_tensor(pr[:], pr[:], ec(first[:]), ALU.max))
            step(dve.tensor_reduce(mx[:], pr[:], AX_X, ALU.max))
            dve.tensor_tensor(oh[:], pr[:], bc(mx[:]), ALU.is_equal).then_inc(chosen_ready, 1)
            dve.wait_ge(chosen_ready, 1)
            step(dve.tensor_tensor(tok_oh[:], oh[:], bc(tok[:]), ALU.mult))
            dve.wait_ge(cn, 2)
            step(dve.tensor_copy(tot[:].rearrange("p e t -> p t e"), b_bank[:, 0:NT * E].rearrange("p (t e) -> p t e", t=NT)))
            for x in range(E):
                step(dve.tensor_tensor_scan(run[:, x, :], one[:], tot[:, x, :], 0.0, ALU.mult, ALU.add))
            step(dve.tensor_scalar(used[:], run[:, :, NT - 1], 0.0, None, ALU.is_gt))
            for k in range(1, K):
                step(dve.scalar_tensor_tensor(out=used[:], in0=run[:, :, NT - 1], scalar=float(k * P), in1=used[:], op0=ALU.is_gt, op1=ALU.add))
            step(dve.tensor_copy(keep["tiles"][:], used[:]))
            step(dve.tensor_tensor(run[:], run[:], tot[:], ALU.subtract))
            step(dve.tensor_tensor(pos[:], a_bank[:, 0:NT * E].rearrange("p (t e) -> p t e", t=NT), run[:].rearrange("p e t -> p t e"), ALU.add))
            step(dve.tensor_tensor(pos[:], pos[:], oh[:], ALU.mult))
            step(dve.tensor_reduce(place[:], pos[:], AX_X, ALU.add))
            step(dve.tensor_scalar(column[:], place[:], float(P), None, ALU.is_gt))
            for k in range(2, K + 1):
                step(dve.scalar_tensor_tensor(out=column[:], in0=place[:], scalar=float(k * P), in1=column[:], op0=ALU.is_gt, op1=ALU.add))
            step(dve.scalar_tensor_tensor(out=row[:], in0=column[:], scalar=-float(P), in1=place[:], op0=ALU.mult, op1=ALU.add))
            columns = by_column[:].rearrange("p t (e k) -> p t e k", k=K)
            for k in range(K):
                step(dve.tensor_scalar(in_column[:, k, :], column[:], float(k), None, ALU.is_equal))
                dve.tensor_tensor(columns[:, :, :, TILE_PLACE[k]], tok_oh[:], bc(in_column[:, k, :]), ALU.mult).then_inc(columns_made, 1)
            for t in range(NT):
                dve.tensor_scalar(by_row[:, t, :], lane[:], row[:, t:t + 1], None, ALU.is_equal).then_inc(rows_made, 1)
            dve.wait_ge(index_sum, 1)
            dve.tensor_scalar(keep["index"][:], i_bank[:, 0:E * K], float(N), None, ALU.add).then_inc(index_made, 1)
            dve.wait_ge(index_made, 1)


def experts(nc, keep, w1, b1, w2, b2, rows_dram, out, CAP):
    E, C, FF = w1.shape
    W = rows_dram.shape[1]
    N = rows_dram.shape[0] - 1
    CT = C // P
    ST = CAP // P
    CH = 4
    FT = FF // P // CH
    FW = FT * P
    HALF = CAP // 2
    TH = HALF // P
    UP = 2 * FT
    TF = 2 * CT
    with ExitStack() as ctx:
        sb, ps, sem = make_pools(nc, ctx)
        w1s = sb("w1s", [P, CT, FW])
        w2s = sb("w2s", [P, FT, C])
        w1h = [sb(f"w1h{i}", [P, CT, FW], F32R) for i in range(2)]
        w1l = [sb(f"w1l{i}", [P, CT, FW], F32R) for i in range(2)]
        w2h = [sb(f"w2h{i}", [P, FT, C], F32R) for i in range(2)]
        w2l = [sb(f"w2l{i}", [P, FT, C], F32R) for i in range(2)]
        b1all = sb("b1all", [P, E * CH * FT])
        b1s = sb("b1s", [P, CH * FT])
        b2b = sb("b2b", [P, C])
        gel = [sb(f"gel{i}", [P, CAP]) for i in range(2)]
        hh = [sb(f"hh{i}", [P, FT, CAP], F32R) for i in range(2)]
        hl = [sb(f"hl{i}", [P, FT, CAP], F32R) for i in range(2)]
        xTh = sb("gTh", [P, CT, CAP], F32R)
        xTl = sb("gTl", [P, CT, CAP], F32R)
        xg = sb("xg", [P, ST, W])
        xn = sb("exn", [P, ST, C])
        res = sb("res", [P, ST, C])
        idx_g = sb("idx_g", [P, ST], I32)
        idx_s = sb("idx_s", [P, ST], I32)
        gp = sb("gp", [P, ST])

        up_bank = [ps(f"up_bank{i}") for i in range(2)]
        y_bank = [ps(f"ey_bank{i}") for i in range(ST)]

        b1_in = sem("d_b1_in")
        b1_set = sem("d_b1_set")
        w1_in = sem("d_w1_in")
        w2_in = sem("d_w2_in")
        b2_in = sem("d_b2_in")
        idx_picked = sem("d_idx_picked")
        w1h_done = sem("d_w1h")
        w1l_done = sem("d_w1l")
        w2h_done = sem("d_w2h")
        w2l_done = sem("d_w2l")
        rows_in = sem("d_rows_in")
        gp_done = sem("d_gp")
        xn_done = sem("d_xn")
        t_full = sem("d_t_full")
        th_done = sem("d_th")
        tl_done = sem("d_tl")
        up_full = sem("d_up_full")
        gelu_done = sem("d_gelu")
        hh_done = sem("d_hh")
        hl_done = sem("d_hl")
        down_done = sem("d_down")
        y_full = sem("d_y_full")
        res_done = sem("d_res")
        idx_kept = sem("d_idx_kept")
        out_done = sem("d_out_done")
        scattered = sem("d_scattered")
        copied = sem("d_copied")

        ident, gate2 = keep["ident"], keep["gate2"]
        w1v = w1.rearrange("e (k p) f -> e p k f", p=P)
        w2v = w2.rearrange("e (c f p) d -> (e c) p f d", p=P, c=CH)
        f32 = lambda t: t.bitcast(F32)

        def at(t, i):
            if isinstance(i, int):
                return t[i]
            names = ["p", "k", "f"][:len(t.shape) - 1]
            return t[bass.ds(i, 1)].rearrange(f"o {' '.join(names)} -> (o p) {' '.join(names[1:])}")

        block = ctx.enter_context(nc.Block())

        @block.sync
        def _(sp):
            sp.dma_start(b1all[:], b1.rearrange("e (t p) -> p (e t)", p=P), allow_slow_non_contiguous=True).then_inc(b1_in, 16)

            def load_w1(e, c):
                wait_apart(sp, keep, w1l_done, e * CH * CT, c * CT)
                sp.dma_start(w1s[:], at(w1v, e)[:, :, c * FW:(c + 1) * FW]).then_inc(w1_in, 16)

            def expert(e, more):
                wait_apart(sp, keep, gp_done, e, 0)
                wait_apart(sp, keep, res_done, e * ST, 0)
                b2row = b2[e:e + 1] if isinstance(e, int) else b2[bass.ds(e, 1)]
                sp.dma_start(b2b[:], b2row.to_broadcast([P, C])).then_inc(b2_in, 16)
                for c in range(CH):
                    if c < CH - 1 or more:
                        load_w1(*((e, c + 1) if c < CH - 1 else (e + 1, 0)))
                    wait_apart(sp, keep, w2l_done, e * CH * FT, c * FT)
                    sp.dma_start(w2s[:], at(w2v, e * CH + c)).then_inc(w2_in, 16)
                    if isinstance(e, int) and e == 0:
                        part = slice(c * N // CH, (c + 1) * N // CH)
                        sp.dma_start(out[part, :], rows_dram[part, 0:C]).then_inc(copied, 16)

            load_w1(0, 0)
            expert(0, True)
            with sp.Fori(1, E - 1) as e:
                expert(e, True)
            expert(E - 1, False)

        @block.gpsimd
        def _(pool):
            def gather(e):
                wait_apart(pool, keep, idx_picked, e, 1)
                wait_apart(pool, keep, xn_done, e * ST, 0)
                wait_apart(pool, keep, res_done, e * ST, 0)
                for k in range(ST):
                    pool.indirect_dma_start(xg[:, k, :], None, rows_dram, bass.IndirectOffsetOnAxis(ap=idx_g[:, k:k + 1], axis=0),
                                            bounds_check=N, oob_is_err=False).then_inc(rows_in, 16)

            def scatter(e):
                for k in range(ST):
                    wait_apart(pool, keep, out_done, e * ST, k + 1)
                    pool.indirect_dma_start(out, bass.IndirectOffsetOnAxis(ap=idx_s[:, k:k + 1], axis=0), res[:, k, :], None,
                                            bounds_check=N - 1, oob_is_err=False).then_inc(scattered, 16)

            gather(0)
            gather(1)
            pool.wait_ge(copied, 16 * CH)
            scatter(0)
            with pool.Fori(1, E - 1) as e:
                gather(e + 1)
                scatter(e)
            scatter(E - 1)
            pool.wait_ge(scattered, 16 * ST * E)

        @block.tensor
        def _(pe):
            def turn(e, n):
                if n == 0:
                    wait(pe, xn_done, e * ST, ST)
                c, half = n // 2, n % 2
                if n < 2:
                    wait(pe, gelu_done, e * CH * UP, n - 1)
                else:
                    wait(pe, tl_done, e * TF, n - 1)
                for k in range(TH):
                    t = half * TH + k
                    last = pe.transpose(up_bank[n % 2][:, k * P:(k + 1) * P], xn[:, t, c * P:(c + 1) * P], ident[:])
                last.then_inc(t_full, 1)

            def up(e, c, banks):
                s = c % 2
                wait(pe, w1l_done, e * CH * CT, (c + 1) * CT)
                if c == 0:
                    wait(pe, tl_done, e * TF, TF)
                for n in range(UP):
                    f, half = n // 2, n % 2
                    if c > 0 or n > 1:
                        wait(pe, gelu_done, e * CH * UP, c * UP + n - 1)
                    parts = ((w1l[s], xTh), (w1h[s], xTl), (w1h[s], xTh))
                    width = max(2, sum(k // TH == half for k in banks)) * P
                    for i, (w, t) in enumerate(parts):
                        for k in range(CT):
                            last = pe.matmul(up_bank[n % 2][:, 0:width], w[:, k, f * P:(f + 1) * P], t[:, k, half * HALF:half * HALF + width],
                                             start=(i == 0 and k == 0), stop=(i == 2 and k == CT - 1))
                    last.then_inc(up_full, 1)

            def down(e, c, banks, more=False):
                s = c % 2
                wait(pe, hl_done, e * CH * FT, (c + 1) * FT)
                wait(pe, w2l_done, e * CH * FT, (c + 1) * FT)
                for k in banks:
                    if c == 0:
                        wait(pe, out_done, e * ST, k + 1 - ST)
                    parts = ((hl[s], w2h[s]), (hh[s], w2l[s]), (hh[s], w2h[s]))
                    for i, (h, w) in enumerate(parts):
                        for f in range(FT):
                            last = pe.matmul(y_bank[k][:], h[:, f, k * P:(k + 1) * P], w[:, f, :],
                                             start=(c == 0 and i == 0 and f == 0), stop=(c == CH - 1 and i == 2 and f == FT - 1))
                    if c == CH - 1:
                        last.then_inc(y_full, min([n for n in banks if n > k], default=ST) - k)
                    elif k == banks[-1]:
                        last.then_inc(down_done, 1)
                    if more and c == CH - 1:
                        i = banks.index(k)
                        for n in range(min(2 * i, TF), TF if k == banks[-1] else min(2 * i + 2, TF)):
                            turn(e + 1, n)

            def products(e, more, used):
                banks = sorted(TILE_PLACE[:used])
                up(e, 0, banks)
                up(e, 1, banks)
                down(e, 0, banks)
                up(e, 2, banks)
                down(e, 1, banks)
                up(e, 3, banks)
                down(e, 2, banks)
                down(e, 3, banks, more)

            def expert(e, more):
                column = keep["tiles"][0:1, e:e + 1] if isinstance(e, int) else keep["tiles"][0:1, bass.ds(e, 1)]
                used = pe.value_load(column, min_val=0, max_val=ST)
                with pe.If(used < ST - 1):
                    with pe.If(used < ST - 2):
                        products(e, more, ST - 3)
                    with pe.Else():
                        products(e, more, ST - 2)
                with pe.Else():
                    with pe.If(used < ST):
                        products(e, more, ST - 1)
                    with pe.Else():
                        products(e, more, ST)

            for k in TILE_PLACE[ST - 3:]:
                for t in range(C // P):
                    pe.transpose(y_bank[k][:, t * P:(t + 1) * P], ident[:], ident[:])
            for n in range(TF):
                turn(0, n)
            expert(0, True)
            with pe.Fori(1, E - 1) as e:
                expert(e, True)
            expert(E - 1, False)

        def downs(e, c):
            if c == CH - 1:
                return y_full, e * ST, ST
            return down_done, e * (CH - 1), c + 1

        @block.scalar
        def _(act):
            def w1_high(e, c, k):
                s = c % 2
                if k == 0:
                    wait(act, w1_in, e * CH * 16, (c + 1) * 16)
                    wait(act, up_full, e * CH * UP, (c - 1) * UP)
                act.activation(w1h[s][:, k, :], w1s[:, k, :], ACT.Copy).then_inc(w1h_done, 1)

            def w2_high(e, c, k):
                s = c % 2
                if k == 0:
                    wait(act, w2_in, e * CH * 16, (c + 1) * 16)
                    if c >= 2:
                        wait(act, *downs(e, c - 2))
                    elif not (isinstance(e, int) and e == 0):
                        wait(act, *downs(e - 1, c + 2))
                act.activation(w2h[s][:, k, :], w2s[:, k, :], ACT.Copy).then_inc(w2h_done, 1)

            def turned(e):
                for n in range(TF):
                    c, half = n // 2, n % 2
                    wait(act, t_full, e * TF, n + 1)
                    act.activation(xTh[:, c, half * HALF:(half + 1) * HALF], up_bank[n % 2][:, 0:HALF], ACT.Copy).then_inc(th_done, 1)

            def expert(e, more):
                wait(act, b1_set, e, 1)
                for c in range(CH):
                    for n in range(UP):
                        f, half = n // 2, n % 2
                        wait(act, up_full, e * CH * UP, c * UP + n + 1)
                        if half == 0:
                            wait(act, hl_done, e * CH * FT, c * FT + f - 1)
                        act.activation(gel[f % 2][:, half * HALF:(half + 1) * HALF], up_bank[n % 2][:, 0:HALF], ACT.Gelu,
                                       bias=b1s[:, c * FT + f:c * FT + f + 1]).then_inc(gelu_done, 1)
                        if n >= CT:
                            w2_high(e, c, n - CT)
                        elif c < CH - 1:
                            w1_high(e, c + 1, n)
                        elif more:
                            w1_high(e + 1, 0, n)
                if more:
                    turned(e + 1)

            for k in range(CT):
                w1_high(0, 0, k)
            turned(0)
            expert(0, True)
            with act.Fori(1, E - 1) as e:
                expert(e, True)
            expert(E - 1, False)

        @block.vector
        def _(dve):
            def w1_low(e, c, k):
                wait(dve, w1h_done, e * CH * CT, c * CT + k + 1)
                if k == 0:
                    wait(dve, up_full, e * CH * UP, (c - 1) * UP)
                s = c % 2
                dve.tensor_tensor(w1l[s][:, k, :], w1s[:, k, :], f32(w1h[s][:, k, :]), ALU.subtract).then_inc(w1l_done, 1)

            def w2_low(e, c, k):
                wait(dve, w2h_done, e * CH * FT, c * FT + k + 1)
                s = c % 2
                dve.tensor_tensor(w2l[s][:, k, :], w2s[:, k, :], f32(w2h[s][:, k, :]), ALU.subtract).then_inc(w2l_done, 1)

            def normalise(e):
                wait(dve, rows_in, e * 16 * ST, 16 * ST)
                wait(dve, t_full, e * TF, 0)
                for k in range(ST):
                    dve.tensor_scalar(xn[:, k, :], xg[:, k, 0:C], xg[:, k, C:C + 1], xg[:, k, C + 1:C + 2],
                                      ALU.subtract, ALU.mult).then_inc(xn_done, 1)

            def turned(e):
                for n in range(TF):
                    c, half = n // 2, n % 2
                    cols = slice(half * HALF, (half + 1) * HALF)
                    wait(dve, th_done, e * TF, n + 1)
                    dve.tensor_tensor(xTl[:, c, cols], up_bank[n % 2][:, 0:HALF], f32(xTh[:, c, cols]), ALU.subtract).then_inc(tl_done, 1)

            def set_bias(e):
                src = b1all[:, e * CH * FT:(e + 1) * CH * FT] if isinstance(e, int) else b1all[:, bass.ds(e * CH * FT, CH * FT)]
                wait(dve, gelu_done, e * CH * UP, 0)
                dve.tensor_copy(b1s[:], src).then_inc(b1_set, 1)

            def pick_index(e):
                cols = slice(e * ST, (e + 1) * ST) if isinstance(e, int) else bass.ds(e * ST, ST)
                dve.tensor_copy(idx_g[:], keep["index"][:, cols]).then_inc(idx_picked, 1)

            def residual(e, more):
                wait(dve, b2_in, e * 16, 16)
                dve.tensor_scalar(gp[:], xg[:, :, C + 2], gate2[:, 0:1], None, ALU.mult).then_inc(gp_done, 1)
                wait(dve, scattered, e * 16 * ST, 0)
                wait(dve, idx_picked, e, 1)
                dve.tensor_copy(idx_s[:], idx_g[:]).then_inc(idx_kept, 1)
                if more:
                    wait(dve, idx_kept, e, 1)
                    pick_index(e + 1)
                wait(dve, gp_done, e, 1)
                for k in range(ST):
                    dve.scalar_tensor_tensor(out=res[:, k, :], in0=b2b[:], scalar=gp[:, k:k + 1], in1=xg[:, k, 0:C],
                                             op0=ALU.mult, op1=ALU.add).then_inc(res_done, 1)

            def finish(e):
                for k in range(ST):
                    wait(dve, y_full, e * ST, k + 1)
                    wait(dve, res_done, e * ST, k + 1)
                    dve.scalar_tensor_tensor(out=res[:, k, :], in0=y_bank[k][:], scalar=gp[:, k:k + 1], in1=res[:, k, :],
                                             op0=ALU.mult, op1=ALU.add).then_inc(out_done, 1)

            def expert(e, more):
                for c in range(CH):
                    s = c % 2
                    for f in range(FT):
                        wait(dve, gelu_done, e * CH * UP, c * UP + 2 * f + 2)
                        if f == 0:
                            if c >= 2:
                                wait(dve, *downs(e, c - 2))
                            elif not (isinstance(e, int) and e == 0):
                                wait(dve, *downs(e - 1, c + 2))
                        dve.tensor_copy(hh[s][:, f, :], gel[f % 2][:]).then_inc(hh_done, 1)
                        if f >= 2:
                            w2_low(e, c, 2 * f - CT)
                            w2_low(e, c, 2 * f - CT + 1)
                        elif c < CH - 1 or more:
                            nxt = (e, c + 1) if c < CH - 1 else (e + 1, 0)
                            w1_low(*nxt, 2 * f)
                            w1_low(*nxt, 2 * f + 1)
                        wait(dve, hh_done, e * CH * FT, c * FT + f + 1)
                        dve.tensor_tensor(hl[s][:, f, :], gel[f % 2][:], f32(hh[s][:, f, :]), ALU.subtract).then_inc(hl_done, 1)
                    if c == 0:
                        residual(e, more)
                    if c == 2 and more:
                        normalise(e + 1)
                if more:
                    set_bias(e + 1)
                    turned(e + 1)
                finish(e)

            pick_index(0)
            dve.wait_ge(b1_in, 16)
            set_bias(0)
            normalise(0)
            for k in range(CT):
                w1_low(0, 0, k)
            turned(0)
            expert(0, True)
            with dve.Fori(1, E - 1) as e:
                expert(e, True)
            expert(E - 1, False)


def program(nc, x, ctx_768, g_xattn, g_ffn, Wq, bq, Wk, bk, Wv, bv, Wo, bo, router_w, w1, b1, w2, b2, out):
    B, S, C = x.shape
    N = B * S
    E = router_w.shape[0]
    CAP = -(-3 * N // (2 * E))
    CT = C // P
    attn_dram = nc.dram_tensor("attn_dram", [B * CT, P, S], F32).ap()
    rows_dram = nc.dram_tensor("rows_dram", [N + 1, C + 4], F32).ap()
    flat_out = out.rearrange("b s c -> (b s) c")
    with ExitStack() as ctx:
        def sb(name, shape, dt=F32):
            return ctx.enter_context(nc.sbuf_tensor(name, shape, dt))

        keep = {
            "ident": sb("ident", [P, P]),
            "ones": sb("ones", [P, P]),
            "eps": sb("eps", [P, 1]),
            "minus_half": sb("minus_half", [P, 1]),
            "index": sb("index", [P, E * (CAP // P)], I32),
            "nan_acc": sb("nan_acc", [P, B * CT]),
            "tiles": sb("tiles", [P, E], I32),
            "meanv": sb("meanv", [P, CT, B]),
            "gate2": sb("gate2", [P, 1]),
            "logits": sb("logits", [P, N // P, E]),
            "token": sb("token", [P, N // P, 4]),
        }
        early_ctx = ctx.enter_context(ExitStack())
        early = {name: early_ctx.enter_context(nc.sbuf_tensor(name, shape, F32)) for name, shape in (
            ("wo", [P, CT, C]), ("bvT", [P, CT]), ("bo_b", [P, C]), ("gate", [P, 1]), ("rw", [E, C]))}
        early["w_in"] = ctx.enter_context(nc.semaphore("b_w_in"))
        made = keep["made"] = ctx.enter_context(nc.semaphore("made"))
        keep["passed"] = ctx.enter_context(nc.semaphore("passed"))
        with nc.Block() as block:
            @block.sync
            def _(sp):
                sp.dma_start(early["bvT"][:], bv.rearrange("(t p) -> p t", p=P), allow_slow_non_contiguous=True).then_inc(early["w_in"], 16)
                sp.dma_start(early["bo_b"][:], bo.rearrange("(o n) -> o n", o=1).to_broadcast([P, C])).then_inc(early["w_in"], 16)
                sp.dma_start(early["rw"][:], router_w).then_inc(early["w_in"], 16)
                sp.dma_start(early["gate"][:], g_xattn.rearrange("(o n) -> o n", o=1).to_broadcast([P, 1])).then_inc(early["w_in"], 16)
                sp.dma_start(keep["gate2"][:], g_ffn.rearrange("(o n) -> o n", o=1).to_broadcast([P, 1])).then_inc(early["w_in"], 16)

            @block.gpsimd
            def _(pool):
                pool.memset(keep["ident"][:], 0.0).then_inc(made, 1)
                pool.memset(keep["ones"][:], 1.0).then_inc(made, 1)
                pool.memset(keep["eps"][:], EPS).then_inc(made, 1)
                pool.memset(keep["minus_half"][:], -0.5).then_inc(made, 1)
                pool.memset(keep["token"][:], 0.0).then_inc(made, 1)
                pool.wait_ge(made, MADE - 1)
                pool.affine_select(out=keep["ident"][:], in_=keep["ident"][:], compare_op=ALU.not_equal, fill=1.0, base=0,
                                   pattern=[[-1, P]], channel_multiplier=1).then_inc(made, 1)
                pool.wait_ge(made, MADE)
        attention(nc, keep, early, Wo, x, ctx_768, Wq, bq, Wk, bk, Wv, attn_dram)
        projection(nc, keep, early, x, attn_dram, rows_dram)
        early_ctx.close()
        routing(nc, keep, N, E, CAP, C, rows_dram)
        experts(nc, keep, w1, b1, w2, b2, rows_dram, flat_out, CAP)


_INS = ["x", "ctx_768", "g_xattn", "g_ffn", "L0_xattn_Wq", "L0_xattn_bq", "L0_xattn_Wk", "L0_xattn_bk", "L0_xattn_Wv",
        "L0_xattn_bv", "L0_xattn_Wo", "L0_xattn_bo", "L0_ffn_router_w", "L0_ffn_w1", "L0_ffn_b1", "L0_ffn_w2", "L0_ffn_b2"]


def kernel(**inputs):
    import numpy as np
    import concourse.bacc as bacc
    from concourse.bass_utils import run_bass_kernel_spmd

    nc = bacc.Bacc("TRN2", target_bir_lowering=False, num_devices=1)
    arrays, args = {}, []
    for name in _INS:
        a = np.ascontiguousarray(inputs[name])
        arrays[f"in_{name}"] = a
        args.append(nc.dram_tensor(f"in_{name}", a.shape, mybir.dt.from_np(a.dtype), kind="ExternalInput").ap())
    args.append(nc.dram_tensor("out_0", inputs["x"].shape, F32, kind="ExternalOutput").ap())
    program(nc, *args)
    return run_bass_kernel_spmd(nc, [arrays], core_ids=[0]).results[0]["out_0"]
```
